# Optimizing a Trainium2 kernel written in Bass

```python
import numpy as np
import jax
import jax.numpy as jnp

def _softmax(x, axis=-1):
    return jax.nn.softmax(x, axis=axis)

def _gelu(x):
    return jax.nn.gelu(x, approximate=True)

def _silu(x):
    return jax.nn.silu(x)

def _sigmoid(x):
    return jax.nn.sigmoid(x)

def _layernorm(x, axis=-1, eps=1e-05):
    m = jnp.mean(x, axis=axis, keepdims=True)
    v = jnp.var(x, axis=axis, keepdims=True)
    return (x - m) / jnp.sqrt(v + eps)

def _scatter_add(tgt, idx, src, axis=0):
    return tgt.at[idx].add(src)

def _segment_sum(src, seg, n):
    return jax.ops.segment_sum(src, seg, n)
kernel_name = 'mk_macaron_d1_jaxref_r4_0aabdf'

def setup_inputs(seed: int=0):
    np.random.seed(seed)
    _w = jnp.asarray

    def _L0_attn_setup():
        import jax, jax.numpy as jnp
        import numpy as np
        import math
        D_MODEL = 512
        NUM_HEADS = 16
        HEAD_DIM = D_MODEL // NUM_HEADS
        key = jax.random.key(seed)
        k_x, k_wqkv, k_bqkv, k_wo, k_bo = jax.random.split(key, 5)
        B, S = (2, 512)
        scale = 1.0 / math.sqrt(D_MODEL)
        return {'x': jax.random.normal(k_x, (B, S, D_MODEL), dtype=jnp.float32), 'w_qkv': jax.random.normal(k_wqkv, (3 * D_MODEL, D_MODEL), dtype=jnp.float32) * scale, 'b_qkv': jax.random.normal(k_bqkv, (3 * D_MODEL,), dtype=jnp.float32) * 0.01, 'w_out': jax.random.normal(k_wo, (D_MODEL, D_MODEL), dtype=jnp.float32) * scale, 'b_out': jax.random.normal(k_bo, (D_MODEL,), dtype=jnp.float32) * 0.01}
    _L0_attn_in = _L0_attn_setup()

    def _L0_ffn_setup():
        import jax, jax.numpy as jnp
        import numpy as np
        BLOCK_SIZE = 32
        HIDDEN_SIZE = 512
        MLP_DIM = 4096
        NVFP4_LUT = jnp.array([0.0, 0.5, 1.0, 1.5, 2.0, 3.0, 4.0, 6.0, 0.0, -0.5, -1.0, -1.5, -2.0, -3.0, -4.0, -6.0], dtype=jnp.float32)

        def dequant_nvfp4(W_packed, scales, block=BLOCK_SIZE):
            N = W_packed.shape[0]
            low = W_packed & 15
            high = W_packed >> 4 & 15
            idx = jnp.stack([low, high], axis=-1).reshape(N, -1)
            vals = NVFP4_LUT[idx]
            K = vals.shape[1]
            vals = vals.reshape(N, K // block, block) * scales[:, :, None]
            return vals.reshape(N, K)
        key = jax.random.key(seed)
        ks = jax.random.split(key, 7)
        x = jax.random.normal(ks[0], (4, 32, HIDDEN_SIZE), dtype=jnp.float32)
        gate_W_packed = jax.random.randint(ks[1], (MLP_DIM, HIDDEN_SIZE // 2), 0, 64, dtype=jnp.int32)
        gate_scales = jax.random.uniform(ks[2], (MLP_DIM, HIDDEN_SIZE // BLOCK_SIZE), dtype=jnp.float32) * 0.1 + 0.001
        up_W_packed = jax.random.randint(ks[3], (MLP_DIM, HIDDEN_SIZE // 2), 0, 64, dtype=jnp.int32)
        up_scales = jax.random.uniform(ks[4], (MLP_DIM, HIDDEN_SIZE // BLOCK_SIZE), dtype=jnp.float32) * 0.1 + 0.001
        down_W_packed = jax.random.randint(ks[5], (HIDDEN_SIZE, MLP_DIM // 2), 0, 64, dtype=jnp.int32)
        down_scales = jax.random.uniform(ks[6], (HIDDEN_SIZE, MLP_DIM // BLOCK_SIZE), dtype=jnp.float32) * 0.1 + 0.001
        return {'x': x, 'gate_W_packed': gate_W_packed, 'gate_scales': gate_scales, 'up_W_packed': up_W_packed, 'up_scales': up_scales, 'down_W_packed': down_W_packed, 'down_scales': down_scales}
    _L0_ffn_in = _L0_ffn_setup()
    _d = {'L0_attn_x': _L0_attn_in['x'], 'L0_attn_w_qkv': _L0_attn_in['w_qkv'], 'L0_attn_b_qkv': _L0_attn_in['b_qkv'], 'L0_attn_w_out': _L0_attn_in['w_out'], 'L0_attn_b_out': _L0_attn_in['b_out'], 'L0_ffn_gate_W_packed': _L0_ffn_in['gate_W_packed'], 'L0_ffn_gate_scales': _L0_ffn_in['gate_scales'], 'L0_ffn_up_W_packed': _L0_ffn_in['up_W_packed'], 'L0_ffn_up_scales': _L0_ffn_in['up_scales'], 'L0_ffn_down_W_packed': _L0_ffn_in['down_W_packed'], 'L0_ffn_down_scales': _L0_ffn_in['down_scales']}
    _x0 = _d['L0_attn_x']
    _d['L0_attn_x'] = jax.random.normal(jax.random.fold_in(jax.random.key(seed), 1), (1, 2048, 512), dtype=_x0.dtype)
    del _x0
    return _d

def reference(L0_attn_x, L0_attn_w_qkv, L0_attn_b_qkv, L0_attn_w_out, L0_attn_b_out, L0_ffn_gate_W_packed, L0_ffn_gate_scales, L0_ffn_up_W_packed, L0_ffn_up_scales, L0_ffn_down_W_packed, L0_ffn_down_scales):

    def _L0_attn_ref(x, w_qkv, b_qkv, w_out, b_out):
        import jax, jax.numpy as jnp
        import numpy as np
        import math
        D_MODEL = 512
        NUM_HEADS = 16
        HEAD_DIM = D_MODEL // NUM_HEADS
        B, S, D = x.shape
        H, Hd = (NUM_HEADS, HEAD_DIM)
        qkv = jnp.einsum('bsd,ed->bse', x, w_qkv) + b_qkv
        qkv = qkv.reshape(B, S, 3, H, Hd)
        q = jnp.transpose(qkv[:, :, 0], (0, 2, 1, 3))
        k = jnp.transpose(qkv[:, :, 1], (0, 2, 1, 3))
        v = jnp.transpose(qkv[:, :, 2], (0, 2, 1, 3))
        scores = jnp.einsum('bhqd,bhkd->bhqk', q, k) / math.sqrt(Hd)
        causal = jnp.triu(jnp.full((S, S), -jnp.inf, dtype=scores.dtype), k=1)
        scores = scores + causal[None, None]
        attn = jax.nn.softmax(scores, axis=-1)
        out = jnp.einsum('bhqk,bhkd->bhqd', attn, v)
        out = jnp.transpose(out, (0, 2, 1, 3)).reshape(B, S, D)
        return jnp.einsum('bsd,ed->bse', out, w_out) + b_out

    def _L0_ffn_ref(x, gate_W_packed, gate_scales, up_W_packed, up_scales, down_W_packed, down_scales):
        import jax, jax.numpy as jnp
        import numpy as np
        BLOCK_SIZE = 32
        HIDDEN_SIZE = 512
        MLP_DIM = 4096
        NVFP4_LUT = jnp.array([0.0, 0.5, 1.0, 1.5, 2.0, 3.0, 4.0, 6.0, 0.0, -0.5, -1.0, -1.5, -2.0, -3.0, -4.0, -6.0], dtype=jnp.float32)

        def dequant_nvfp4(W_packed, scales, block=BLOCK_SIZE):
            N = W_packed.shape[0]
            low = W_packed & 15
            high = W_packed >> 4 & 15
            idx = jnp.stack([low, high], axis=-1).reshape(N, -1)
            vals = NVFP4_LUT[idx]
            K = vals.shape[1]
            vals = vals.reshape(N, K // block, block) * scales[:, :, None]
            return vals.reshape(N, K)
        B, S, H = x.shape
        xt = x.reshape(B * S, H)
        Wg = dequant_nvfp4(gate_W_packed, gate_scales)
        Wu = dequant_nvfp4(up_W_packed, up_scales)
        Wd = dequant_nvfp4(down_W_packed, down_scales)
        gate = jnp.einsum('th,nh->tn', xt, Wg)
        up = jnp.einsum('th,nh->tn', xt, Wu)
        gelu = jnp.tanh(0.7978845608028654 * (gate + 0.044715 * gate ** 3)) * gate * 0.5 + gate * 0.5
        inter = gelu * up
        out = jnp.einsum('tn,hn->th', inter, Wd)
        return out.reshape(B, S, H)
    x = L0_attn_x
    x = x + 0.5 * _L0_ffn_ref(_layernorm(x, axis=-1), L0_ffn_gate_W_packed, L0_ffn_gate_scales, L0_ffn_up_W_packed, L0_ffn_up_scales, L0_ffn_down_W_packed, L0_ffn_down_scales)
    x = x + _L0_attn_ref(_layernorm(x, axis=-1), L0_attn_w_qkv, L0_attn_b_qkv, L0_attn_w_out, L0_attn_b_out)
    x = x + 0.5 * _L0_ffn_ref(_layernorm(x, axis=-1), L0_ffn_gate_W_packed, L0_ffn_gate_scales, L0_ffn_up_W_packed, L0_ffn_up_scales, L0_ffn_down_W_packed, L0_ffn_down_scales)
    return x

_drawn_inputs = setup_inputs


def setup_inputs(seed=0):
    import zlib

    import numpy as np

    out = dict(_drawn_inputs(seed))
    spreads = {}
    factors = {'L0_attn_w_qkv': 8.0, 'L0_attn_b_qkv': 8.0, 'L0_attn_w_out': 8.0, 'L0_attn_b_out': 200.0}
    for name, (base, spread) in spreads.items():
        noise = np.random.default_rng([zlib.crc32(name.encode()), seed]).standard_normal(out[name].shape)
        drawn = base * np.exp(spread * noise) if base else spread * noise
        out[name] = jnp.asarray(drawn.astype(out[name].dtype))
    for name, factor in factors.items():
        out[name] = (out[name] * factor).astype(out[name].dtype)
    return out
```

```python
from contextlib import ExitStack

import concourse.bass as bass
from concourse import mybir

ALU = mybir.AluOpType
ACT = mybir.ActivationFunctionType
AX = mybir.AxisListType
F32 = mybir.dt.float32
F32R = mybir.dt.float32r
F16 = mybir.dt.float16
BF16 = mybir.dt.bfloat16
I32 = mybir.dt.int32

P = 128
TOKENS = 2048
D = 512
KT = D // P
TB = 512
NTB = TOKENS // TB
MLP = 4096
GROUP = 256
NGROUP = MLP // GROUP
PIECE = 512
NPIECE = 3
GATE, UP, DOWN = 0, 1, 2
FP4_BLOCK = 32
SCALE_ROWS = 8
HEADS = 16
HD = D // HEADS
TT = TOKENS // P
VCOLS = 2 * HD + 1
SM_SCALE = 1.0 / float(HD) ** 0.5
EPS = 1e-5

CODE = 2.0 ** 14
GELU_A = 0.044715
GELU_C = 0.7978845608028654
FFN_BACK = CODE * CODE * CODE * 0.25
MASKED = -1e30


def f32(ap):
    return ap.bitcast(F32)


def cols(i, n):
    return slice(i * n, (i + 1) * n)


def split_products(pe, out, w_high, w_low, x_high, x_low, first, last):
    pe.matmul(out, w_high, x_high, start=first, stop=False, skip_group_check=True)
    pe.matmul(out, w_high, x_low, start=False, stop=False, skip_group_check=True)
    return pe.matmul(out, w_low, x_high, start=False, stop=last, skip_group_check=True)


class Norm:

    def __init__(self, nc, ctx, tag, x, x_high, x_low, centred, square, std, averager, eps,
                 mean_bank, var_bank):
        def sem(name):
            return ctx.enter_context(nc.semaphore(f"{tag}_{name}"))

        self.x, self.x_high, self.x_low = x, x_high, x_low
        self.centred, self.square, self.std = centred, square, std
        self.averager, self.eps = averager, eps
        self.mean_bank, self.var_bank = mean_bank, var_bank
        self.constants_ready = sem("constants_ready")
        self.mean_ready = sem("mean_ready")
        self.centred_ready = sem("centred_ready")
        self.square_ready = sem("square_ready")
        self.square_used = sem("square_used")
        self.std_ready = sem("std_ready")
        self.rstd_ready = sem("rstd_ready")
        self.normed_ready = sem("normed_ready")
        self.high_ready = sem("high_ready")
        self.low_ready = sem("low_ready")


def norm_tensor(pe, n, x_loaded):
    def mean(tb):
        if x_loaded is not None:
            pe.wait_ge(x_loaded[tb], 16)
        if tb == 0:
            pe.wait_ge(n.constants_ready, 2)
        if tb >= 2:
            pe.wait_ge(n.centred_ready, tb - 1)
        for k in range(KT):
            last = pe.matmul(n.mean_bank[tb % 2], n.averager[:], n.x[:, k, cols(tb, TB)],
                             start=(k == 0), stop=(k == KT - 1))
        last.then_inc(n.mean_ready, 1)

    def variance(tb):
        if tb >= 2:
            pe.wait_ge(n.std_ready, tb - 1)
        for k in range(KT):
            pe.wait_ge(n.square_ready, KT * tb + k + 1)
            pe.matmul(n.var_bank[tb % 2], n.averager[:], n.square[:, k % 2, :],
                      start=(k == 0), stop=(k == KT - 1)).then_inc(n.square_used, 1)

    mean(0)
    mean(1)
    for tb in range(NTB):
        variance(tb)
        if tb + 2 < NTB:
            mean(tb + 2)


def norm_vector(dve, n):
    def centre(tb):
        dve.wait_ge(n.mean_ready, tb + 1)
        if tb >= 2:
            dve.wait_ge(n.low_ready, tb - 1)
        dve.tensor_tensor(n.centred[tb % 2], n.x[:, :, cols(tb, TB)],
                          n.mean_bank[tb % 2].unsqueeze(1).broadcast_to([P, KT, TB]),
                          ALU.subtract).then_inc(n.centred_ready, 1)

    def normalize(tb):
        dve.wait_ge(n.std_ready, tb + 1)
        dve.reciprocal(n.std[:], n.std[:]).then_inc(n.rstd_ready, 1)
        dve.wait_ge(n.rstd_ready, tb + 1)
        dve.wait_ge(n.square_used, KT * (tb + 1))
        dve.tensor_tensor(n.centred[tb % 2], n.centred[tb % 2],
                          n.std[:].unsqueeze(1).broadcast_to([P, KT, TB]),
                          ALU.mult).then_inc(n.normed_ready, 1)

    centre(0)
    centre(1)
    for tb in range(NTB):
        normalize(tb)
        if tb + 2 < NTB:
            centre(tb + 2)


def norm_scalar(act, n):
    def high(tb):
        act.wait_ge(n.normed_ready, tb + 1)
        act.activation(n.x_high[:, :, cols(tb, TB)], n.centred[tb % 2], ACT.Copy).then_inc(n.high_ready, 1)

    for tb in range(NTB):
        act.wait_ge(n.centred_ready, tb + 1)
        for k in range(KT):
            if KT * tb + k >= 2:
                act.wait_ge(n.square_used, KT * tb + k - 1)
            act.activation(n.square[:, k % 2, :], n.centred[tb % 2][:, k, :],
                           ACT.Square).then_inc(n.square_ready, 1)
        act.wait_ge(n.square_used, KT * (tb + 1))
        if tb >= 1:
            act.wait_ge(n.normed_ready, tb)
        act.activation(n.std[:], n.var_bank[tb % 2], ACT.Sqrt, bias=n.eps[:]).then_inc(n.std_ready, 1)
        if tb >= 1:
            high(tb - 1)
    high(NTB - 1)


def norm_gpsimd(pool, n):
    for tb in range(NTB):
        pool.wait_ge(n.high_ready, tb + 1)
        pool.tensor_tensor(n.x_low[:, :, cols(tb, TB)], n.centred[tb % 2],
                           f32(n.x_high[:, :, cols(tb, TB)]), ALU.subtract).then_inc(n.low_ready, 1)


def ffn(nc, tag, x, bank, packed, scales, x_in, x_out):
    with ExitStack() as ctx:
        def sb(name, shape, dtype):
            return ctx.enter_context(nc.sbuf_tensor(f"{tag}_{name}", shape, dtype))

        def sem(name):
            return ctx.enter_context(nc.semaphore(f"{tag}_{name}"))

        x_high = sb("x_high", [P, KT, TOKENS], F32R)
        x_low = sb("x_low", [P, KT, TOKENS], F32R)
        words = sb("words", [P, NPIECE, PIECE], I32)
        word_scales = sb("word_scales", [P, NPIECE, PIECE], F32)
        nibbles = sb("nibbles", [P, 2, PIECE], I32)
        weight = sb("weight", [P, 2, 2, PIECE], F32)
        w_high = [sb(f"w_high{s}", [P, 2, NPIECE, PIECE], F32R) for s in range(2)]
        w_low = [sb(f"w_low{s}", [P, 2, NPIECE, PIECE], F32R) for s in range(2)]
        gelu = sb("gelu", [P, 6, TB], F32)
        inner = sb("inner", [P, 2, 2, 2, TB], F32R)
        centred1 = sb("centred1", [P, KT, TB], F32)
        std = sb("std", [P, TB], F32)
        averager = sb("averager", [P, P], F32)
        eps = sb("eps", [P, 1], F32)

        gate_bank, up_bank, down_bank = bank[0:2], bank[2:4], bank[4:8]
        square = [gelu[:, n, :] for n in range(2)]
        cubic = [gelu[:, 2 + n, :] for n in range(2)]
        product = [gelu[:, 4 + n, :] for n in range(2)]

        n = Norm(nc, ctx, tag, x, x_high, x_low, [gelu[:, 0:KT, :], centred1[:, :, :]],
                 gelu[:, KT:KT + 2, :], std, averager, eps, down_bank[0:2], down_bank[2:4])
        x_loaded = [sem(f"x_loaded{tb}") for tb in range(NTB)] if x_in is not None else None

        words_loaded = [sem(f"words_loaded{p}") for p in range(NPIECE)]
        nibbles_ready = sem("nibbles_ready")
        weight_ready = sem("weight_ready")
        w_high_ready = sem("w_high_ready")
        w_low_ready = sem("w_low_ready")
        gate_up_ready = sem("gate_up_ready")
        square_ready = sem("gate_square_ready")
        cubic_ready = sem("cubic_ready")
        tanh_ready = sem("tanh_ready")
        gated_ready = sem("gated_ready")
        product_ready = sem("product_ready")
        inner_high_ready = sem("inner_high_ready")
        inner_low_ready = sem("inner_low_ready")
        down_ready = sem("down_ready")
        down_free = sem("down_free")
        stored = sem("stored")

        block = ctx.enter_context(nc.Block())

        @block.sync
        def _(sp):
            def load_words(g, piece):
                sp.dma_start(words[:, piece, :], packed[g, piece]).then_inc(words_loaded[piece], 16)
                sp.dma_start(word_scales[:, piece, :],
                             scales[g, piece].unsqueeze(1).broadcast_to([SCALE_ROWS, P // SCALE_ROWS, PIECE]))\
                  .then_inc(words_loaded[piece], 16)

            if x_in is not None:
                sp.dma_start(x[:, :, cols(0, TB)], x_in[:, :, cols(0, TB)]).then_inc(x_loaded[0], 16)
            for piece in range(NPIECE):
                load_words(0, piece)
            if x_in is not None:
                for tb in range(1, NTB):
                    sp.dma_start(x[:, :, cols(tb, TB)], x_in[:, :, cols(tb, TB)]).then_inc(x_loaded[tb], 16)
            with sp.Fori(1, NGROUP) as g:
                for piece in range(NPIECE):
                    sp.wait_ge(weight_ready, NPIECE * g + (piece + 1 - NPIECE))
                    load_words(g, piece)
            if x_out is not None:
                for tb in range(NTB):
                    st = NTB * (NGROUP - 1) + tb
                    sp.wait_ge(down_free, KT * (st + 1) + KT)
                    sp.dma_start(x_out[:, :, cols(tb, TB)], x[:, :, cols(tb, TB)]).then_inc(stored, 16)
                sp.wait_ge(stored, 16 * NTB)

        @block.tensor
        def _(pe):
            def gate_up(gg, s, tb, first=False):
                for m in range(2):
                    if not first:
                        pe.wait_ge(product_ready, 16 * gg + (8 * s + 2 * tb + m - 1))
                    if m == 0:
                        pe.wait_ge(n.low_ready, tb + 1)
                        if tb == 0:
                            pe.wait_ge(w_low_ready, 6 * gg + (3 * s + 2))
                    for out, piece in ((gate_bank[m], GATE), (up_bank[m], UP)):
                        for k in range(KT):
                            c, b = divmod(k, 2)
                            w = slice(c * GROUP + m * P, c * GROUP + (m + 1) * P)
                            last = split_products(
                                pe, out, w_high[s][:, b, piece, w], w_low[s][:, b, piece, w],
                                x_high[:, k, cols(tb, TB)], x_low[:, k, cols(tb, TB)],
                                k == 0, k == KT - 1)
                    last.then_inc(gate_up_ready, 1)

            def down(gg, s, tb):
                pe.wait_ge(inner_low_ready, 16 * gg + (8 * s + 2 * tb + 2))
                if tb == 0:
                    pe.wait_ge(w_low_ready, 6 * gg + (3 * s + 3))
                for k in range(KT):
                    pe.wait_ge(down_free, 32 * gg + (16 * s + 4 * tb + k + 1))
                    for m in range(2):
                        last = split_products(
                            pe, down_bank[k], w_high[s][:, m, DOWN, cols(k, P)],
                            w_low[s][:, m, DOWN, cols(k, P)],
                            inner[:, tb % 2, m, 0, :], inner[:, tb % 2, m, 1, :], m == 0, m == 1)
                    last.then_inc(down_ready, 1)

            def group(gg, s, last_group):
                for tb in range(NTB):
                    if tb < NTB - 1:
                        gate_up(gg, s, tb + 1)
                    elif not last_group:
                        gate_up(gg + s, 1 - s, 0)
                    down(gg, s, tb)

            norm_tensor(pe, n, x_loaded)
            gate_up(0, 0, 0, first=True)
            with pe.Fori(0, NGROUP // 2 - 1) as gg:
                group(gg, 0, False)
                group(gg, 1, False)
            group(NGROUP // 2 - 1, 0, False)
            group(NGROUP // 2 - 1, 1, True)

        @block.vector
        def _(dve):
            def unpack(gg, s, piece, first=False):
                q = 3 * s + piece
                dve.wait_ge(words_loaded[piece], 64 * gg + 32 * (s + 1))
                a, b = nibbles[:, 0, :], nibbles[:, 1, :]
                w = words[:, piece, :]
                dve.tensor_scalar(a, w, 0xF0, 12, ALU.bitwise_and, ALU.logical_shift_left)\
                   .then_inc(nibbles_ready, 1)
                dve.wait_ge(nibbles_ready, 24 * gg + (4 * q + 1))
                dve.scalar_tensor_tensor(out=b, in0=w, scalar=0xF, in1=a, op0=ALU.bitwise_and,
                                         op1=ALU.bitwise_or).then_inc(nibbles_ready, 1)
                dve.wait_ge(nibbles_ready, 24 * gg + (4 * q + 2))
                dve.scalar_tensor_tensor(out=a, in0=b, scalar=3, in1=b, op0=ALU.logical_shift_left,
                                         op1=ALU.bitwise_or).then_inc(nibbles_ready, 1)
                dve.wait_ge(nibbles_ready, 24 * gg + (4 * q + 3))
                dve.tensor_scalar(b, a, 0x00470047, 9, ALU.bitwise_and, ALU.logical_shift_left)\
                   .then_inc(nibbles_ready, 1)
                dve.wait_ge(nibbles_ready, 24 * gg + (4 * q + 4))
                if not first:
                    dve.wait_ge(w_low_ready, 6 * gg + (q - 1))
                halves = b.bitcast(F16).rearrange("p (w b) -> p b w", b=2)
                dve.tensor_tensor(weight[:, q % 2, :, :], halves,
                                  word_scales[:, piece, :].unsqueeze(1).broadcast_to([P, 2, PIECE]),
                                  ALU.mult).then_inc(weight_ready, 1)

            def gelu_tiles(gg, s, tb, first=False):
                for m in range(2):
                    i = 8 * s + 2 * tb + m
                    dve.wait_ge(square_ready, 16 * gg + (i + 1))
                    dve.scalar_tensor_tensor(out=cubic[m], in0=square[m], scalar=1.0 / GELU_A,
                                             in1=gate_bank[m], op0=ALU.add, op1=ALU.mult)\
                       .then_inc(cubic_ready, 1)
                    dve.wait_ge(tanh_ready, 16 * gg + (i + 1))
                    dve.scalar_tensor_tensor(out=cubic[m], in0=square[m], scalar=1.0,
                                             in1=gate_bank[m], op0=ALU.add, op1=ALU.mult)\
                       .then_inc(gated_ready, 1)
                    dve.wait_ge(gated_ready, 16 * gg + (i + 1))
                    if not first:
                        dve.wait_ge(inner_low_ready, 16 * gg + (i - 1))
                    dve.tensor_tensor(product[m], cubic[m], up_bank[m], ALU.mult)\
                       .then_inc(product_ready, 1)

            def add_down(gg, s, tb):
                for k in range(KT):
                    dve.wait_ge(down_ready, 32 * gg + (16 * s + 4 * tb + k + 1))
                    dve.scalar_tensor_tensor(out=x[:, k, cols(tb, TB)], in0=down_bank[k],
                                             scalar=FFN_BACK, in1=x[:, k, cols(tb, TB)],
                                             op0=ALU.mult, op1=ALU.add).then_inc(down_free, 1)

            def group(gg, s, last_group):
                for tb in range(NTB):
                    if tb < NTB - 1:
                        gelu_tiles(gg, s, tb + 1)
                    elif not last_group:
                        gelu_tiles(gg + s, 1 - s, 0)
                    if tb < NPIECE and not last_group:
                        unpack(gg + s, 1 - s, tb)
                    add_down(gg, s, tb)

            dve.memset(averager[:], 1.0 / D).then_inc(n.constants_ready, 1)
            dve.memset(eps[:], EPS).then_inc(n.constants_ready, 1)
            for piece in range(NPIECE):
                unpack(0, 0, piece, first=(piece < 2))
            norm_vector(dve, n)
            dve.wait_ge(n.normed_ready, NTB)
            dve.memset(std[:, 0:1], 0.0).then_inc(down_free, KT)
            gelu_tiles(0, 0, 0, first=True)
            with dve.Fori(0, NGROUP // 2 - 1) as gg:
                group(gg, 0, False)
                group(gg, 1, False)
            group(NGROUP // 2 - 1, 0, False)
            group(NGROUP // 2 - 1, 1, True)

        @block.scalar
        def _(act):
            def weight_high(gg, s, piece):
                q = 3 * s + piece
                act.wait_ge(weight_ready, 6 * gg + (q + 1))
                act.activation(w_high[s][:, :, piece, :], weight[:, q % 2, :, :], ACT.Copy)\
                   .then_inc(w_high_ready, 1)

            def gelu_tiles(gg, s, tb):
                for m in range(2):
                    i = 8 * s + 2 * tb + m
                    act.wait_ge(gate_up_ready, 16 * gg + (i + 1))
                    act.activation(square[m], gate_bank[m], ACT.Square, scale=CODE).then_inc(square_ready, 1)
                    act.wait_ge(cubic_ready, 16 * gg + (i + 1))
                    act.activation(square[m], cubic[m], ACT.Tanh, scale=GELU_C * GELU_A * CODE)\
                       .then_inc(tanh_ready, 1)
                    act.wait_ge(product_ready, 16 * gg + (i + 1))
                    act.activation(inner[:, tb % 2, m, 0, :], product[m], ACT.Copy).then_inc(inner_high_ready, 1)

            def group(gg, s, last_group):
                for tb in range(NTB):
                    if tb < NTB - 1:
                        gelu_tiles(gg, s, tb + 1)
                    elif not last_group:
                        gelu_tiles(gg + s, 1 - s, 0)
                    if tb < NPIECE and not last_group:
                        weight_high(gg + s, 1 - s, tb)

            for piece in range(NPIECE):
                weight_high(0, 0, piece)
            act.wait_ge(n.constants_ready, 2)
            norm_scalar(act, n)
            act.wait_ge(n.low_ready, NTB - 1)
            gelu_tiles(0, 0, 0)
            with act.Fori(0, NGROUP // 2 - 1) as gg:
                group(gg, 0, False)
                group(gg, 1, False)
            group(NGROUP // 2 - 1, 0, False)
            group(NGROUP // 2 - 1, 1, True)

        @block.gpsimd
        def _(pool):
            def weight_low(gg, s, piece):
                q = 3 * s + piece
                pool.wait_ge(w_high_ready, 6 * gg + (q + 1))
                pool.tensor_tensor(w_low[s][:, :, piece, :], weight[:, q % 2, :, :],
                                   f32(w_high[s][:, :, piece, :]), ALU.subtract).then_inc(w_low_ready, 1)

            def gelu_tiles(gg, s, tb):
                for m in range(2):
                    pool.wait_ge(inner_high_ready, 16 * gg + (8 * s + 2 * tb + m + 1))
                    pool.tensor_tensor(inner[:, tb % 2, m, 1, :], product[m],
                                       f32(inner[:, tb % 2, m, 0, :]), ALU.subtract)\
                        .then_inc(inner_low_ready, 1)

            def group(gg, s, last_group):
                for tb in range(NTB):
                    if tb < NTB - 1:
                        gelu_tiles(gg, s, tb + 1)
                    elif not last_group:
                        gelu_tiles(gg + s, 1 - s, 0)
                    if tb < NPIECE and not last_group:
                        weight_low(gg + s, 1 - s, tb)

            for piece in range(NPIECE):
                weight_low(0, 0, piece)
            norm_gpsimd(pool, n)
            gelu_tiles(0, 0, 0)
            with pool.Fori(0, NGROUP // 2 - 1) as gg:
                group(gg, 0, False)
                group(gg, 1, False)
            group(NGROUP // 2 - 1, 0, False)
            group(NGROUP // 2 - 1, 1, True)


def project_in(nc, x, bank, w_v, b_v, w_qk, b_qk, qk_parts, v_parts):
    with ExitStack() as ctx:
        def sb(name, shape, dtype):
            return ctx.enter_context(nc.sbuf_tensor(name, shape, dtype))

        def sem(name):
            return ctx.enter_context(nc.semaphore(name))

        RING = 4
        NTILES = 2 * KT
        x_high = sb("qkv_x_high", [P, KT, TOKENS], F32R)
        x_low = sb("qkv_x_low", [P, KT, TOKENS], F32R)
        centred = sb("qkv_centred", [P, 2, KT, TB], F32)
        square = sb("qkv_square", [P, 2, TB], F32)
        std = sb("qkv_std", [P, TB], F32)
        averager = sb("qkv_averager", [P, P], F32)
        eps = sb("qkv_eps", [P, 1], F32)
        wv = sb("wv", [P, KT, D], F32)
        wv_high = sb("wv_high", [P, KT, D], F32R)
        wv_low = sb("wv_low", [P, KT, D], F32R)
        wt = sb("wt", [P, 2, KT, P], F32)
        wt_high = [sb(f"wt_high{s}", [P, KT, P], F32R) for s in range(2)]
        wt_low = [sb(f"wt_low{s}", [P, KT, P], F32R) for s in range(2)]
        v_bias = sb("v_bias", [P, D], F32)
        qk_bias = sb("qk_bias", [P, NTILES], F32)
        full = sb("full", [P, 2, TB], F32)
        parts = sb("parts", [P, RING, 2, TB], F32R)

        n = Norm(nc, ctx, "qkv", x, x_high, x_low, [centred[:, 0, :, :], centred[:, 1, :, :]],
                 square, std, averager, eps, bank[4:6], bank[6:8])
        wv_loaded = sem("wv_loaded")
        bias_loaded = sem("bias_loaded")
        wt_loaded = [sem(f"wt_loaded{s}") for s in range(2)]
        wv_high_ready = sem("wv_high_ready")
        wv_low_ready = sem("wv_low_ready")
        wt_high_ready = sem("wt_high_ready")
        wt_low_ready = sem("wt_low_ready")
        item_ready = sem("item_ready")
        full_ready = sem("full_ready")
        part_high_ready = sem("part_high_ready")
        part_low_ready = sem("part_low_ready")
        stored = [sem(f"parts_stored{s}") for s in range(RING)]

        block = ctx.enter_context(nc.Block())

        @block.sync
        def _(sp):
            def load_tile(e, s):
                sp.dma_start(wt[:, s, :, :], w_qk[e]).then_inc(wt_loaded[s], 16)

            sp.dma_start(wv[:], w_v).then_inc(wv_loaded, 16)
            sp.dma_start(v_bias[:], b_v.partition_broadcast(P)).then_inc(bias_loaded, 16)
            sp.dma_start(qk_bias[:], b_qk).then_inc(bias_loaded, 16)
            load_tile(0, 0)
            load_tile(1, 1)
            for tt in range(TT):
                sp.wait_ge(part_low_ready, tt + 1)
                sp.dma_start(v_parts[:, :, tt, :].rearrange("h p c -> p h c"),
                             f32(parts[:, tt % RING]).rearrange("p l (h c) -> p (l h) c", h=HEADS // 2))\
                  .then_inc(stored[tt % RING], 16)

            def store_tile(ep, s, tb):
                sp.wait_ge(part_low_ready, 8 * ep + (TT + 4 * s + tb + 1))
                sp.dma_start(
                    qk_parts[:, bass.ds(2 * P * ep + s * P, P), cols(tb, TB)].rearrange("l e t -> e l t"),
                    f32(parts[:, tb])).then_inc(stored[tb], 16)

            def pair(ep, last_pair):
                for s in range(2):
                    for tb in range(NTB):
                        store_tile(ep, s, tb)
                    if not last_pair:
                        sp.wait_ge(wt_low_ready, 2 * ep + (s + 1))
                        load_tile(2 * ep + (s + 2), s)

            with sp.Fori(0, NTILES // 2 - 1) as ep:
                pair(ep, False)
            pair(NTILES // 2 - 1, True)
            for s in range(RING):
                sp.wait_ge(stored[s], 16 * (TT + NTILES * NTB) // RING)

        @block.tensor
        def _(pe):
            norm_tensor(pe, n, None)
            pe.wait_ge(wv_low_ready, 1)
            for tt in range(TT):
                if tt % NTB == 0:
                    pe.wait_ge(n.low_ready, tt // NTB + 1)
                if tt >= RING:
                    pe.wait_ge(full_ready, tt - RING + 1)
                for k in range(KT):
                    pe.matmul(bank[tt % RING], x_high[:, k, cols(tt, P)], wv_high[:, k, :],
                              start=(k == 0), stop=False)
                    pe.matmul(bank[tt % RING], x_low[:, k, cols(tt, P)], wv_high[:, k, :],
                              start=False, stop=False)
                    last = pe.matmul(bank[tt % RING], x_high[:, k, cols(tt, P)], wv_low[:, k, :],
                                     start=False, stop=(k == KT - 1))
                last.then_inc(item_ready, 1)
            with pe.Fori(0, NTILES // 2) as ep:
                for s in range(2):
                    pe.wait_ge(wt_low_ready, 2 * ep + (s + 1))
                    for tb in range(NTB):
                        pe.wait_ge(full_ready, 8 * ep + (TT + 4 * s + tb - RING + 1))
                        for k in range(KT):
                            last = split_products(pe, bank[tb], wt_high[s][:, k, :], wt_low[s][:, k, :],
                                                  x_high[:, k, cols(tb, TB)], x_low[:, k, cols(tb, TB)],
                                                  k == 0, k == KT - 1)
                        last.then_inc(item_ready, 1)

        @block.vector
        def _(dve):
            dve.memset(averager[:], 1.0 / D).then_inc(n.constants_ready, 1)
            dve.memset(eps[:], EPS).then_inc(n.constants_ready, 1)
            norm_vector(dve, n)
            dve.wait_ge(bias_loaded, 32)
            for tt in range(TT):
                dve.wait_ge(item_ready, tt + 1)
                if tt >= 2:
                    dve.wait_ge(part_low_ready, tt - 1)
                dve.tensor_tensor(full[:, tt % 2, :], bank[tt % RING], v_bias[:], ALU.add)\
                   .then_inc(full_ready, 1)
            with dve.Fori(0, NTILES // 2) as ep:
                for s in range(2):
                    for tb in range(NTB):
                        i = TT + 4 * s + tb
                        dve.wait_ge(item_ready, 8 * ep + (i + 1))
                        dve.wait_ge(part_low_ready, 8 * ep + (i - 1))
                        dve.tensor_scalar(full[:, tb % 2, :], bank[tb],
                                          qk_bias[:, bass.ds(2 * ep + s, 1)], None, ALU.add)\
                           .then_inc(full_ready, 1)

        @block.scalar
        def _(act):
            def tile_high(ep, s):
                act.wait_ge(wt_loaded[s], 16 * ep + 16)
                act.wait_ge(item_ready, 8 * ep + (TT + 4 * (s - 1)))
                act.activation(wt_high[s][:], wt[:, s, :, :], ACT.Copy).then_inc(wt_high_ready, 1)

            def pair(ep, last_pair):
                for s in range(2):
                    if not (last_pair and s == 1):
                        tile_high(ep + s, 1 - s)
                    for tb in range(NTB):
                        i = TT + 4 * s + tb
                        act.wait_ge(full_ready, 8 * ep + (i + 1))
                        act.wait_ge(stored[tb], 32 * ep + 16 * (i // RING))
                        act.activation(parts[:, tb, 0, :], full[:, tb % 2, :], ACT.Copy)\
                           .then_inc(part_high_ready, 1)

            act.wait_ge(wv_loaded, 16)
            act.activation(wv_high[:], wv[:], ACT.Copy).then_inc(wv_high_ready, 1)
            act.wait_ge(n.constants_ready, 2)
            norm_scalar(act, n)
            act.wait_ge(wt_loaded[0], 16)
            act.activation(wt_high[0][:], wt[:, 0, :, :], ACT.Copy).then_inc(wt_high_ready, 1)
            for tt in range(TT):
                act.wait_ge(full_ready, tt + 1)
                if tt >= RING:
                    act.wait_ge(stored[tt % RING], 16 * (tt // RING))
                act.activation(parts[:, tt % RING].rearrange("p a (h l d) -> p (a h) l d", l=2, d=HD)[:, :, 0, :],
                               full[:, tt % 2, :].rearrange("p (h d) -> p h d", d=HD), ACT.Copy)\
                   .then_inc(part_high_ready, 1)
            with act.Fori(0, NTILES // 2 - 1) as ep:
                pair(ep, False)
            pair(NTILES // 2 - 1, True)

        @block.gpsimd
        def _(pool):
            def tile_low(ep, s):
                pool.wait_ge(wt_high_ready, 2 * ep + (s + 1))
                pool.tensor_tensor(wt_low[s][:], wt[:, s, :, :], f32(wt_high[s][:]), ALU.subtract)\
                    .then_inc(wt_low_ready, 1)

            def pair(ep, last_pair):
                for s in range(2):
                    if not (last_pair and s == 1):
                        tile_low(ep + s, 1 - s)
                    for tb in range(NTB):
                        pool.wait_ge(part_high_ready, 8 * ep + (TT + 4 * s + tb + 1))
                        pool.tensor_tensor(parts[:, tb, 1, :], full[:, tb % 2, :],
                                           f32(parts[:, tb, 0, :]), ALU.subtract).then_inc(part_low_ready, 1)

            pool.wait_ge(wv_high_ready, 1)
            pool.tensor_tensor(wv_low[:], wv[:], f32(wv_high[:]), ALU.subtract).then_inc(wv_low_ready, 1)
            norm_gpsimd(pool, n)
            tile_low(0, 0)
            for tt in range(TT):
                by_head = parts[:, tt % RING].rearrange("p a (h l d) -> p (a h) l d", l=2, d=HD)
                pool.wait_ge(part_high_ready, tt + 1)
                pool.tensor_tensor(by_head[:, :, 1, :], full[:, tt % 2, :].rearrange("p (h d) -> p h d", d=HD),
                                   f32(by_head[:, :, 0, :]), ALU.subtract).then_inc(part_low_ready, 1)
            with pool.Fori(0, NTILES // 2 - 1) as ep:
                pair(ep, False)
            pair(NTILES // 2 - 1, True)


TILES = [(b, kt) for b in range(NTB) for kt in range(4 * b + 4)]
CHUNKS = [(b, qt, c) for b in range(NTB) for qt in range(4 * b, 4 * b + 4) for c in range(b + 1)]
SLOTS = len(TILES)
HEADS_IN_LOOP = 3
BY_GPSIMD = 2


def chunks_of_slot(t):
    return [m for m in range(SLOTS) if m * (SLOTS - 3) // SLOTS == t]


MAXED_AT = {[t for t in range(SLOTS) if b * (b + 1) * 2 + 4 * (b + 1) - 1 in chunks_of_slot(t)][0]: b
            for b in range(NTB)}
ROWS_AT = {t + 3: b for t, b in MAXED_AT.items()}


def low_by_gpsimd(t):
    return t % BY_GPSIMD == 1


def low_rank(t):
    mine = [u for u in range(SLOTS) if low_by_gpsimd(u) == low_by_gpsimd(t)]
    return mine.index(t) + 1, len(mine)


def attention(nc, bank, qk_parts, v_parts, o_parts, sums):
    with ExitStack() as ctx:
        def sb(name, shape, dtype):
            return ctx.enter_context(nc.sbuf_tensor(name, shape, dtype))

        def sem(name):
            return ctx.enter_context(nc.semaphore(name))

        STACK = 3 * HD
        ROWS = STACK + 2
        queries = [sb(f"queries{i}", [ROWS, TOKENS], F32R) for i in range(3)]
        keys = [sb(f"keys{i}", [ROWS, TOKENS], F32R) for i in range(3)]
        values = [sb(f"values{i}", [P, TT, VCOLS], F32R) for i in range(3)]
        probs = sb("probs", [P, 4, TB], F32)
        probs_high = sb("probs_high", [P, 4, TB], F32R)
        probs_low = sb("probs_low", [P, 4, TB], F32R)
        chunk_max = sb("chunk_max", [P, 2, 4, NTB], F32)
        minus_max = sb("minus_max", [P, 2, 4], F32)
        max_parts = sb("max_parts", [P, 2, 4, 2], F32R)
        heads_out = sb("heads_out", [VCOLS, 2, TB], F32)
        ident = sb("ident", [P, P], F32)
        ident_r = sb("ident_r", [P, P], F32R)
        ident_b = sb("ident_b", [P, P], BF16)
        key_mask = sb("key_mask", [P, P], F32)
        query_mask = sb("query_mask", [P, P], F32)
        key_mask_b = sb("key_mask_b", [P, P], BF16)
        query_mask_b = sb("query_mask_b", [P, P], BF16)

        start = sb("start", [P, 3], F32)

        score_bank, max_bank, out_bank, row_bank = bank[0:2], bank[2:4], bank[4:6], bank[6]

        filled = sem("filled")
        constants_ready = sem("attn_constants_ready")
        loaded = [sem(f"head_loaded{i}") for i in range(3)]
        max_scores_ready = sem("max_scores_ready")
        max_taken = sem("max_taken")
        max_steps = sem("max_steps")
        max_parts_ready = sem("max_parts_ready")
        row_bank_ready = sem("row_bank_ready")
        rows_ready = sem("rows_ready")
        scores_ready = sem("scores_ready")
        probs_ready = sem("probs_ready")
        probs_high_ready = sem("probs_high_ready")
        low_by_dve = sem("low_by_dve")
        low_by_pool = sem("low_by_pool")
        out_ready = sem("out_ready")
        out_free = sem("out_free")
        out_stored = [sem(f"out_stored{i}") for i in range(2)]

        LOAD = 7 * 16

        block = ctx.enter_context(nc.Block())

        @block.sync
        def _(sp):
            def load(h, i):
                for part, row in ((0, 0), (1, HD), (0, 2 * HD)):
                    sp.dma_start(f32(queries[i][row:row + HD, :]),
                                 qk_parts[part, bass.ds(h * HD, HD), :]).then_inc(loaded[i], 16)
                for part, row in ((0, 0), (0, HD), (1, 2 * HD)):
                    sp.dma_start(f32(keys[i][row:row + HD, :]),
                                 qk_parts[part, bass.ds(h * HD + D, HD), :]).then_inc(loaded[i], 16)
                sp.dma_start(f32(values[i][:, :, 0:2 * HD]),
                             v_parts[bass.ds(h, 1)].rearrange("o p t c -> (o p) t c")).then_inc(loaded[i], 16)

            def store(h0, s):
                for b in range(NTB):
                    sp.wait_ge(out_free, 4 * h0 + (4 * s + b + 1 + 2))
                    sp.dma_start(o_parts[bass.ds(h0 + s, 1), :, cols(b, TB)].rearrange("o c t -> (o c) t"),
                                 heads_out[0:2 * HD, b % 2, :]).then_inc(out_stored[b % 2], 16)
                    sp.dma_start(sums[bass.ds(h0 + s, 1), cols(b, TB)],
                                 heads_out[2 * HD:VCOLS, b % 2, :]).then_inc(out_stored[b % 2], 16)

            for h in range(3):
                load(h, h)
            with sp.Fori(0, HEADS // 3 - 1) as hp:
                for s in range(3):
                    store(3 * hp, s)
                    load(3 * hp + (s + 3), s)
            store(HEADS - 4, 0)
            load(HEADS - 1, 0)
            for s in range(1, 4):
                store(HEADS - 4, s)
            for i in range(2):
                sp.wait_ge(out_stored[i], 32 * (HEADS * NTB // 2 + 1))

        @block.tensor
        def _(pe):
            def max_chunk(hp, s, m, first=False):
                b, qt, c = CHUNKS[m]
                i = s % 3
                if m == 0:
                    pe.wait_ge(loaded[i], LOAD * hp + LOAD * (s // 3 + 1))
                if not (first and m < 2):
                    pe.wait_ge(max_taken, 120 * hp + (SLOTS * s + m - 1))
                width = TB if c < b else (qt % 4 + 1) * P
                out = max_bank[m % 2]
                last = pe.matmul(out[:, 0:width], queries[i][0:STACK, cols(qt, P)],
                                 keys[i][0:STACK, c * TB:c * TB + width], start=True, stop=(c < b),
                                 skip_group_check=True)
                if c == b:
                    last = pe.matmul(out[:, width - P:width], ident_b[:], query_mask_b[:],
                                     start=False, stop=True, skip_group_check=True)
                last.then_inc(max_scores_ready, 1)

            def rows(hp, s, b, first=False):
                n = 4 * s + b
                pe.wait_ge(max_parts_ready, 12 * hp + (n + 1))
                if not (first and b == 0):
                    pe.wait_ge(rows_ready, 12 * hp + n)
                for j in range(4):
                    last = pe.matmul(row_bank[0:2, cols(j, P)], max_parts[:, b % 2, j, :], ident_r[:],
                                     start=True, stop=True, skip_group_check=True)
                last.then_inc(row_bank_ready, 1)

            def scores(hp, s, t, first=False):
                b, kt = TILES[t]
                i = s % 3
                if kt == 0:
                    pe.wait_ge(rows_ready, 12 * hp + (4 * s + b + 1))
                if not (first and t < 2):
                    pe.wait_ge(probs_high_ready, 120 * hp + (SLOTS * s + t - 1))
                q0 = max(b * TB, kt * P)
                width = (b + 1) * TB - q0
                last = pe.matmul(score_bank[t % 2][:, 0:width], keys[i][0:ROWS, cols(kt, P)],
                                 queries[i][0:ROWS, q0:q0 + width], start=True, stop=(kt < 4 * b),
                                 skip_group_check=True)
                if kt >= 4 * b:
                    last = pe.matmul(score_bank[t % 2][:, 0:P], ident_b[:], key_mask_b[:],
                                     start=False, stop=True, skip_group_check=True)
                last.then_inc(scores_ready, 1)

            def with_values(hp, s, t):
                b, kt = TILES[t]
                i = s % 3
                if kt == 0:
                    pe.wait_ge(out_free, 12 * hp + (4 * s + b + 1))
                rank, per_head = low_rank(t)
                pe.wait_ge(low_by_pool if low_by_gpsimd(t) else low_by_dve,
                           3 * per_head * hp + (per_head * s + rank))
                off = max(0, kt * P - b * TB)
                out = out_bank[b % 2][0:VCOLS, off:TB]
                pe.matmul(out, values[i][:, kt, :], probs_high[:, t % 4, 0:TB - off],
                          start=(kt == 0), stop=False, skip_group_check=True)
                last = pe.matmul(out, values[i][:, kt, :], probs_low[:, t % 4, 0:TB - off],
                                 start=False, stop=(kt == 4 * b + 3), skip_group_check=True)
                if kt == 4 * b + 3:
                    last.then_inc(out_ready, 1)

            def head(hp, s, has_next):
                for t in range(SLOTS):
                    if t + 2 < SLOTS:
                        scores(hp, s, t + 2)
                    elif has_next:
                        scores(hp, s + 1, t + 2 - SLOTS)
                    if has_next:
                        for m in chunks_of_slot(t):
                            max_chunk(hp, s + 1, m)
                        if t in ROWS_AT:
                            rows(hp, s + 1, ROWS_AT[t])
                    with_values(hp, s, t)

            pe.wait_ge(constants_ready, 10)
            for b in range(NTB):
                for m, chunk in enumerate(CHUNKS):
                    if chunk[0] == b:
                        max_chunk(0, 0, m, first=True)
                rows(0, 0, b, first=True)
            scores(0, 0, 0, first=True)
            scores(0, 0, 1, first=True)
            with pe.Fori(0, HEADS // 3) as hp:
                for s in range(3):
                    head(hp, s, True)
            head(HEADS // 3, 0, False)

        @block.vector
        def _(dve):
            def take_max(hp, s, m):
                b, qt, c = CHUNKS[m]
                dve.wait_ge(max_scores_ready, 120 * hp + (SLOTS * s + m + 1))
                width = TB if c < b else (qt % 4 + 1) * P
                dve.tensor_reduce(chunk_max[:, b % 2, qt % 4, c:c + 1], max_bank[m % 2][:, 0:width],
                                  AX.X, ALU.max).then_inc(max_taken, 1)

            def split_max(hp, s, b, first=False):
                n = 4 * s + b
                m = [chunk[0] for chunk in CHUNKS].index(b) + 4 * (b + 1)
                dve.wait_ge(max_taken, 120 * hp + (SLOTS * s + m))
                dve.tensor_reduce(minus_max[:, b % 2, :], chunk_max[:, b % 2, :, 0:b + 1], AX.X, ALU.max,
                                  negate=True).then_inc(max_steps, 1)
                dve.wait_ge(max_steps, 24 * hp + (2 * n + 1))
                if not (first and b < 2):
                    dve.wait_ge(row_bank_ready, 12 * hp + (n - 1))
                dve.tensor_copy(max_parts[:, b % 2, :, 0], minus_max[:, b % 2, :]).then_inc(max_steps, 1)
                dve.wait_ge(max_steps, 24 * hp + (2 * n + 2))
                dve.tensor_tensor(max_parts[:, b % 2, :, 1], minus_max[:, b % 2, :],
                                  f32(max_parts[:, b % 2, :, 0]), ALU.subtract).then_inc(max_parts_ready, 1)

            def low(hp, s, t):
                if low_by_gpsimd(t):
                    return
                b, kt = TILES[t]
                width = TB - max(0, kt * P - b * TB)
                dve.wait_ge(probs_high_ready, 120 * hp + (SLOTS * s + t + 1))
                dve.tensor_tensor(probs_low[:, t % 4, 0:width], probs[:, t % 4, 0:width],
                                  f32(probs_high[:, t % 4, 0:width]), ALU.subtract).then_inc(low_by_dve, 1)

            def head(hp, s, has_next):
                for t in range(SLOTS):
                    if has_next:
                        for m in chunks_of_slot(t):
                            take_max(hp, s + 1, m)
                        if t in MAXED_AT:
                            split_max(hp, s + 1, MAXED_AT[t])
                    if t + 1 < SLOTS:
                        low(hp, s, t + 1)
                    elif has_next:
                        low(hp, s + 1, 0)

            for i in range(3):
                dve.memset(f32(keys[i][STACK:ROWS, :]), 1.0).then_inc(constants_ready, 1)
                dve.memset(f32(values[i][:, :, 2 * HD:VCOLS]), 1.0).then_inc(constants_ready, 1)
            dve.wait_ge(filled, 6)
            dve.tensor_copy(ident_r[:], ident[:]).then_inc(constants_ready, 1)
            dve.tensor_copy(ident_b[:], ident[:]).then_inc(constants_ready, 1)
            dve.tensor_copy(key_mask_b[:], key_mask[:]).then_inc(constants_ready, 1)
            dve.tensor_copy(query_mask_b[:], query_mask[:]).then_inc(constants_ready, 1)
            for b in range(NTB):
                for m, chunk in enumerate(CHUNKS):
                    if chunk[0] == b:
                        take_max(0, 0, m)
                split_max(0, 0, b, first=True)
            low(0, 0, 0)
            with dve.Fori(0, HEADS // 3) as hp:
                for s in range(3):
                    head(hp, s, True)
            head(HEADS // 3, 0, False)

        @block.scalar
        def _(act):
            def rows(hp, s, b):
                act.wait_ge(row_bank_ready, 12 * hp + (4 * s + b + 1))
                act.activation(queries[s % 3][STACK:ROWS, cols(b, TB)], row_bank[0:2, :], ACT.Copy)\
                   .then_inc(rows_ready, 1)

            def exps(hp, s, t):
                b, kt = TILES[t]
                width = TB - max(0, kt * P - b * TB)
                act.wait_ge(scores_ready, 120 * hp + (SLOTS * s + t + 1))
                act.activation(probs[:, t % 4, 0:width], score_bank[t % 2][:, 0:width], ACT.Exp,
                               scale=SM_SCALE).then_inc(probs_ready, 1)
                act.activation(probs_high[:, t % 4, 0:width], score_bank[t % 2][:, 0:width], ACT.Exp,
                               scale=SM_SCALE).then_inc(probs_high_ready, 1)

            def take_out(hp, s, b):
                act.wait_ge(out_ready, 12 * hp + (4 * s + b + 1))
                act.wait_ge(out_stored[b % 2], 192 * hp + 32 * ((4 * s + b) // 2 + 1))
                act.activation(heads_out[:, b % 2, :], out_bank[b % 2][0:VCOLS, :], ACT.Copy)\
                   .then_inc(out_free, 1)

            def head(hp, s, has_next):
                for t in range(SLOTS):
                    if t + 2 < SLOTS:
                        exps(hp, s, t + 2)
                    elif has_next:
                        exps(hp, s + 1, t + 2 - SLOTS)
                    if has_next and t in ROWS_AT:
                        rows(hp, s + 1, ROWS_AT[t])
                    b, kt = TILES[t - 1]
                    if t > 0 and kt == 4 * b + 3:
                        take_out(hp, s, b)
                take_out(hp, s, NTB - 1)

            for b in range(NTB):
                rows(0, 0, b)
            exps(0, 0, 0)
            exps(0, 0, 1)
            with act.Fori(0, HEADS // 3) as hp:
                for s in range(3):
                    head(hp, s, True)
            head(HEADS // 3, 0, False)

        @block.gpsimd
        def _(pool):
            def low(hp, s, t):
                if not low_by_gpsimd(t):
                    return
                b, kt = TILES[t]
                width = TB - max(0, kt * P - b * TB)
                pool.wait_ge(probs_high_ready, 120 * hp + (SLOTS * s + t + 1))
                pool.tensor_tensor(probs_low[:, t % 4, 0:width], probs[:, t % 4, 0:width],
                                   f32(probs_high[:, t % 4, 0:width]), ALU.subtract).then_inc(low_by_pool, 1)

            def head(hp, s):
                for t in range(SLOTS):
                    low(hp, s, t)

            pool.memset(ident[:], 0.0).then_inc(filled, 1)
            pool.memset(key_mask[:], 0.0).then_inc(filled, 1)
            pool.memset(query_mask[:], 0.0).then_inc(filled, 1)
            pool.wait_ge(filled, 3)
            pool.affine_select(out=ident[:], in_=ident[:], compare_op=ALU.not_equal, fill=1.0, base=0,
                               pattern=[[-1, P]], channel_multiplier=1).then_inc(filled, 1)
            pool.affine_select(out=key_mask[:], in_=key_mask[:], compare_op=ALU.is_ge, fill=MASKED, base=0,
                               pattern=[[1, P]], channel_multiplier=-1).then_inc(filled, 1)
            pool.affine_select(out=query_mask[:], in_=query_mask[:], compare_op=ALU.is_ge, fill=MASKED,
                               base=0, pattern=[[-1, P]], channel_multiplier=1).then_inc(filled, 1)
            pool.memset(start[:, 0:1], 0.0).then_inc(out_free, 2)
            pool.memset(start[:, 1:2], 0.0).then_inc(out_stored[0], 32)
            pool.memset(start[:, 2:3], 0.0).then_inc(out_stored[1], 32)
            with pool.Fori(0, HEADS // 3) as hp:
                for s in range(3):
                    head(hp, s)
            head(HEADS // 3, 0)


def project_out(nc, x, bank, o_parts, sums, inverses, w_out, b_out):
    with ExitStack() as ctx:
        def sb(name, shape, dtype):
            return ctx.enter_context(nc.sbuf_tensor(name, shape, dtype))

        def sem(name):
            return ctx.enter_context(nc.semaphore(name))

        HPT = P // HD
        SUMS = HEADS * TOKENS // P
        wo = sb("wo", [P, KT, D], F32)
        wo_high = sb("wo_high", [P, KT, D], F32R)
        wo_low = sb("wo_low", [P, KT, D], F32R)
        out_bias = sb("out_bias", [P, KT], F32)
        inverse_all = sb("inverse_all", [P, SUMS], F32)
        from_high = sb("from_high", [P, 2, KT, TB], F32)
        from_low = sb("from_low", [P, 2, KT, TB], F32)
        inverse = sb("inverse", [P, 2, KT, TB], F32)
        normed_high = sb("normed_high", [P, 2, KT, TB], F32R)
        normed_low = sb("normed_low", [P, 2, KT, TB], F32R)

        sums_loaded = sem("sums_loaded")
        inverse_ready = sem("inverse_ready")
        inverse_stored = sem("inverse_stored")
        wo_loaded = sem("wo_loaded")
        bias_loaded = sem("out_bias_loaded")
        wo_high_ready = sem("wo_high_ready")
        wo_low_ready = sem("wo_low_ready")
        block_loaded = [sem(f"block_loaded{i}") for i in range(2)]
        added = sem("added")
        scaled = sem("scaled")
        scaled_high = sem("scaled_high")
        scaled_low = sem("scaled_low")
        out_tile_ready = sem("out_tile_ready")
        x_updated = sem("x_updated")

        block = ctx.enter_context(nc.Block())

        @block.sync
        def _(sp):
            sp.dma_start(inverse_all[:], sums.rearrange("h (a t) -> (h a) t", t=SUMS)).then_inc(sums_loaded, 16)
            sp.dma_start(wo[:], w_out).then_inc(wo_loaded, 16)
            sp.dma_start(out_bias[:], b_out).then_inc(bias_loaded, 16)
            for tb in range(NTB):
                if tb >= 2:
                    sp.wait_ge(scaled_low, tb - 1)
                for k in range(KT):
                    for dst, row in ((from_high, 0), (from_low, HD)):
                        for hh in range(HPT):
                            sp.dma_start(dst[cols(hh, HD), tb % 2, k, :],
                                         o_parts[HPT * k + hh, row:row + HD, cols(tb, TB)])\
                              .then_inc(block_loaded[tb % 2], 16)
                if tb == 0:
                    sp.wait_ge(inverse_ready, 1)
                    sp.dma_start(inverses.rearrange("h (a t) -> (h a) t", t=SUMS), inverse_all[:])\
                      .then_inc(inverse_stored, 16)
                    sp.wait_ge(inverse_stored, 16)
                for k in range(KT):
                    sp.dma_start(inverse[:, tb % 2, k, :],
                                 inverses[cols(k, HPT), cols(tb, TB)].unsqueeze(1)
                                 .broadcast_to([HPT, HD, TB])).then_inc(block_loaded[tb % 2], 16)

        @block.tensor
        def _(pe):
            pe.wait_ge(wo_low_ready, 1)
            for tb in range(NTB):
                pe.wait_ge(scaled_low, tb + 1)
                for f in range(KT):
                    t = KT * tb + f
                    if t >= 8:
                        pe.wait_ge(x_updated, t - 7)
                    for k in range(KT):
                        last = split_products(pe, bank[t % 8], wo_high[:, k, cols(f, P)],
                                              wo_low[:, k, cols(f, P)], normed_high[:, tb % 2, k, :],
                                              normed_low[:, tb % 2, k, :], k == 0, k == KT - 1)
                    last.then_inc(out_tile_ready, 1)

        @block.vector
        def _(dve):
            def scale(tb):
                i = tb % 2
                dve.wait_ge(block_loaded[i], 16 * KT * (2 * HPT + 1) * (tb // 2 + 1))
                dve.tensor_tensor(from_high[:, i], from_high[:, i], from_low[:, i], ALU.add).then_inc(added, 1)
                dve.wait_ge(added, tb + 1)
                dve.tensor_tensor(from_high[:, i], from_high[:, i], inverse[:, i], ALU.mult).then_inc(scaled, 1)

            dve.wait_ge(sums_loaded, 16)
            dve.reciprocal(inverse_all[:], inverse_all[:]).then_inc(inverse_ready, 1)
            scale(0)
            dve.wait_ge(bias_loaded, 16)
            for tb in range(NTB):
                if tb + 1 < NTB:
                    scale(tb + 1)
                for f in range(KT):
                    t = KT * tb + f
                    dve.wait_ge(out_tile_ready, t + 1)
                    dve.scalar_tensor_tensor(out=x[:, f, cols(tb, TB)], in0=bank[t % 8],
                                             scalar=out_bias[:, f:f + 1], in1=x[:, f, cols(tb, TB)],
                                             op0=ALU.add, op1=ALU.add).then_inc(x_updated, 1)

        @block.scalar
        def _(act):
            act.wait_ge(wo_loaded, 16)
            act.activation(wo_high[:], wo[:], ACT.Copy).then_inc(wo_high_ready, 1)
            for tb in range(NTB):
                act.wait_ge(scaled, tb + 1)
                if tb >= 2:
                    act.wait_ge(out_tile_ready, KT * (tb - 1))
                act.activation(normed_high[:, tb % 2], from_high[:, tb % 2], ACT.Copy).then_inc(scaled_high, 1)

        @block.gpsimd
        def _(pool):
            pool.wait_ge(wo_high_ready, 1)
            pool.tensor_tensor(wo_low[:], wo[:], f32(wo_high[:]), ALU.subtract).then_inc(wo_low_ready, 1)
            for tb in range(NTB):
                pool.wait_ge(scaled_high, tb + 1)
                pool.tensor_tensor(normed_low[:, tb % 2], from_high[:, tb % 2],
                                   f32(normed_high[:, tb % 2]), ALU.subtract).then_inc(scaled_low, 1)


def build(nc, x_in, packed, scales, w_v, b_v, w_qk, b_qk, w_out, b_out, out):
    def scratch(name, shape):
        return nc.dram_tensor(name, shape, F32, kind="Internal").ap()

    qk_parts = scratch("qk_parts", (2, 2 * D, TOKENS))
    v_parts = scratch("v_parts", (HEADS, P, TT, 2 * HD))
    o_parts = scratch("o_parts", (HEADS, 2 * HD, TOKENS))
    sums = scratch("sums", (HEADS, TOKENS))
    inverses = scratch("inverses", (HEADS, TOKENS))
    with ExitStack() as ctx:
        x = ctx.enter_context(nc.sbuf_tensor("x", [P, KT, TOKENS], F32))
        psum = ctx.enter_context(nc.psum_tensor("psum", [P, 8, TB], F32))
        bank = [psum[:, i, :] for i in range(8)]
        ffn(nc, "ffn1", x, bank, packed, scales, x_in, None)
        project_in(nc, x, bank, w_v, b_v, w_qk, b_qk, qk_parts, v_parts)
        attention(nc, bank, qk_parts, v_parts, o_parts, sums)
        project_out(nc, x, bank, o_parts, sums, inverses, w_out, b_out)
        ffn(nc, "ffn2", x, bank, packed, scales, None, out)
def laid_out(L0_attn_x, L0_attn_w_qkv, L0_attn_b_qkv, L0_attn_w_out, L0_attn_b_out,
             L0_ffn_gate_W_packed, L0_ffn_gate_scales, L0_ffn_up_W_packed, L0_ffn_up_scales,
             L0_ffn_down_W_packed, L0_ffn_down_scales):
    import numpy as np

    def features(a):
        return a.reshape(2, P, 2, -1).transpose(1, 0, 2, 3).reshape(P, KT, -1)

    def gate_words(w):
        w = w.reshape(NGROUP, P, 2, 2, P)
        return w.transpose(0, 4, 3, 2, 1).reshape(NGROUP, P, PIECE)

    def gate_scales(s):
        s = s.reshape(NGROUP, P, 2, 2, SCALE_ROWS)
        return s.transpose(0, 4, 3, 2, 1).reshape(NGROUP, SCALE_ROWS, PIECE)

    def out_features(w):
        return w.reshape(w.shape[0], 2, P, 2).transpose(0, 1, 3, 2).reshape(w.shape[0], D)

    x = np.asarray(L0_attn_x)[0]
    down = out_features(np.asarray(L0_ffn_down_W_packed).T).reshape(NGROUP, P, PIECE)
    down_s = out_features(np.asarray(L0_ffn_down_scales).T).reshape(NGROUP, SCALE_ROWS, PIECE)
    packed = np.stack([gate_words(np.asarray(L0_ffn_gate_W_packed)),
                       gate_words(np.asarray(L0_ffn_up_W_packed)), down], axis=1)
    scales = np.stack([gate_scales(np.asarray(L0_ffn_gate_scales)),
                       gate_scales(np.asarray(L0_ffn_up_scales)), down_s], axis=1)
    w_qkv = features(np.asarray(L0_attn_w_qkv).T)
    b_qkv = np.asarray(L0_attn_b_qkv)
    arrays = {
        "x_in": features(x.T),
        "packed": packed,
        "scales": scales,
        "w_v": w_qkv[:, :, 2 * D:],
        "b_v": b_qkv[2 * D:].reshape(1, D),
        "w_qk": w_qkv[:, :, :2 * D].reshape(P, KT, 2 * KT, P).transpose(2, 0, 1, 3),
        "b_qk": b_qkv[:2 * D].reshape(2 * KT, P).T,
        "w_out": out_features(np.asarray(L0_attn_w_out).T).reshape(KT, P, D).transpose(1, 0, 2),
        "b_out": out_features(np.asarray(L0_attn_b_out).reshape(1, D)).reshape(KT, P).T,
    }
    return {name: np.ascontiguousarray(a) for name, a in arrays.items()}


def kernel(**inputs):
    import numpy as np
    import concourse.bacc as bacc
    from concourse.bass_utils import run_bass_kernel_spmd

    arrays = laid_out(**inputs)
    nc = bacc.Bacc("TRN2", target_bir_lowering=False, num_devices=1)
    args = [nc.dram_tensor(name, a.shape, mybir.dt.from_np(a.dtype), kind="ExternalInput").ap()
            for name, a in arrays.items()]
    out = nc.dram_tensor("out", (P, KT, TOKENS), F32, kind="ExternalOutput").ap()
    build(nc, *args, out)
    result = run_bass_kernel_spmd(nc, [arrays], core_ids=[0]).results[0]["out"]
    y = np.asarray(result).reshape(P, 2, 2, TOKENS).transpose(3, 1, 0, 2)
    return np.ascontiguousarray(y.reshape(1, TOKENS, D))
```

```python
from contextlib import ExitStack

import concourse.bass as bass
from concourse import mybir

ALU = mybir.AluOpType
ACT = mybir.ActivationFunctionType
AX = mybir.AxisListType
F32 = mybir.dt.float32
F32R = mybir.dt.float32r
F16 = mybir.dt.float16
BF16 = mybir.dt.bfloat16
I32 = mybir.dt.int32

P = 128
TOKENS = 2048
D = 512
KT = D // P
TB = 512
NTB = TOKENS // TB
MLP = 4096
GROUP = 256
NGROUP = MLP // GROUP
PIECE = 512
NPIECE = 3
GATE, UP, DOWN = 0, 1, 2
FP4_BLOCK = 32
SCALE_ROWS = 8
HEADS = 16
HD = D // HEADS
TT = TOKENS // P
VCOLS = 2 * HD + 1
SM_SCALE = 1.0 / float(HD) ** 0.5
EPS = 1e-5

CODE = 2.0 ** 14
GELU_A = 0.044715
GELU_C = 0.7978845608028654
FFN_BACK = CODE * CODE * CODE * 0.25
MASKED = -1e30


def f32(ap):
    return ap.bitcast(F32)


def cols(i, n):
    return slice(i * n, (i + 1) * n)


def split_products(pe, out, w_high, w_low, x_high, x_low, first, last):
    pe.matmul(out, w_high, x_high, start=first, stop=False, skip_group_check=True)
    pe.matmul(out, w_high, x_low, start=False, stop=False, skip_group_check=True)
    return pe.matmul(out, w_low, x_high, start=False, stop=last, skip_group_check=True)


class Norm:

    def __init__(self, nc, ctx, tag, x, x_high, x_low, centred, squares, pairs, std, averager, eps,
                 mean_bank, var_bank, x_loaded):
        def sem(name):
            return ctx.enter_context(nc.semaphore(f"{tag}_{name}"))

        self.x, self.x_high, self.x_low = x, x_high, x_low
        self.centred, self.squares, self.pairs, self.std = centred, squares, pairs, std
        self.averager, self.eps = averager, eps
        self.mean_bank, self.var_bank = mean_bank, var_bank
        self.x_loaded = x_loaded
        self.constants_ready = sem("constants_ready")
        self.pairs_ready = sem("pairs_ready")
        self.mean_ready = sem("mean_ready")
        self.centred_ready = sem("centred_ready")
        self.squares_ready = sem("squares_ready")
        self.square_pairs_ready = sem("square_pairs_ready")
        self.variance_ready = sem("variance_ready")
        self.std_ready = sem("std_ready")
        self.rstd_ready = sem("rstd_ready")
        self.normed_ready = sem("normed_ready")
        self.high_ready = sem("high_ready")
        self.low_ready = sem("low_ready")

    def sum_pairs(self, engine, tb):
        if self.x_loaded is not None:
            engine.wait_ge(self.x_loaded[tb], 16)
        if tb >= 1:
            engine.wait_ge(self.mean_ready, tb)
        engine.tensor_tensor(self.pairs, self.x[:, 0:2, cols(tb, TB)], self.x[:, 2:4, cols(tb, TB)],
                             ALU.add).then_inc(self.pairs_ready, 1)

    def mean(self, pe, tb):
        if tb == 0:
            pe.wait_ge(self.constants_ready, 2)
        if tb >= 2:
            pe.wait_ge(self.centred_ready, tb - 1)
        pe.wait_ge(self.pairs_ready, tb + 1)
        for k in range(2):
            last = pe.matmul(self.mean_bank[tb % 2], self.averager[:], self.pairs[:, k, :],
                             start=(k == 0), stop=(k == 1))
        last.then_inc(self.mean_ready, 1)

    def centre(self, dve, tb):
        dve.wait_ge(self.mean_ready, tb + 1)
        if tb >= 2:
            dve.wait_ge(self.low_ready, KT * (tb - 1))
        dve.tensor_tensor(self.centred[tb % 2], self.x[:, :, cols(tb, TB)],
                          self.mean_bank[tb % 2].unsqueeze(1).broadcast_to([P, KT, TB]),
                          ALU.subtract).then_inc(self.centred_ready, 1)

    def square(self, act, tb):
        act.wait_ge(self.centred_ready, tb + 1)
        if tb >= 1:
            act.wait_ge(self.variance_ready, tb)
        for k in range(KT):
            act.activation(self.squares[:, k, :], self.centred[tb % 2][:, k, :], ACT.Square)\
               .then_inc(self.squares_ready, 1)

    def sum_square_pairs(self, dve, tb):
        dve.wait_ge(self.squares_ready, KT * (tb + 1))
        dve.tensor_tensor(self.squares[:, 0:2, :], self.squares[:, 0:2, :], self.squares[:, 2:4, :],
                          ALU.add).then_inc(self.square_pairs_ready, 1)

    def variance(self, pe, tb):
        pe.wait_ge(self.square_pairs_ready, tb + 1)
        if tb >= 2:
            pe.wait_ge(self.std_ready, tb - 1)
        for k in range(2):
            last = pe.matmul(self.var_bank[tb % 2], self.averager[:], self.squares[:, k, :],
                             start=(k == 0), stop=(k == 1))
        last.then_inc(self.variance_ready, 1)

    def standard_deviation(self, act, tb):
        act.wait_ge(self.variance_ready, tb + 1)
        if tb >= 1:
            act.wait_ge(self.normed_ready, KT * tb)
        act.activation(self.std[:], self.var_bank[tb % 2], ACT.Sqrt, bias=self.eps[:]).then_inc(self.std_ready, 1)

    def scale(self, dve, tb):
        dve.wait_ge(self.std_ready, tb + 1)
        dve.reciprocal(self.std[:], self.std[:]).then_inc(self.rstd_ready, 1)
        dve.wait_ge(self.rstd_ready, tb + 1)
        for k in range(KT):
            tile = self.centred[tb % 2][:, k, :]
            dve.tensor_tensor(tile, tile, self.std[:], ALU.mult).then_inc(self.normed_ready, 1)

    def high(self, act, tb):
        for k in range(KT):
            act.wait_ge(self.normed_ready, KT * tb + k + 1)
            act.activation(self.x_high[:, k, cols(tb, TB)], self.centred[tb % 2][:, k, :], ACT.Copy)\
               .then_inc(self.high_ready, 1)

    def low(self, pool, tb):
        for k in range(KT):
            pool.wait_ge(self.high_ready, KT * tb + k + 1)
            pool.tensor_tensor(self.x_low[:, k, cols(tb, TB)], self.centred[tb % 2][:, k, :],
                               f32(self.x_high[:, k, cols(tb, TB)]), ALU.subtract).then_inc(self.low_ready, 1)


def ffn(nc, tag, x, bank, packed, scales, x_in, x_out):
    with ExitStack() as ctx:
        def sb(name, shape, dtype):
            return ctx.enter_context(nc.sbuf_tensor(f"{tag}_{name}", shape, dtype))

        def sem(name):
            return ctx.enter_context(nc.semaphore(f"{tag}_{name}"))

        x_high = sb("x_high", [P, KT, TOKENS], F32R)
        x_low = sb("x_low", [P, KT, TOKENS], F32R)
        words = sb("words", [P, NPIECE, PIECE], I32)
        word_scales = sb("word_scales", [P, NPIECE, PIECE], F32)
        nibbles = sb("nibbles", [P, 2, PIECE], I32)
        weight = sb("weight", [P, 2, 2, PIECE], F32)
        with ExitStack() as overlaid:
            def norm_sb(name, shape):
                return overlaid.enter_context(nc.sbuf_tensor(f"{tag}_{name}", shape, F32))

            centred0 = norm_sb("centred0", [P, KT, TB])
            squares = norm_sb("squares", [P, KT, TB])
            pairs = norm_sb("pairs", [P, 2, TB])
        w_high, w_low = [None, None], [None, None]
        for s in (1, 0):
            w_high[s] = sb(f"w_high{s}", [P, 2, NPIECE, PIECE], F32R)
            w_low[s] = sb(f"w_low{s}", [P, 2, NPIECE, PIECE], F32R)
        gelu = sb("gelu", [P, 6, TB], F32)
        inner = sb("inner", [P, 2, 2, 2, TB], F32R)
        centred1 = sb("centred1", [P, KT, TB], F32)
        std = sb("std", [P, TB], F32)
        averager = sb("averager", [P, P], F32)
        eps = sb("eps", [P, 1], F32)
        signal = sb("signal", [P, 1], F32)

        gate_bank, up_bank, down_bank = bank[0:2], bank[2:4], bank[4:8]
        square = [gelu[:, n, :] for n in range(2)]
        cubic = [gelu[:, 2 + n, :] for n in range(2)]
        product = [gelu[:, 4 + n, :] for n in range(2)]

        x_loaded = [sem(f"x_loaded{tb}") for tb in range(NTB)] if x_in is not None else None
        n = Norm(nc, ctx, tag, x, x_high, x_low, [centred0[:, :, :], centred1[:, :, :]],
                 squares[:, :, :], pairs[:, :, :], std, averager, eps,
                 down_bank[0:2], down_bank[2:4], x_loaded)

        words_loaded = [sem(f"words_loaded{p}") for p in range(NPIECE)]
        nibbles_ready = sem("nibbles_ready")
        weight_ready = sem("weight_ready")
        w_high_ready = sem("w_high_ready")
        w_low_ready = sem("w_low_ready")
        gate_up_ready = sem("gate_up_ready")
        square_ready = sem("gate_square_ready")
        cubic_ready = sem("cubic_ready")
        tanh_ready = sem("tanh_ready")
        gated_ready = sem("gated_ready")
        product_ready = sem("product_ready")
        inner_high_ready = sem("inner_high_ready")
        inner_low_ready = sem("inner_low_ready")
        down_ready = sem("down_ready")
        down_free = sem("down_free")
        stored = sem("stored")

        block = ctx.enter_context(nc.Block())

        @block.sync
        def _(sp):
            def load_words(g, piece):
                sp.dma_start(words[:, piece, :], packed[g, piece]).then_inc(words_loaded[piece], 16)
                sp.dma_start(word_scales[:, piece, :],
                             scales[g, piece].unsqueeze(1).broadcast_to([SCALE_ROWS, P // SCALE_ROWS, PIECE]))\
                  .then_inc(words_loaded[piece], 16)

            if x_in is not None:
                sp.dma_start(x[:, :, cols(0, TB)], x_in[:, :, cols(0, TB)]).then_inc(x_loaded[0], 16)
            for piece in range(NPIECE):
                load_words(0, piece)
            if x_in is not None:
                for tb in range(1, NTB):
                    sp.dma_start(x[:, :, cols(tb, TB)], x_in[:, :, cols(tb, TB)]).then_inc(x_loaded[tb], 16)
            with sp.Fori(1, NGROUP) as g:
                for piece in range(NPIECE):
                    sp.wait_ge(weight_ready, NPIECE * g + (piece + 1 - NPIECE))
                    load_words(g, piece)
            if x_out is not None:
                for tb in range(NTB):
                    st = NTB * (NGROUP - 1) + tb
                    sp.wait_ge(down_free, KT * (st + 1) + KT)
                    sp.dma_start(x_out[:, :, cols(tb, TB)], x[:, :, cols(tb, TB)]).then_inc(stored, 16)
                sp.wait_ge(stored, 16 * NTB)

        @block.tensor
        def _(pe):
            def gate_up_tile(gg, s, tb, m, first=False, norm=False):
                if not first:
                    pe.wait_ge(product_ready, 16 * gg + (8 * s + 2 * tb + m - 1))
                for out, piece in ((gate_bank[m], GATE), (up_bank[m], UP)):
                    if m == 0 and tb == 0:
                        pe.wait_ge(w_low_ready, 6 * gg + (3 * s + piece + 1))
                    for k in range(KT):
                        if norm and m == 0 and piece == GATE:
                            pe.wait_ge(n.low_ready, KT * tb + k + 1)
                        c, b = divmod(k, 2)
                        w = slice(c * GROUP + m * P, c * GROUP + (m + 1) * P)
                        last = split_products(
                            pe, out, w_high[s][:, b, piece, w], w_low[s][:, b, piece, w],
                            x_high[:, k, cols(tb, TB)], x_low[:, k, cols(tb, TB)],
                            k == 0, k == KT - 1)
                last.then_inc(gate_up_ready, 1)

            def gate_up(gg, s, tb, norm=False):
                for m in range(2):
                    gate_up_tile(gg, s, tb, m, norm=norm)

            def down(gg, s, tb):
                pe.wait_ge(inner_low_ready, 16 * gg + (8 * s + 2 * tb + 2))
                if tb == 0:
                    pe.wait_ge(w_low_ready, 6 * gg + (3 * s + 3))
                for k in range(KT):
                    pe.wait_ge(down_free, 32 * gg + (16 * s + 4 * tb + k + 1))
                    for m in range(2):
                        last = split_products(
                            pe, down_bank[k], w_high[s][:, m, DOWN, cols(k, P)],
                            w_low[s][:, m, DOWN, cols(k, P)],
                            inner[:, tb % 2, m, 0, :], inner[:, tb % 2, m, 1, :], m == 0, m == 1)
                    last.then_inc(down_ready, 1)

            def group(gg, s, last_group):
                for tb in range(NTB):
                    if tb < NTB - 1:
                        gate_up(gg, s, tb + 1)
                    elif not last_group:
                        gate_up(gg + s, 1 - s, 0)
                    down(gg, s, tb)

            n.mean(pe, 0)
            n.mean(pe, 1)
            n.variance(pe, 0)
            n.mean(pe, 2)
            n.variance(pe, 1)
            gate_up_tile(0, 0, 0, 0, first=True, norm=True)
            n.mean(pe, 3)
            gate_up_tile(0, 0, 0, 1, first=True)
            gate_up_tile(0, 0, 1, 0, norm=True)
            n.variance(pe, 2)
            gate_up_tile(0, 0, 1, 1)
            gate_up_tile(0, 0, 2, 0, norm=True)
            n.variance(pe, 3)
            gate_up_tile(0, 0, 2, 1)
            down(0, 0, 0)
            down(0, 0, 1)
            gate_up(0, 0, 3, norm=True)
            down(0, 0, 2)
            gate_up(0, 1, 0)
            down(0, 0, 3)
            group(0, 1, False)
            with pe.Fori(1, NGROUP // 2 - 1) as gg:
                group(gg, 0, False)
                group(gg, 1, False)
            group(NGROUP // 2 - 1, 0, False)
            group(NGROUP // 2 - 1, 1, True)

        @block.vector
        def _(dve):
            def unpack(gg, s, piece, first=False):
                q = 3 * s + piece
                dve.wait_ge(words_loaded[piece], 64 * gg + 32 * (s + 1))
                a, b = nibbles[:, 0, :], nibbles[:, 1, :]
                w = words[:, piece, :]
                dve.tensor_scalar(a, w, 0xF0, 12, ALU.bitwise_and, ALU.logical_shift_left)\
                   .then_inc(nibbles_ready, 1)
                dve.wait_ge(nibbles_ready, 24 * gg + (4 * q + 1))
                dve.scalar_tensor_tensor(out=b, in0=w, scalar=0xF, in1=a, op0=ALU.bitwise_and,
                                         op1=ALU.bitwise_or).then_inc(nibbles_ready, 1)
                dve.wait_ge(nibbles_ready, 24 * gg + (4 * q + 2))
                dve.scalar_tensor_tensor(out=a, in0=b, scalar=3, in1=b, op0=ALU.logical_shift_left,
                                         op1=ALU.bitwise_or).then_inc(nibbles_ready, 1)
                dve.wait_ge(nibbles_ready, 24 * gg + (4 * q + 3))
                dve.tensor_scalar(b, a, 0x00470047, 9, ALU.bitwise_and, ALU.logical_shift_left)\
                   .then_inc(nibbles_ready, 1)
                dve.wait_ge(nibbles_ready, 24 * gg + (4 * q + 4))
                if not first:
                    dve.wait_ge(w_low_ready, 6 * gg + (q - 1))
                halves = b.bitcast(F16).rearrange("p (w b) -> p b w", b=2)
                dve.tensor_tensor(weight[:, q % 2, :, :], halves,
                                  word_scales[:, piece, :].unsqueeze(1).broadcast_to([P, 2, PIECE]),
                                  ALU.mult).then_inc(weight_ready, 1)

            def gelu_tiles(gg, s, tb, tiles=range(2), first=False):
                for m in tiles:
                    i = 8 * s + 2 * tb + m
                    dve.wait_ge(square_ready, 16 * gg + (i + 1))
                    dve.scalar_tensor_tensor(out=cubic[m], in0=square[m], scalar=1.0 / GELU_A,
                                             in1=gate_bank[m], op0=ALU.add, op1=ALU.mult)\
                       .then_inc(cubic_ready, 1)
                    dve.wait_ge(tanh_ready, 16 * gg + (i + 1))
                    dve.scalar_tensor_tensor(out=cubic[m], in0=square[m], scalar=1.0,
                                             in1=gate_bank[m], op0=ALU.add, op1=ALU.mult)\
                       .then_inc(gated_ready, 1)
                    dve.wait_ge(gated_ready, 16 * gg + (i + 1))
                    if not first:
                        dve.wait_ge(inner_low_ready, 16 * gg + (i - 1))
                    dve.tensor_tensor(product[m], cubic[m], up_bank[m], ALU.mult)\
                       .then_inc(product_ready, 1)

            def add_down(gg, s, tb):
                for k in range(KT):
                    dve.wait_ge(down_ready, 32 * gg + (16 * s + 4 * tb + k + 1))
                    dve.scalar_tensor_tensor(out=x[:, k, cols(tb, TB)], in0=down_bank[k],
                                             scalar=FFN_BACK, in1=x[:, k, cols(tb, TB)],
                                             op0=ALU.mult, op1=ALU.add).then_inc(down_free, 1)

            def group(gg, s, last_group):
                for tb in range(NTB):
                    if tb < NTB - 1:
                        gelu_tiles(gg, s, tb + 1)
                    elif not last_group:
                        gelu_tiles(gg + s, 1 - s, 0)
                    if tb < NPIECE and not last_group:
                        unpack(gg + s, 1 - s, tb)
                    add_down(gg, s, tb)

            dve.memset(averager[:], 1.0 / D).then_inc(n.constants_ready, 1)
            dve.memset(eps[:], EPS).then_inc(n.constants_ready, 1)
            n.sum_pairs(dve, 0)
            n.centre(dve, 0)
            unpack(0, 0, GATE, first=True)
            n.sum_square_pairs(dve, 0)
            n.centre(dve, 1)
            n.scale(dve, 0)
            n.sum_square_pairs(dve, 1)
            unpack(0, 0, UP, first=True)
            n.scale(dve, 1)
            n.centre(dve, 2)
            gelu_tiles(0, 0, 0, [0], first=True)
            n.sum_square_pairs(dve, 2)
            gelu_tiles(0, 0, 0, [1], first=True)
            n.centre(dve, 3)
            unpack(0, 0, DOWN)
            n.scale(dve, 2)
            n.sum_square_pairs(dve, 3)
            gelu_tiles(0, 0, 1)
            dve.wait_ge(n.std_ready, NTB)
            dve.memset(signal[:], 0.0).then_inc(down_free, KT)
            n.scale(dve, 3)
            add_down(0, 0, 0)
            gelu_tiles(0, 0, 2)
            add_down(0, 0, 1)
            unpack(0, 1, GATE)
            unpack(0, 1, UP)
            gelu_tiles(0, 0, 3)
            add_down(0, 0, 2)
            unpack(0, 1, DOWN)
            gelu_tiles(0, 1, 0)
            add_down(0, 0, 3)
            group(0, 1, False)
            with dve.Fori(1, NGROUP // 2 - 1) as gg:
                group(gg, 0, False)
                group(gg, 1, False)
            group(NGROUP // 2 - 1, 0, False)
            group(NGROUP // 2 - 1, 1, True)

        @block.scalar
        def _(act):
            def weight_high(gg, s, piece):
                q = 3 * s + piece
                act.wait_ge(weight_ready, 6 * gg + (q + 1))
                act.activation(w_high[s][:, :, piece, :], weight[:, q % 2, :, :], ACT.Copy)\
                   .then_inc(w_high_ready, 1)

            def gelu_tiles(gg, s, tb, after_down=None):
                for m in range(2):
                    i = 8 * s + 2 * tb + m
                    act.wait_ge(gate_up_ready, 16 * gg + (i + 1))
                    act.activation(square[m], gate_bank[m], ACT.Square, scale=CODE).then_inc(square_ready, 1)
                    act.wait_ge(cubic_ready, 16 * gg + (i + 1))
                    act.activation(square[m], cubic[m], ACT.Tanh, scale=GELU_C * GELU_A * CODE)\
                       .then_inc(tanh_ready, 1)
                    act.wait_ge(product_ready, 16 * gg + (i + 1))
                    if after_down is not None:
                        act.wait_ge(down_ready, KT * (after_down + 1))
                    act.activation(inner[:, tb % 2, m, 0, :], product[m], ACT.Copy).then_inc(inner_high_ready, 1)

            def group(gg, s, last_group):
                for tb in range(NTB):
                    if tb < NTB - 1:
                        gelu_tiles(gg, s, tb + 1)
                    elif not last_group:
                        gelu_tiles(gg + s, 1 - s, 0)
                    if tb < NPIECE and not last_group:
                        weight_high(gg + s, 1 - s, tb)

            act.wait_ge(n.constants_ready, 2)
            n.square(act, 0)
            weight_high(0, 0, GATE)
            n.standard_deviation(act, 0)
            n.square(act, 1)
            n.high(act, 0)
            n.standard_deviation(act, 1)
            weight_high(0, 0, UP)
            n.high(act, 1)
            n.square(act, 2)
            gelu_tiles(0, 0, 0)
            n.standard_deviation(act, 2)
            weight_high(0, 0, DOWN)
            n.square(act, 3)
            n.high(act, 2)
            gelu_tiles(0, 0, 1)
            n.standard_deviation(act, 3)
            n.high(act, 3)
            gelu_tiles(0, 0, 2, after_down=0)
            act.wait_ge(n.low_ready, KT * NTB)
            weight_high(0, 1, GATE)
            weight_high(0, 1, UP)
            gelu_tiles(0, 0, 3)
            weight_high(0, 1, DOWN)
            gelu_tiles(0, 1, 0)
            group(0, 1, False)
            with act.Fori(1, NGROUP // 2 - 1) as gg:
                group(gg, 0, False)
                group(gg, 1, False)
            group(NGROUP // 2 - 1, 0, False)
            group(NGROUP // 2 - 1, 1, True)

        @block.gpsimd
        def _(pool):
            def weight_low(gg, s, piece):
                q = 3 * s + piece
                pool.wait_ge(w_high_ready, 6 * gg + (q + 1))
                pool.tensor_tensor(w_low[s][:, :, piece, :], weight[:, q % 2, :, :],
                                   f32(w_high[s][:, :, piece, :]), ALU.subtract).then_inc(w_low_ready, 1)

            def gelu_tiles(gg, s, tb):
                for m in range(2):
                    pool.wait_ge(inner_high_ready, 16 * gg + (8 * s + 2 * tb + m + 1))
                    pool.tensor_tensor(inner[:, tb % 2, m, 1, :], product[m],
                                       f32(inner[:, tb % 2, m, 0, :]), ALU.subtract)\
                        .then_inc(inner_low_ready, 1)

            def group(gg, s, last_group):
                for tb in range(NTB):
                    if tb < NTB - 1:
                        gelu_tiles(gg, s, tb + 1)
                    elif not last_group:
                        gelu_tiles(gg + s, 1 - s, 0)
                    if tb < NPIECE and not last_group:
                        weight_low(gg + s, 1 - s, tb)

            n.sum_pairs(pool, 1)
            weight_low(0, 0, GATE)
            n.sum_pairs(pool, 2)
            n.low(pool, 0)
            n.sum_pairs(pool, 3)
            weight_low(0, 0, UP)
            n.low(pool, 1)
            gelu_tiles(0, 0, 0)
            weight_low(0, 0, DOWN)
            n.low(pool, 2)
            gelu_tiles(0, 0, 1)
            n.low(pool, 3)
            gelu_tiles(0, 0, 2)
            weight_low(0, 1, GATE)
            weight_low(0, 1, UP)
            gelu_tiles(0, 0, 3)
            weight_low(0, 1, DOWN)
            gelu_tiles(0, 1, 0)
            group(0, 1, False)
            with pool.Fori(1, NGROUP // 2 - 1) as gg:
                group(gg, 0, False)
                group(gg, 1, False)
            group(NGROUP // 2 - 1, 0, False)
            group(NGROUP // 2 - 1, 1, True)


def project_in(nc, x, bank, w_v, b_v, w_qk, b_qk, qk_parts, v_parts):
    with ExitStack() as ctx:
        def sb(name, shape, dtype):
            return ctx.enter_context(nc.sbuf_tensor(name, shape, dtype))

        def sem(name):
            return ctx.enter_context(nc.semaphore(name))

        ITEM_BANKS = 4
        NTILES = 2 * KT
        x_high = sb("qkv_x_high", [P, KT, TOKENS], F32R)
        x_low = sb("qkv_x_low", [P, KT, TOKENS], F32R)
        centred = sb("qkv_centred", [P, 2, KT, TB], F32)
        squares = sb("qkv_squares", [P, KT, TB], F32)
        pairs = sb("qkv_pairs", [P, 2, TB], F32)
        std = sb("qkv_std", [P, TB], F32)
        averager = sb("qkv_averager", [P, P], F32)
        eps = sb("qkv_eps", [P, 1], F32)
        wv = sb("wv", [P, KT, D], F32)
        wv_high = sb("wv_high", [P, KT, D], F32R)
        wv_low = sb("wv_low", [P, KT, D], F32R)
        wt = sb("wt", [P, NTILES, KT, P], F32)
        wt_high = [sb(f"wt_high{s}", [P, KT, P], F32R) for s in range(2)]
        wt_low = [sb(f"wt_low{s}", [P, KT, P], F32R) for s in range(2)]
        v_bias = sb("v_bias", [P, D], F32)
        qk_bias = sb("qk_bias", [P, NTILES], F32)
        full = sb("full", [P, 2, TB], F32)
        parts = sb("parts", [P, ITEM_BANKS, 2, TB], F32R)

        n = Norm(nc, ctx, "qkv", x, x_high, x_low, [centred[:, 0, :, :], centred[:, 1, :, :]],
                 squares, pairs[:], std, averager, eps, bank[4:6], bank[6:8], None)
        wv_loaded = sem("wv_loaded")
        bias_loaded = sem("bias_loaded")
        wt_loaded = sem("wt_loaded")
        wv_high_ready = sem("wv_high_ready")
        wv_low_ready = sem("wv_low_ready")
        wt_high_ready = sem("wt_high_ready")
        wt_low_ready = sem("wt_low_ready")
        item_ready = sem("item_ready")
        full_ready = sem("full_ready")
        part_high_ready = sem("part_high_ready")
        part_low_ready = sem("part_low_ready")
        stored = [sem(f"parts_stored{s}") for s in range(ITEM_BANKS)]

        block = ctx.enter_context(nc.Block())

        @block.sync
        def _(sp):
            sp.dma_start(wv[:], w_v).then_inc(wv_loaded, 16)
            sp.dma_start(v_bias[:], b_v.partition_broadcast(P)).then_inc(bias_loaded, 16)
            sp.dma_start(qk_bias[:], b_qk).then_inc(bias_loaded, 16)
            sp.dma_start(wt[:], w_qk.rearrange("e p k o -> p e k o")).then_inc(wt_loaded, 16)
            for tt in range(TT):
                sp.wait_ge(part_low_ready, tt + 1)
                sp.dma_start(v_parts[:, :, tt, :].rearrange("h p c -> p h c"),
                             f32(parts[:, tt % ITEM_BANKS]).rearrange("p l (h c) -> p (l h) c", h=HEADS // 2))\
                  .then_inc(stored[tt % ITEM_BANKS], 16)

            def store_tile(ep, s, tb):
                sp.wait_ge(part_low_ready, 8 * ep + (TT + 4 * s + tb + 1))
                sp.dma_start(
                    qk_parts[:, bass.ds(2 * P * ep + s * P, P), cols(tb, TB)].rearrange("l e t -> e l t"),
                    f32(parts[:, tb])).then_inc(stored[tb], 16)

            with sp.Fori(0, NTILES // 2) as ep:
                for s in range(2):
                    for tb in range(NTB):
                        store_tile(ep, s, tb)
            for s in range(ITEM_BANKS):
                sp.wait_ge(stored[s], 16 * (TT + NTILES * NTB) // ITEM_BANKS)

        @block.tensor
        def _(pe):
            def value_items(tts):
                for tt in tts:
                    tb, token_tile = divmod(tt, NTB)
                    if tt >= ITEM_BANKS:
                        pe.wait_ge(full_ready, tt - ITEM_BANKS + 1)
                    for k in range(KT):
                        if token_tile == 0:
                            pe.wait_ge(n.low_ready, KT * tb + k + 1)
                        pe.matmul(bank[tt % ITEM_BANKS], x_high[:, k, cols(tt, P)], wv_high[:, k, :],
                                  start=(k == 0), stop=False)
                        pe.matmul(bank[tt % ITEM_BANKS], x_low[:, k, cols(tt, P)], wv_high[:, k, :],
                                  start=False, stop=False)
                        last = pe.matmul(bank[tt % ITEM_BANKS], x_high[:, k, cols(tt, P)], wv_low[:, k, :],
                                         start=False, stop=(k == KT - 1))
                    last.then_inc(item_ready, 1)

            n.mean(pe, 0)
            n.mean(pe, 1)
            n.variance(pe, 0)
            n.mean(pe, 2)
            n.variance(pe, 1)
            pe.wait_ge(wv_low_ready, 1)
            value_items(range(0, 2))
            n.mean(pe, 3)
            value_items(range(2, 6))
            n.variance(pe, 2)
            value_items(range(6, 10))
            n.variance(pe, 3)
            value_items(range(10, TT))
            with pe.Fori(0, NTILES // 2) as ep:
                for s in range(2):
                    pe.wait_ge(wt_low_ready, 2 * ep + (s + 1))
                    for tb in range(NTB):
                        pe.wait_ge(full_ready, 8 * ep + (TT + 4 * s + tb - ITEM_BANKS + 1))
                        for k in range(KT):
                            last = split_products(pe, bank[tb], wt_high[s][:, k, :], wt_low[s][:, k, :],
                                                  x_high[:, k, cols(tb, TB)], x_low[:, k, cols(tb, TB)],
                                                  k == 0, k == KT - 1)
                        last.then_inc(item_ready, 1)

        @block.vector
        def _(dve):
            dve.memset(averager[:], 1.0 / D).then_inc(n.constants_ready, 1)
            dve.memset(eps[:], EPS).then_inc(n.constants_ready, 1)
            def value_items(tts):
                for tt in tts:
                    dve.wait_ge(item_ready, tt + 1)
                    if tt >= 2:
                        dve.wait_ge(part_low_ready, tt - 1)
                    dve.tensor_tensor(full[:, tt % 2, :], bank[tt % ITEM_BANKS], v_bias[:], ALU.add)\
                       .then_inc(full_ready, 1)

            n.sum_pairs(dve, 0)
            n.centre(dve, 0)
            n.sum_square_pairs(dve, 0)
            n.centre(dve, 1)
            n.scale(dve, 0)
            n.sum_square_pairs(dve, 1)
            n.scale(dve, 1)
            n.centre(dve, 2)
            dve.wait_ge(bias_loaded, 32)
            value_items(range(0, 3))
            n.sum_square_pairs(dve, 2)
            value_items(range(3, 4))
            n.centre(dve, 3)
            n.scale(dve, 2)
            n.sum_square_pairs(dve, 3)
            value_items(range(4, 8))
            n.scale(dve, 3)
            value_items(range(8, TT))
            with dve.Fori(0, NTILES // 2) as ep:
                for s in range(2):
                    for tb in range(NTB):
                        i = TT + 4 * s + tb
                        dve.wait_ge(item_ready, 8 * ep + (i + 1))
                        dve.wait_ge(part_low_ready, 8 * ep + (i - 1))
                        dve.tensor_scalar(full[:, tb % 2, :], bank[tb],
                                          qk_bias[:, bass.ds(2 * ep + s, 1)], None, ALU.add)\
                           .then_inc(full_ready, 1)

        @block.scalar
        def _(act):
            def tile_high(ep, s):
                act.wait_ge(item_ready, 8 * ep + (TT + 4 * (s - 1)))
                act.activation(wt_high[s][:], wt[:, bass.ds(2 * ep + s, 1), :, :].rearrange("p o k c -> p (o k) c"),
                               ACT.Copy).then_inc(wt_high_ready, 1)

            def pair(ep, last_pair):
                for s in range(2):
                    if not (last_pair and s == 1):
                        tile_high(ep + s, 1 - s)
                    for tb in range(NTB):
                        i = TT + 4 * s + tb
                        act.wait_ge(full_ready, 8 * ep + (i + 1))
                        act.wait_ge(stored[tb], 32 * ep + 16 * (i // ITEM_BANKS))
                        act.activation(parts[:, tb, 0, :], full[:, tb % 2, :], ACT.Copy)\
                           .then_inc(part_high_ready, 1)

            def value_items(tts):
                for tt in tts:
                    act.wait_ge(full_ready, tt + 1)
                    if tt >= ITEM_BANKS:
                        act.wait_ge(stored[tt % ITEM_BANKS], 16 * (tt // ITEM_BANKS))
                    act.activation(parts[:, tt % ITEM_BANKS].rearrange("p a (h l d) -> p (a h) l d", l=2, d=HD)[:, :, 0, :],
                                   full[:, tt % 2, :].rearrange("p (h d) -> p h d", d=HD), ACT.Copy)\
                       .then_inc(part_high_ready, 1)

            act.wait_ge(n.constants_ready, 2)
            n.square(act, 0)
            act.wait_ge(wv_loaded, 16)
            act.activation(wv_high[:], wv[:], ACT.Copy).then_inc(wv_high_ready, 1)
            n.standard_deviation(act, 0)
            n.square(act, 1)
            n.high(act, 0)
            n.standard_deviation(act, 1)
            n.high(act, 1)
            n.square(act, 2)
            value_items(range(0, 4))
            n.standard_deviation(act, 2)
            n.square(act, 3)
            n.high(act, 2)
            act.wait_ge(wt_loaded, 16)
            act.activation(wt_high[0][:], wt[:, 0, :, :], ACT.Copy).then_inc(wt_high_ready, 1)
            value_items(range(4, 8))
            n.standard_deviation(act, 3)
            n.high(act, 3)
            value_items(range(8, TT))
            with act.Fori(0, NTILES // 2 - 1) as ep:
                pair(ep, False)
            pair(NTILES // 2 - 1, True)

        @block.gpsimd
        def _(pool):
            def tile_low(ep, s):
                pool.wait_ge(wt_high_ready, 2 * ep + (s + 1))
                pool.tensor_tensor(wt_low[s][:],
                                   wt[:, bass.ds(2 * ep + s, 1), :, :].rearrange("p o k c -> p (o k) c"),
                                   f32(wt_high[s][:]), ALU.subtract)\
                    .then_inc(wt_low_ready, 1)

            def pair(ep, last_pair):
                for s in range(2):
                    if not (last_pair and s == 1):
                        tile_low(ep + s, 1 - s)
                    for tb in range(NTB):
                        pool.wait_ge(part_high_ready, 8 * ep + (TT + 4 * s + tb + 1))
                        pool.tensor_tensor(parts[:, tb, 1, :], full[:, tb % 2, :],
                                           f32(parts[:, tb, 0, :]), ALU.subtract).then_inc(part_low_ready, 1)

            def value_items(tts):
                for tt in tts:
                    by_head = parts[:, tt % ITEM_BANKS].rearrange("p a (h l d) -> p (a h) l d", l=2, d=HD)
                    pool.wait_ge(part_high_ready, tt + 1)
                    pool.tensor_tensor(by_head[:, :, 1, :], full[:, tt % 2, :].rearrange("p (h d) -> p h d", d=HD),
                                       f32(by_head[:, :, 0, :]), ALU.subtract).then_inc(part_low_ready, 1)

            n.sum_pairs(pool, 1)
            n.sum_pairs(pool, 2)
            pool.wait_ge(wv_high_ready, 1)
            pool.tensor_tensor(wv_low[:], wv[:], f32(wv_high[:]), ALU.subtract).then_inc(wv_low_ready, 1)
            n.low(pool, 0)
            n.sum_pairs(pool, 3)
            n.low(pool, 1)
            value_items(range(0, 4))
            n.low(pool, 2)
            value_items(range(4, 8))
            n.low(pool, 3)
            tile_low(0, 0)
            value_items(range(8, TT))
            with pool.Fori(0, NTILES // 2 - 1) as ep:
                pair(ep, False)
            pair(NTILES // 2 - 1, True)


TILES = [(b, kt) for b in range(NTB) for kt in range(4 * b + 4)]
CHUNKS = [(b, qt, c) for b in range(NTB) for qt in range(4 * b, 4 * b + 4) for c in range(b + 1)]
SLOTS = len(TILES)
SCORE_BANKS = 3
AHEAD = 4
RING = AHEAD + 1
LOW_AHEAD = 2
ROUNDED_BY_DVE = 2
LOW_BY_DVE = 99


def chunks_of_slot(t):
    return [m for m in range(SLOTS) if m * (SLOTS - 3) // SLOTS == t]


MAXED_AT = {[t for t in range(SLOTS) if b * (b + 1) * 2 + 4 * (b + 1) - 1 in chunks_of_slot(t)][0]: b
            for b in range(NTB)}
ROWS_AT = {t + 3: b for t, b in MAXED_AT.items()}
ITEMS = [item for t in range(SLOTS)
         for item in [("chunk", m) for m in chunks_of_slot(t)] + ([("rows", ROWS_AT[t])] if t in ROWS_AT else [])]
MAX_BANKS = 3


def max_bank_of(s, item):
    return (len(ITEMS) * s + ITEMS.index(item)) % MAX_BANKS


def high_by_dve(t):
    return t % 4 == ROUNDED_BY_DVE


def low_by_gpsimd(t):
    return not high_by_dve(t) and t % 8 != LOW_BY_DVE


def low_rank(t):
    mine = [u for u in range(SLOTS) if low_by_gpsimd(u) == low_by_gpsimd(t)]
    return mine.index(t) + 1, len(mine)


class OutProjection:

    def __init__(self, nc, ctx):
        def sb(name, shape, dtype):
            return ctx.enter_context(nc.sbuf_tensor(name, shape, dtype))

        def sem(name):
            return ctx.enter_context(nc.semaphore(name))

        self.wo = sb("wo", [P, KT, D], F32)
        self.wo_high = sb("wo_high", [P, KT, D], F32R)
        self.wo_low = sb("wo_low", [P, KT, D], F32R)
        self.out_bias = sb("out_bias", [P, KT], F32)
        self.inverse_all = sb("inverse_all", [P, HEADS * TOKENS // P], F32)
        self.from_high = sb("from_high", [P, 2, KT, TB], F32)
        self.from_low = sb("from_low", [P, 2, KT, TB], F32)
        self.inverse = sb("inverse", [P, 2, KT, TB], F32)
        self.wo_loaded = sem("wo_loaded")
        self.bias_loaded = sem("out_bias_loaded")
        self.wo_high_ready = sem("wo_high_ready")
        self.wo_low_ready = sem("wo_low_ready")
        self.sums_loaded = sem("sums_loaded")
        self.inverse_ready = sem("inverse_ready")
        self.inverse_stored = sem("inverse_stored")
        self.early_loaded = [sem(f"early_loaded{i}") for i in range(2)]

    def inverse_tile(self, heads):
        per_row = len(heads) * TOKENS // P
        first = heads[0] * TOKENS // P
        return self.inverse_all[:, first:first + per_row], per_row


HPT = P // HD
EARLY_HEADS = range(0, HEADS - HPT)
LAST_HEADS = range(HEADS - HPT, HEADS)
EARLY = KT - 1


def load_from_heads(queue, o, o_parts, tb, tiles, loaded):
    for part, dst in ((0, o.from_high), (1, o.from_low)):
        queue.dma_start(dst[:, tb % 2, tiles, :],
                        o_parts[part].rearrange("(k p) t -> p k t", p=P)[:, tiles, cols(tb, TB)])\
             .then_inc(loaded, 16)


def load_inverse(queue, o, inverses, tb, k, loaded):
    queue.dma_start(o.inverse[:, tb % 2, k, :],
                    inverses[cols(k, HPT), cols(tb, TB)].unsqueeze(1).broadcast_to([HPT, HD, TB]))\
         .then_inc(loaded, 16)


def move_sums(queue, o, dram, heads, to_chip, moved):
    tile, per_row = o.inverse_tile(heads)
    rows = dram[heads[0]:heads[-1] + 1].rearrange("h t -> (h t)").rearrange("(a t) -> a t", t=per_row)
    queue.dma_start(tile if to_chip else rows, rows if to_chip else tile).then_inc(moved, 16)


def attention(nc, bank, qk_parts, v_parts, o_parts, sums, inverses, w_out, b_out, o):
    with ExitStack() as ctx:
        def sb(name, shape, dtype):
            return ctx.enter_context(nc.sbuf_tensor(name, shape, dtype))

        def sem(name):
            return ctx.enter_context(nc.semaphore(name))

        STACK = 3 * HD
        ROWS = STACK + 2
        queries = [sb(f"queries{i}", [ROWS, TOKENS], F32R) for i in range(3)]
        keys = [sb(f"keys{i}", [ROWS, TOKENS], F32R) for i in range(3)]
        values = [sb(f"values{i}", [P, TT, VCOLS], F32R) for i in range(3)]
        probs = sb("probs", [P, RING, TB], F32)
        probs_high = sb("probs_high", [P, RING, TB], F32R)
        probs_low = sb("probs_low", [P, RING, TB], F32R)
        chunk_max = sb("chunk_max", [P, 2, 4, NTB], F32)
        minus_max = sb("minus_max", [P, 2, 4], F32)
        max_parts = sb("max_parts", [P, 2, 4, 2], F32R)
        heads_out = sb("heads_out", [VCOLS, 2, TB], F32)
        ident = sb("ident", [P, P], F32)
        ident_r = sb("ident_r", [P, P], F32R)
        ident_b = sb("ident_b", [P, P], BF16)
        key_mask = sb("key_mask", [P, P], F32)
        query_mask = sb("query_mask", [P, P], F32)
        key_mask_b = sb("key_mask_b", [P, P], BF16)
        query_mask_b = sb("query_mask_b", [P, P], BF16)

        start = sb("start", [P, 3], F32)

        score_bank, max_bank, out_bank = bank[0:SCORE_BANKS], bank[3:6], bank[6:8]

        filled = sem("filled")
        constants_ready = sem("attn_constants_ready")
        loaded = [sem(f"head_loaded{i}") for i in range(3)]
        max_scores_ready = sem("max_scores_ready")
        max_taken = sem("max_taken")
        max_steps = sem("max_steps")
        max_parts_ready = sem("max_parts_ready")
        rows_in_bank = sem("rows_in_bank")
        rows_ready = sem("rows_ready")
        scores_ready = sem("scores_ready")
        probs_ready = sem("probs_ready")
        high_ready = sem("high_ready")
        low_by_dve = sem("low_by_dve")
        low_by_pool = sem("low_by_pool")
        out_ready = sem("out_ready")
        out_free = sem("out_free")
        out_stored = [sem(f"out_stored{i}") for i in range(2)]

        LOAD = 7 * 16

        block = ctx.enter_context(nc.Block())

        @block.sync
        def _(sp):
            def load(h, i):
                for part, row in ((0, 0), (1, HD), (0, 2 * HD)):
                    sp.dma_start(f32(queries[i][row:row + HD, :]),
                                 qk_parts[part, bass.ds(h * HD, HD), :]).then_inc(loaded[i], 16)
                for part, row in ((0, 0), (0, HD), (1, 2 * HD)):
                    sp.dma_start(f32(keys[i][row:row + HD, :]),
                                 qk_parts[part, bass.ds(h * HD + D, HD), :]).then_inc(loaded[i], 16)
                sp.dma_start(f32(values[i][:, :, 0:2 * HD]),
                             v_parts[bass.ds(h, 1)].rearrange("o p t c -> (o p) t c")).then_inc(loaded[i], 16)

            def store(h0, s, blocks=range(NTB)):
                for b in blocks:
                    sp.wait_ge(out_free, 4 * h0 + (4 * s + b + 1 + 2))
                    sp.dma_start(o_parts[:, bass.ds(h0 * HD + s * HD, HD), cols(b, TB)],
                                 heads_out[0:2 * HD, b % 2, :]).then_inc(out_stored[b % 2], 16)
                    sp.dma_start(sums[bass.ds(h0 + s, 1), cols(b, TB)],
                                 heads_out[2 * HD:VCOLS, b % 2, :]).then_inc(out_stored[b % 2], 16)

            load(0, 0)
            sp.dma_start(o.wo[:], w_out).then_inc(o.wo_loaded, 16)
            sp.dma_start(o.out_bias[:], b_out).then_inc(o.bias_loaded, 16)
            load(1, 1)
            load(2, 2)
            with sp.Fori(0, HEADS // 3 - 1) as hp:
                for s in range(3):
                    store(3 * hp, s)
                    load(3 * hp + (s + 3), s)
            store(HEADS - 4, 0)
            load(HEADS - 1, 0)
            for i in range(2):
                sp.wait_ge(out_stored[i], 32 * (len(EARLY_HEADS) * NTB // 2 + 1))
            move_sums(sp, o, sums, EARLY_HEADS, True, o.sums_loaded)
            for tb in range(2):
                load_from_heads(sp, o, o_parts, tb, slice(0, EARLY), o.early_loaded[tb])
            store(HEADS - 4, 1)
            store(HEADS - 4, 2)
            sp.wait_ge(o.inverse_ready, 1)
            move_sums(sp, o, inverses, EARLY_HEADS, False, o.inverse_stored)
            store(HEADS - 4, 3, [0, 1])
            sp.wait_ge(o.inverse_stored, 16)
            for tb in range(2):
                for k in range(EARLY):
                    load_inverse(sp, o, inverses, tb, k, o.early_loaded[tb])
            store(HEADS - 4, 3, [2, 3])
            for i in range(2):
                sp.wait_ge(out_stored[i], 32 * (HEADS * NTB // 2 + 1))

        @block.tensor
        def _(pe):
            def wait_for_max_bank(hp, s, item):
                before = len(ITEMS) * s + ITEMS.index(item) - MAX_BANKS
                if before < 0:
                    return
                (kind, j), s = ITEMS[before % len(ITEMS)], before // len(ITEMS)
                if kind == "chunk":
                    pe.wait_ge(max_taken, 120 * hp + (SLOTS * s + j + 1))
                else:
                    pe.wait_ge(rows_ready, 12 * hp + (NTB * s + j + 1))

            def max_chunk(hp, s, m):
                b, qt, c = CHUNKS[m]
                i = s % 3
                if m == 0:
                    pe.wait_ge(loaded[i], LOAD * hp + LOAD * (s // 3 + 1))
                wait_for_max_bank(hp, s, ("chunk", m))
                width = TB if c < b else (qt % 4 + 1) * P
                out = max_bank[max_bank_of(s, ("chunk", m))]
                last = pe.matmul(out[:, 0:width], queries[i][0:STACK, cols(qt, P)],
                                 keys[i][0:STACK, c * TB:c * TB + width], start=True, stop=(c < b),
                                 skip_group_check=True)
                if c == b:
                    last = pe.matmul(out[:, width - P:width], ident_b[:], query_mask_b[:],
                                     start=False, stop=True, skip_group_check=True)
                last.then_inc(max_scores_ready, 1)

            def rows(hp, s, b):
                n = 4 * s + b
                pe.wait_ge(max_parts_ready, 12 * hp + (n + 1))
                wait_for_max_bank(hp, s, ("rows", b))
                for j in range(4):
                    last = pe.matmul(max_bank[max_bank_of(s, ("rows", b))][0:2, cols(j, P)], max_parts[:, b % 2, j, :], ident_r[:],
                                     start=True, stop=True, skip_group_check=True)
                last.then_inc(rows_in_bank, 1)

            def scores(hp, s, t, first=False):
                b, kt = TILES[t]
                i = s % 3
                if kt == 0:
                    pe.wait_ge(rows_ready, 12 * hp + (4 * s + b + 1))
                if not (first and t < SCORE_BANKS):
                    pe.wait_ge(probs_ready, 120 * hp + (SLOTS * s + t - SCORE_BANKS + 1))
                q0 = max(b * TB, kt * P)
                width = (b + 1) * TB - q0
                out = score_bank[(SLOTS * s + t) % SCORE_BANKS]
                last = pe.matmul(out[:, 0:width], keys[i][0:ROWS, cols(kt, P)],
                                 queries[i][0:ROWS, q0:q0 + width], start=True, stop=(kt < 4 * b),
                                 skip_group_check=True)
                if kt >= 4 * b:
                    last = pe.matmul(out[:, 0:P], ident_b[:], key_mask_b[:],
                                     start=False, stop=True, skip_group_check=True)
                last.then_inc(scores_ready, 1)

            def with_values(hp, s, t):
                b, kt = TILES[t]
                i = s % 3
                if kt == 0:
                    pe.wait_ge(out_free, 12 * hp + (4 * s + b + 1))
                rank, per_head = low_rank(t)
                pe.wait_ge(low_by_pool if low_by_gpsimd(t) else low_by_dve,
                           3 * per_head * hp + (per_head * s + rank))
                off = max(0, kt * P - b * TB)
                out = out_bank[b % 2][0:VCOLS, off:TB]
                pe.matmul(out, values[i][:, kt, :], probs_high[:, t % RING, 0:TB - off],
                          start=(kt == 0), stop=False, skip_group_check=True)
                last = pe.matmul(out, values[i][:, kt, :], probs_low[:, t % RING, 0:TB - off],
                                 start=False, stop=(kt == 4 * b + 3), skip_group_check=True)
                if kt == 4 * b + 3:
                    last.then_inc(out_ready, 1)

            def head(hp, s, has_next):
                for t in range(SLOTS):
                    if t + AHEAD < SLOTS:
                        scores(hp, s, t + AHEAD)
                    elif has_next:
                        scores(hp, s + 1, t + AHEAD - SLOTS)
                    if has_next:
                        for m in chunks_of_slot(t):
                            max_chunk(hp, s + 1, m)
                        if t in ROWS_AT:
                            rows(hp, s + 1, ROWS_AT[t])
                    with_values(hp, s, t)

            pe.wait_ge(constants_ready, 10)
            for kind, j in ITEMS:
                if kind == "chunk":
                    max_chunk(0, 0, j)
                else:
                    rows(0, 0, j)
            for t in range(AHEAD):
                scores(0, 0, t, first=True)
            with pe.Fori(0, HEADS // 3) as hp:
                for s in range(3):
                    head(hp, s, True)
            head(HEADS // 3, 0, False)

        @block.vector
        def _(dve):
            def take_max(hp, s, m):
                b, qt, c = CHUNKS[m]
                dve.wait_ge(max_scores_ready, 120 * hp + (SLOTS * s + m + 1))
                width = TB if c < b else (qt % 4 + 1) * P
                dve.tensor_reduce(chunk_max[:, b % 2, qt % 4, c:c + 1], max_bank[max_bank_of(s, ("chunk", m))][:, 0:width],
                                  AX.X, ALU.max).then_inc(max_taken, 1)

            def split_max(hp, s, b, first=False):
                n = 4 * s + b
                m = [chunk[0] for chunk in CHUNKS].index(b) + 4 * (b + 1)
                dve.wait_ge(max_taken, 120 * hp + (SLOTS * s + m))
                dve.tensor_reduce(minus_max[:, b % 2, :], chunk_max[:, b % 2, :, 0:b + 1], AX.X, ALU.max,
                                  negate=True).then_inc(max_steps, 1)
                dve.wait_ge(max_steps, 24 * hp + (2 * n + 1))
                if not (first and b < 2):
                    dve.wait_ge(rows_in_bank, 12 * hp + (n - 1))
                dve.tensor_copy(max_parts[:, b % 2, :, 0], minus_max[:, b % 2, :]).then_inc(max_steps, 1)
                dve.wait_ge(max_steps, 24 * hp + (2 * n + 2))
                dve.tensor_tensor(max_parts[:, b % 2, :, 1], minus_max[:, b % 2, :],
                                  f32(max_parts[:, b % 2, :, 0]), ALU.subtract).then_inc(max_parts_ready, 1)

            def low(hp, s, t):
                if low_by_gpsimd(t):
                    return
                b, kt = TILES[t]
                width = TB - max(0, kt * P - b * TB)
                dve.wait_ge(probs_ready, 120 * hp + (SLOTS * s + t + 1))
                if high_by_dve(t):
                    per_head = SLOTS // 4
                    dve.tensor_copy(probs_high[:, t % RING, 0:width], probs[:, t % RING, 0:width])\
                       .then_inc(high_ready, 1)
                    dve.wait_ge(high_ready, 3 * per_head * hp + (per_head * s + t // 4 + 1))
                dve.tensor_tensor(probs_low[:, t % RING, 0:width], probs[:, t % RING, 0:width],
                                  f32(probs_high[:, t % RING, 0:width]), ALU.subtract).then_inc(low_by_dve, 1)

            def head(hp, s, has_next):
                for t in range(SLOTS):
                    if has_next:
                        for m in chunks_of_slot(t):
                            take_max(hp, s + 1, m)
                        if t in MAXED_AT:
                            split_max(hp, s + 1, MAXED_AT[t])
                    if t + LOW_AHEAD < SLOTS:
                        low(hp, s, t + LOW_AHEAD)
                    elif has_next:
                        low(hp, s + 1, t + LOW_AHEAD - SLOTS)

            for i in range(3):
                dve.memset(f32(keys[i][STACK:ROWS, :]), 1.0).then_inc(constants_ready, 1)
                dve.memset(f32(values[i][:, :, 2 * HD:VCOLS]), 1.0).then_inc(constants_ready, 1)
            dve.wait_ge(filled, 6)
            dve.tensor_copy(ident_r[:], ident[:]).then_inc(constants_ready, 1)
            dve.tensor_copy(ident_b[:], ident[:]).then_inc(constants_ready, 1)
            dve.tensor_copy(key_mask_b[:], key_mask[:]).then_inc(constants_ready, 1)
            dve.tensor_copy(query_mask_b[:], query_mask[:]).then_inc(constants_ready, 1)
            for b in range(NTB):
                for m, chunk in enumerate(CHUNKS):
                    if chunk[0] == b:
                        take_max(0, 0, m)
                split_max(0, 0, b, first=True)
            for t in range(LOW_AHEAD):
                low(0, 0, t)
            with dve.Fori(0, HEADS // 3) as hp:
                for s in range(3):
                    head(hp, s, True)
            dve.wait_ge(o.sums_loaded, 16)
            early, _ = o.inverse_tile(EARLY_HEADS)
            dve.reciprocal(early, early).then_inc(o.inverse_ready, 1)
            head(HEADS // 3, 0, False)

        @block.scalar
        def _(act):
            def rows(hp, s, b):
                act.wait_ge(rows_in_bank, 12 * hp + (4 * s + b + 1))
                act.activation(queries[s % 3][STACK:ROWS, cols(b, TB)], max_bank[max_bank_of(s, ("rows", b))][0:2, :],
                               ACT.Copy)\
                   .then_inc(rows_ready, 1)

            def exps(hp, s, t):
                b, kt = TILES[t]
                width = TB - max(0, kt * P - b * TB)
                act.wait_ge(scores_ready, 120 * hp + (SLOTS * s + t + 1))
                source = score_bank[(SLOTS * s + t) % SCORE_BANKS][:, 0:width]
                last = act.activation(probs[:, t % RING, 0:width], source, ACT.Exp, scale=SM_SCALE)
                if not high_by_dve(t):
                    last = act.activation(probs_high[:, t % RING, 0:width], source, ACT.Exp, scale=SM_SCALE)
                last.then_inc(probs_ready, 1)

            def take_out(hp, s, b):
                act.wait_ge(out_ready, 12 * hp + (4 * s + b + 1))
                act.wait_ge(out_stored[b % 2], 192 * hp + 32 * ((4 * s + b) // 2 + 1))
                act.activation(heads_out[:, b % 2, :], out_bank[b % 2][0:VCOLS, :], ACT.Copy)\
                   .then_inc(out_free, 1)

            def head(hp, s, has_next):
                for t in range(SLOTS):
                    if t + AHEAD < SLOTS:
                        exps(hp, s, t + AHEAD)
                    elif has_next:
                        exps(hp, s + 1, t + AHEAD - SLOTS)
                    if has_next and t in ROWS_AT:
                        rows(hp, s + 1, ROWS_AT[t])
                    b, kt = TILES[t - 1]
                    if t > 0 and kt == 4 * b + 3:
                        take_out(hp, s, b)
                take_out(hp, s, NTB - 1)

            act.wait_ge(o.wo_loaded, 16)
            act.activation(o.wo_high[:], o.wo[:], ACT.Copy).then_inc(o.wo_high_ready, 1)
            for b in range(NTB):
                rows(0, 0, b)
            for t in range(AHEAD):
                exps(0, 0, t)
            with act.Fori(0, HEADS // 3) as hp:
                for s in range(3):
                    head(hp, s, True)
            head(HEADS // 3, 0, False)

        @block.gpsimd
        def _(pool):
            def low(hp, s, t):
                if not low_by_gpsimd(t):
                    return
                b, kt = TILES[t]
                width = TB - max(0, kt * P - b * TB)
                pool.wait_ge(probs_ready, 120 * hp + (SLOTS * s + t + 1))
                pool.tensor_tensor(probs_low[:, t % RING, 0:width], probs[:, t % RING, 0:width],
                                   f32(probs_high[:, t % RING, 0:width]), ALU.subtract).then_inc(low_by_pool, 1)

            def head(hp, s):
                for t in range(SLOTS):
                    low(hp, s, t)

            pool.memset(ident[:], 0.0).then_inc(filled, 1)
            pool.memset(key_mask[:], 0.0).then_inc(filled, 1)
            pool.memset(query_mask[:], 0.0).then_inc(filled, 1)
            pool.wait_ge(filled, 3)
            pool.affine_select(out=ident[:], in_=ident[:], compare_op=ALU.not_equal, fill=1.0, base=0,
                               pattern=[[-1, P]], channel_multiplier=1).then_inc(filled, 1)
            pool.affine_select(out=key_mask[:], in_=key_mask[:], compare_op=ALU.is_ge, fill=MASKED, base=0,
                               pattern=[[1, P]], channel_multiplier=-1).then_inc(filled, 1)
            pool.affine_select(out=query_mask[:], in_=query_mask[:], compare_op=ALU.is_ge, fill=MASKED,
                               base=0, pattern=[[-1, P]], channel_multiplier=1).then_inc(filled, 1)
            pool.memset(start[:, 0:1], 0.0).then_inc(out_free, 2)
            pool.memset(start[:, 1:2], 0.0).then_inc(out_stored[0], 32)
            pool.memset(start[:, 2:3], 0.0).then_inc(out_stored[1], 32)
            pool.wait_ge(o.wo_high_ready, 1)
            pool.tensor_tensor(o.wo_low[:], o.wo[:], f32(o.wo_high[:]), ALU.subtract).then_inc(o.wo_low_ready, 1)
            with pool.Fori(0, HEADS // 3) as hp:
                for s in range(3):
                    head(hp, s)
            head(HEADS // 3, 0)


STEPS = [(tb, k) for tb in range(2) for k in range(EARLY)] + [(tb, k) for tb in range(2) for k in range(EARLY, KT)]
STEPS += [(tb, k) for tb in range(2, NTB) for k in range(KT)]


def steps_to(tb, k):
    return STEPS.index((tb, k)) + 1


def project_out(nc, x, bank, o_parts, sums, inverses, o):
    with ExitStack() as ctx:
        def sb(name, shape, dtype):
            return ctx.enter_context(nc.sbuf_tensor(name, shape, dtype))

        def sem(name):
            return ctx.enter_context(nc.semaphore(name))

        from_high, from_low, inverse = o.from_high, o.from_low, o.inverse
        normed_high = sb("normed_high", [P, 2, KT, TB], F32R)
        normed_low = sb("normed_low", [P, 2, KT, TB], F32R)

        block_loaded = [sem(f"block_loaded{i}") for i in range(2)]
        inverse_loaded = [sem(f"inverse_loaded{i}") for i in range(2)]
        added = sem("added")
        scaled = sem("scaled")
        scaled_high = sem("scaled_high")
        scaled_low = sem("scaled_low")
        out_tile_ready = sem("out_tile_ready")
        x_updated = sem("x_updated")

        block = ctx.enter_context(nc.Block())

        @block.sync
        def _(sp):
            for tb in range(2):
                load_from_heads(sp, o, o_parts, tb, slice(EARLY, KT), block_loaded[tb])
            for tb in range(2, NTB):
                sp.wait_ge(scaled_low, steps_to(tb - 2, KT - 1))
                load_from_heads(sp, o, o_parts, tb, slice(0, KT), block_loaded[tb % 2])

        @block.tensor
        def _(pe):
            def step(tb, k, f, last_of_tile):
                last = split_products(pe, bank[(KT * tb + f) % 8], o.wo_high[:, k, cols(f, P)],
                                      o.wo_low[:, k, cols(f, P)], normed_high[:, tb % 2, k, :],
                                      normed_low[:, tb % 2, k, :], k == 0, k == KT - 1)
                if last_of_tile:
                    last.then_inc(out_tile_ready, 1)

            pe.wait_ge(o.wo_low_ready, 1)
            for tb, k in STEPS[:2 * KT]:
                pe.wait_ge(scaled_low, steps_to(tb, k))
                for f in range(KT):
                    step(tb, k, f, k == KT - 1)
            for tb in range(2, NTB):
                for f in range(KT):
                    pe.wait_ge(x_updated, KT * tb + f - 7)
                    for k in range(KT):
                        if f == 0:
                            pe.wait_ge(scaled_low, steps_to(tb, k))
                        step(tb, k, f, k == KT - 1)

        @block.vector
        def _(dve):
            def scale(tb, k):
                i = tb % 2
                if tb < 2 and k < EARLY:
                    dve.wait_ge(o.early_loaded[i], 32 + 16 * EARLY)
                else:
                    dve.wait_ge(block_loaded[i], 32 * (tb // 2 + 1))
                dve.tensor_tensor(from_high[:, i, k], from_high[:, i, k], from_low[:, i, k], ALU.add)\
                   .then_inc(added, 1)
                dve.wait_ge(added, steps_to(tb, k))
                if tb >= 2:
                    dve.wait_ge(inverse_loaded[i], 16 + 16 * KT)
                elif k == EARLY:
                    dve.wait_ge(inverse_loaded[i], 16)
                dve.tensor_tensor(from_high[:, i, k], from_high[:, i, k], inverse[:, i, k], ALU.mult)\
                   .then_inc(scaled, 1)

            def update(tb):
                for f in range(KT):
                    t = KT * tb + f
                    dve.wait_ge(out_tile_ready, t + 1)
                    dve.scalar_tensor_tensor(out=x[:, f, cols(tb, TB)], in0=bank[t % 8],
                                             scalar=o.out_bias[:, f:f + 1], in1=x[:, f, cols(tb, TB)],
                                             op0=ALU.add, op1=ALU.add).then_inc(x_updated, 1)

            for tb, k in STEPS[:EARLY]:
                scale(tb, k)
            dve.wait_ge(o.sums_loaded, 32)
            last_heads, _ = o.inverse_tile(LAST_HEADS)
            dve.reciprocal(last_heads, last_heads).then_inc(o.inverse_ready, 1)
            for tb, k in STEPS[EARLY:2 * KT]:
                scale(tb, k)
            dve.wait_ge(o.bias_loaded, 16)
            for tb in range(NTB):
                update(tb)
                if tb + 2 < NTB:
                    for k in range(KT):
                        scale(tb + 2, k)

        @block.scalar
        def _(act):
            move_sums(act, o, sums, LAST_HEADS, True, o.sums_loaded)
            for n, (tb, k) in enumerate(STEPS):
                if n == EARLY:
                    act.wait_ge(o.inverse_ready, 2)
                    move_sums(act, o, inverses, LAST_HEADS, False, o.inverse_stored)
                    act.wait_ge(o.inverse_stored, 32)
                    load_inverse(act, o, inverses, 0, EARLY, inverse_loaded[0])
                    load_inverse(act, o, inverses, 1, EARLY, inverse_loaded[1])
                act.wait_ge(scaled, n + 1)
                if tb >= 2 and k == 0:
                    act.wait_ge(out_tile_ready, KT * (tb - 1))
                act.activation(normed_high[:, tb % 2, k], from_high[:, tb % 2, k], ACT.Copy)\
                   .then_inc(scaled_high, 1)
                if tb < 2 and k == KT - 1:
                    for k2 in range(KT):
                        load_inverse(act, o, inverses, tb + 2, k2, inverse_loaded[tb])

        @block.gpsimd
        def _(pool):
            for n, (tb, k) in enumerate(STEPS):
                pool.wait_ge(scaled_high, n + 1)
                pool.tensor_tensor(normed_low[:, tb % 2, k], from_high[:, tb % 2, k],
                                   f32(normed_high[:, tb % 2, k]), ALU.subtract).then_inc(scaled_low, 1)


def build(nc, x_in, packed, scales, w_v, b_v, w_qk, b_qk, w_out, b_out, out):
    def scratch(name, shape):
        return nc.dram_tensor(name, shape, F32, kind="Internal").ap()

    qk_parts = scratch("qk_parts", (2, 2 * D, TOKENS))
    v_parts = scratch("v_parts", (HEADS, P, TT, 2 * HD))
    o_parts = scratch("o_parts", (2, D, TOKENS))
    sums = scratch("sums", (HEADS, TOKENS))
    inverses = scratch("inverses", (HEADS, TOKENS))
    with ExitStack() as ctx:
        x = ctx.enter_context(nc.sbuf_tensor("x", [P, KT, TOKENS], F32))
        psum = ctx.enter_context(nc.psum_tensor("psum", [P, 8, TB], F32))
        bank = [psum[:, i, :] for i in range(8)]
        ffn(nc, "ffn1", x, bank, packed, scales, x_in, None)
        project_in(nc, x, bank, w_v, b_v, w_qk, b_qk, qk_parts, v_parts)
        with ExitStack() as projection:
            o = OutProjection(nc, projection)
            attention(nc, bank, qk_parts, v_parts, o_parts, sums, inverses, w_out, b_out, o)
            project_out(nc, x, bank, o_parts, sums, inverses, o)
        ffn(nc, "ffn2", x, bank, packed, scales, None, out)
def laid_out(L0_attn_x, L0_attn_w_qkv, L0_attn_b_qkv, L0_attn_w_out, L0_attn_b_out,
             L0_ffn_gate_W_packed, L0_ffn_gate_scales, L0_ffn_up_W_packed, L0_ffn_up_scales,
             L0_ffn_down_W_packed, L0_ffn_down_scales):
    import numpy as np

    def features(a):
        return a.reshape(2, P, 2, -1).transpose(1, 0, 2, 3).reshape(P, KT, -1)

    def gate_words(w):
        w = w.reshape(NGROUP, P, 2, 2, P)
        return w.transpose(0, 4, 3, 2, 1).reshape(NGROUP, P, PIECE)

    def gate_scales(s):
        s = s.reshape(NGROUP, P, 2, 2, SCALE_ROWS)
        return s.transpose(0, 4, 3, 2, 1).reshape(NGROUP, SCALE_ROWS, PIECE)

    def out_features(w):
        return w.reshape(w.shape[0], 2, P, 2).transpose(0, 1, 3, 2).reshape(w.shape[0], D)

    x = np.asarray(L0_attn_x)[0]
    down = out_features(np.asarray(L0_ffn_down_W_packed).T).reshape(NGROUP, P, PIECE)
    down_s = out_features(np.asarray(L0_ffn_down_scales).T).reshape(NGROUP, SCALE_ROWS, PIECE)
    packed = np.stack([gate_words(np.asarray(L0_ffn_gate_W_packed)),
                       gate_words(np.asarray(L0_ffn_up_W_packed)), down], axis=1)
    scales = np.stack([gate_scales(np.asarray(L0_ffn_gate_scales)),
                       gate_scales(np.asarray(L0_ffn_up_scales)), down_s], axis=1)
    w_qkv = features(np.asarray(L0_attn_w_qkv).T)
    b_qkv = np.asarray(L0_attn_b_qkv)
    arrays = {
        "x_in": features(x.T),
        "packed": packed,
        "scales": scales,
        "w_v": w_qkv[:, :, 2 * D:],
        "b_v": b_qkv[2 * D:].reshape(1, D),
        "w_qk": w_qkv[:, :, :2 * D].reshape(P, KT, 2 * KT, P).transpose(2, 0, 1, 3),
        "b_qk": b_qkv[:2 * D].reshape(2 * KT, P).T,
        "w_out": out_features(np.asarray(L0_attn_w_out).T).reshape(KT, P, D).transpose(1, 0, 2),
        "b_out": out_features(np.asarray(L0_attn_b_out).reshape(1, D)).reshape(KT, P).T,
    }
    return {name: np.ascontiguousarray(a) for name, a in arrays.items()}


def kernel(**inputs):
    import numpy as np
    import concourse.bacc as bacc
    from concourse.bass_utils import run_bass_kernel_spmd

    arrays = laid_out(**inputs)
    nc = bacc.Bacc("TRN2", target_bir_lowering=False, num_devices=1)
    args = [nc.dram_tensor(name, a.shape, mybir.dt.from_np(a.dtype), kind="ExternalInput").ap()
            for name, a in arrays.items()]
    out = nc.dram_tensor("out", (P, KT, TOKENS), F32, kind="ExternalOutput").ap()
    build(nc, *args, out)
    result = run_bass_kernel_spmd(nc, [arrays], core_ids=[0]).results[0]["out"]
    y = np.asarray(result).reshape(P, 2, 2, TOKENS).transpose(3, 1, 0, 2)
    return np.ascontiguousarray(y.reshape(1, TOKENS, D))
```

```python
from contextlib import ExitStack

import concourse.bass as bass
from concourse import mybir

ALU = mybir.AluOpType
ACT = mybir.ActivationFunctionType
AX = mybir.AxisListType
F32 = mybir.dt.float32
F32R = mybir.dt.float32r
F16 = mybir.dt.float16
BF16 = mybir.dt.bfloat16
I32 = mybir.dt.int32

P = 128
TOKENS = 2048
D = 512
KT = D // P
TB = 512
NTB = TOKENS // TB
MLP = 4096
GROUP = 256
NGROUP = MLP // GROUP
PIECE = 512
NPIECE = 3
GATE, UP, DOWN = 0, 1, 2
FP4_BLOCK = 32
SCALE_ROWS = 8
HEADS = 16
HD = D // HEADS
TT = TOKENS // P
VCOLS = 2 * HD + 1
SM_SCALE = 1.0 / float(HD) ** 0.5
EPS = 1e-5

CODE = 2.0 ** 14
GELU_A = 0.044715
GELU_C = 0.7978845608028654
FFN_BACK = CODE * CODE * CODE * 0.25
MASKED = -1e30


def f32(ap):
    return ap.bitcast(F32)


def cols(i, n):
    return slice(i * n, (i + 1) * n)


def split_products(pe, out, w_high, w_low, x_high, x_low, first, last):
    pe.matmul(out, w_high, x_high, start=first, stop=False, skip_group_check=True)
    pe.matmul(out, w_high, x_low, start=False, stop=False, skip_group_check=True)
    return pe.matmul(out, w_low, x_high, start=False, stop=last, skip_group_check=True)


class Norm:

    def __init__(self, nc, ctx, tag, x, x_high, x_low, centred, squares, pairs, std, averager, eps,
                 mean_bank, var_bank, x_loaded):
        def sem(name):
            return ctx.enter_context(nc.semaphore(f"{tag}_{name}"))

        self.x, self.x_high, self.x_low = x, x_high, x_low
        self.centred, self.squares, self.pairs, self.std = centred, squares, pairs, std
        self.averager, self.eps = averager, eps
        self.mean_bank, self.var_bank = mean_bank, var_bank
        self.x_loaded = x_loaded
        self.constants_ready = sem("constants_ready")
        self.pairs_ready = sem("pairs_ready")
        self.mean_ready = sem("mean_ready")
        self.centred_ready = sem("centred_ready")
        self.squares_ready = sem("squares_ready")
        self.square_pairs_ready = sem("square_pairs_ready")
        self.variance_ready = sem("variance_ready")
        self.std_ready = sem("std_ready")
        self.rstd_ready = sem("rstd_ready")
        self.normed_ready = sem("normed_ready")
        self.high_ready = sem("high_ready")
        self.low_ready = sem("low_ready")

    def sum_pairs(self, engine, tb):
        if self.x_loaded is not None:
            engine.wait_ge(self.x_loaded[tb], 16)
        if tb >= 1:
            engine.wait_ge(self.mean_ready, tb)
        engine.tensor_tensor(self.pairs, self.x[:, 0:2, cols(tb, TB)], self.x[:, 2:4, cols(tb, TB)],
                             ALU.add).then_inc(self.pairs_ready, 1)

    def mean(self, pe, tb):
        if tb == 0:
            pe.wait_ge(self.constants_ready, 2)
        if tb >= 2:
            pe.wait_ge(self.centred_ready, tb - 1)
        pe.wait_ge(self.pairs_ready, tb + 1)
        for k in range(2):
            last = pe.matmul(self.mean_bank[tb % 2], self.averager[:], self.pairs[:, k, :],
                             start=(k == 0), stop=(k == 1))
        last.then_inc(self.mean_ready, 1)

    def centre(self, dve, tb):
        dve.wait_ge(self.mean_ready, tb + 1)
        if tb >= 2:
            dve.wait_ge(self.low_ready, KT * (tb - 1))
        dve.tensor_tensor(self.centred[tb % 2], self.x[:, :, cols(tb, TB)],
                          self.mean_bank[tb % 2].unsqueeze(1).broadcast_to([P, KT, TB]),
                          ALU.subtract).then_inc(self.centred_ready, 1)

    def square(self, act, tb):
        act.wait_ge(self.centred_ready, tb + 1)
        if tb >= 1:
            act.wait_ge(self.variance_ready, tb)
        for k in range(KT):
            act.activation(self.squares[:, k, :], self.centred[tb % 2][:, k, :], ACT.Square)\
               .then_inc(self.squares_ready, 1)

    def sum_square_pairs(self, dve, tb):
        dve.wait_ge(self.squares_ready, KT * (tb + 1))
        dve.tensor_tensor(self.squares[:, 0:2, :], self.squares[:, 0:2, :], self.squares[:, 2:4, :],
                          ALU.add).then_inc(self.square_pairs_ready, 1)

    def variance(self, pe, tb):
        pe.wait_ge(self.square_pairs_ready, tb + 1)
        if tb >= 2:
            pe.wait_ge(self.std_ready, tb - 1)
        for k in range(2):
            last = pe.matmul(self.var_bank[tb % 2], self.averager[:], self.squares[:, k, :],
                             start=(k == 0), stop=(k == 1))
        last.then_inc(self.variance_ready, 1)

    def standard_deviation(self, act, tb):
        act.wait_ge(self.variance_ready, tb + 1)
        if tb >= 1:
            act.wait_ge(self.normed_ready, KT * tb)
        act.activation(self.std[:], self.var_bank[tb % 2], ACT.Sqrt, bias=self.eps[:]).then_inc(self.std_ready, 1)

    def scale(self, dve, tb):
        dve.wait_ge(self.std_ready, tb + 1)
        dve.reciprocal(self.std[:], self.std[:]).then_inc(self.rstd_ready, 1)
        dve.wait_ge(self.rstd_ready, tb + 1)
        for k in range(KT):
            tile = self.centred[tb % 2][:, k, :]
            dve.tensor_tensor(tile, tile, self.std[:], ALU.mult).then_inc(self.normed_ready, 1)

    def high(self, act, tb):
        for k in range(KT):
            act.wait_ge(self.normed_ready, KT * tb + k + 1)
            act.activation(self.x_high[:, k, cols(tb, TB)], self.centred[tb % 2][:, k, :], ACT.Copy)\
               .then_inc(self.high_ready, 1)

    def low(self, pool, tb):
        for k in range(KT):
            pool.wait_ge(self.high_ready, KT * tb + k + 1)
            pool.tensor_tensor(self.x_low[:, k, cols(tb, TB)], self.centred[tb % 2][:, k, :],
                               f32(self.x_high[:, k, cols(tb, TB)]), ALU.subtract).then_inc(self.low_ready, 1)


def ffn(nc, tag, x, bank, packed, scales, x_in, x_out):
    with ExitStack() as ctx:
        def sb(name, shape, dtype):
            return ctx.enter_context(nc.sbuf_tensor(f"{tag}_{name}", shape, dtype))

        def sem(name):
            return ctx.enter_context(nc.semaphore(f"{tag}_{name}"))

        x_high = sb("x_high", [P, KT, TOKENS], F32R)
        x_low = sb("x_low", [P, KT, TOKENS], F32R)
        words = sb("words", [P, NPIECE, PIECE], I32)
        word_scales = sb("word_scales", [P, NPIECE, PIECE], F32)
        nibbles = sb("nibbles", [P, 2, PIECE], I32)
        weight = sb("weight", [P, 2, 2, PIECE], F32)
        with ExitStack() as overlaid:
            def norm_sb(name, shape):
                return overlaid.enter_context(nc.sbuf_tensor(f"{tag}_{name}", shape, F32))

            centred0 = norm_sb("centred0", [P, KT, TB])
            squares = norm_sb("squares", [P, KT, TB])
            pairs = norm_sb("pairs", [P, 2, TB])
        w_high, w_low = [None, None], [None, None]
        for s in (1, 0):
            w_high[s] = sb(f"w_high{s}", [P, 2, NPIECE, PIECE], F32R)
            w_low[s] = sb(f"w_low{s}", [P, 2, NPIECE, PIECE], F32R)
        gelu = sb("gelu", [P, 6, TB], F32)
        inner = sb("inner", [P, 2, 2, 2, TB], F32R)
        centred1 = sb("centred1", [P, KT, TB], F32)
        std = sb("std", [P, TB], F32)
        averager = sb("averager", [P, P], F32)
        eps = sb("eps", [P, 1], F32)
        signal = sb("signal", [P, 1], F32)

        gate_bank, up_bank, down_bank = bank[0:2], bank[2:4], bank[4:8]
        square = [gelu[:, n, :] for n in range(2)]
        cubic = [gelu[:, 2 + n, :] for n in range(2)]
        product = [gelu[:, 4 + n, :] for n in range(2)]

        x_loaded = [sem(f"x_loaded{tb}") for tb in range(NTB)] if x_in is not None else None
        n = Norm(nc, ctx, tag, x, x_high, x_low, [centred0[:, :, :], centred1[:, :, :]],
                 squares[:, :, :], pairs[:, :, :], std, averager, eps,
                 down_bank[0:2], down_bank[2:4], x_loaded)

        words_loaded = [sem(f"words_loaded{p}") for p in range(NPIECE)]
        nibbles_ready = sem("nibbles_ready")
        weight_ready = sem("weight_ready")
        w_high_ready = sem("w_high_ready")
        w_low_ready = sem("w_low_ready")
        gate_up_ready = sem("gate_up_ready")
        square_ready = sem("gate_square_ready")
        cubic_ready = sem("cubic_ready")
        tanh_ready = sem("tanh_ready")
        gated_ready = sem("gated_ready")
        product_ready = sem("product_ready")
        inner_high_ready = sem("inner_high_ready")
        inner_low_ready = sem("inner_low_ready")
        down_ready = sem("down_ready")
        down_free = sem("down_free")
        stored = sem("stored")

        block = ctx.enter_context(nc.Block())

        @block.sync
        def _(sp):
            def load_words(g, piece):
                sp.dma_start(words[:, piece, :], packed[g, piece]).then_inc(words_loaded[piece], 16)
                sp.dma_start(word_scales[:, piece, :],
                             scales[g, piece].unsqueeze(1).broadcast_to([SCALE_ROWS, P // SCALE_ROWS, PIECE]))\
                  .then_inc(words_loaded[piece], 16)

            if x_in is not None:
                sp.dma_start(x[:, :, cols(0, TB)], x_in[:, :, cols(0, TB)]).then_inc(x_loaded[0], 16)
            for piece in range(NPIECE):
                load_words(0, piece)
            if x_in is not None:
                for tb in range(1, NTB):
                    sp.dma_start(x[:, :, cols(tb, TB)], x_in[:, :, cols(tb, TB)]).then_inc(x_loaded[tb], 16)
            with sp.Fori(1, NGROUP) as g:
                for piece in range(NPIECE):
                    sp.wait_ge(weight_ready, NPIECE * g + (piece + 1 - NPIECE))
                    load_words(g, piece)
            if x_out is not None:
                for tb in range(NTB):
                    for k in range(KT):
                        st = NTB * (NGROUP - 1) + tb
                        sp.wait_ge(down_free, KT * st + KT + k + 1)
                        sp.dma_start(x_out[:, k, cols(tb, TB)], x[:, k, cols(tb, TB)]).then_inc(stored, 16)
                sp.wait_ge(stored, 16 * NTB * KT)

        @block.tensor
        def _(pe):
            def gate_up_tile(gg, s, tb, m, first=False, norm=False):
                if not first:
                    pe.wait_ge(product_ready, 16 * gg + (8 * s + 2 * tb + m - 1))
                for out, piece in ((gate_bank[m], GATE), (up_bank[m], UP)):
                    if m == 0 and tb == 0:
                        pe.wait_ge(w_low_ready, 6 * gg + (3 * s + piece + 1))
                    for k in range(KT):
                        if norm and m == 0 and piece == GATE:
                            pe.wait_ge(n.low_ready, KT * tb + k + 1)
                        c, b = divmod(k, 2)
                        w = slice(c * GROUP + m * P, c * GROUP + (m + 1) * P)
                        last = split_products(
                            pe, out, w_high[s][:, b, piece, w], w_low[s][:, b, piece, w],
                            x_high[:, k, cols(tb, TB)], x_low[:, k, cols(tb, TB)],
                            k == 0, k == KT - 1)
                last.then_inc(gate_up_ready, 1)

            def gate_up(gg, s, tb, norm=False):
                for m in range(2):
                    gate_up_tile(gg, s, tb, m, norm=norm)

            def down(gg, s, tb):
                pe.wait_ge(inner_low_ready, 16 * gg + (8 * s + 2 * tb + 2))
                if tb == 0:
                    pe.wait_ge(w_low_ready, 6 * gg + (3 * s + 3))
                for k in range(KT):
                    pe.wait_ge(down_free, 32 * gg + (16 * s + 4 * tb + k + 1))
                    for m in range(2):
                        last = split_products(
                            pe, down_bank[k], w_high[s][:, m, DOWN, cols(k, P)],
                            w_low[s][:, m, DOWN, cols(k, P)],
                            inner[:, tb % 2, m, 0, :], inner[:, tb % 2, m, 1, :], m == 0, m == 1)
                    last.then_inc(down_ready, 1)

            def group(gg, s, last_group):
                for tb in range(NTB):
                    if tb < NTB - 1:
                        gate_up(gg, s, tb + 1)
                    elif not last_group:
                        gate_up(gg + s, 1 - s, 0)
                    down(gg, s, tb)

            n.mean(pe, 0)
            n.mean(pe, 1)
            n.variance(pe, 0)
            n.mean(pe, 2)
            n.variance(pe, 1)
            gate_up_tile(0, 0, 0, 0, first=True, norm=True)
            n.mean(pe, 3)
            gate_up_tile(0, 0, 0, 1, first=True)
            n.variance(pe, 2)
            gate_up_tile(0, 0, 1, 0, norm=True)
            gate_up_tile(0, 0, 1, 1)
            gate_up_tile(0, 0, 2, 0, norm=True)
            n.variance(pe, 3)
            gate_up_tile(0, 0, 2, 1)
            down(0, 0, 0)
            down(0, 0, 1)
            gate_up(0, 0, 3, norm=True)
            down(0, 0, 2)
            gate_up(0, 1, 0)
            down(0, 0, 3)
            group(0, 1, False)
            with pe.Fori(1, NGROUP // 2 - 1) as gg:
                group(gg, 0, False)
                group(gg, 1, False)
            group(NGROUP // 2 - 1, 0, False)
            group(NGROUP // 2 - 1, 1, True)

        @block.vector
        def _(dve):
            def unpack(gg, s, piece, first=False):
                q = 3 * s + piece
                dve.wait_ge(words_loaded[piece], 64 * gg + 32 * (s + 1))
                a, b = nibbles[:, 0, :], nibbles[:, 1, :]
                w = words[:, piece, :]
                dve.tensor_scalar(a, w, 0xF0, 12, ALU.bitwise_and, ALU.logical_shift_left)\
                   .then_inc(nibbles_ready, 1)
                dve.wait_ge(nibbles_ready, 24 * gg + (4 * q + 1))
                dve.scalar_tensor_tensor(out=b, in0=w, scalar=0xF, in1=a, op0=ALU.bitwise_and,
                                         op1=ALU.bitwise_or).then_inc(nibbles_ready, 1)
                dve.wait_ge(nibbles_ready, 24 * gg + (4 * q + 2))
                dve.scalar_tensor_tensor(out=a, in0=b, scalar=3, in1=b, op0=ALU.logical_shift_left,
                                         op1=ALU.bitwise_or).then_inc(nibbles_ready, 1)
                dve.wait_ge(nibbles_ready, 24 * gg + (4 * q + 3))
                dve.tensor_scalar(b, a, 0x00470047, 9, ALU.bitwise_and, ALU.logical_shift_left)\
                   .then_inc(nibbles_ready, 1)
                dve.wait_ge(nibbles_ready, 24 * gg + (4 * q + 4))
                if not first:
                    dve.wait_ge(w_low_ready, 6 * gg + (q - 1))
                halves = b.bitcast(F16).rearrange("p (w b) -> p b w", b=2)
                dve.tensor_tensor(weight[:, q % 2, :, :], halves,
                                  word_scales[:, piece, :].unsqueeze(1).broadcast_to([P, 2, PIECE]),
                                  ALU.mult).then_inc(weight_ready, 1)

            def gelu_tiles(gg, s, tb, tiles=range(2), first=False):
                for m in tiles:
                    i = 8 * s + 2 * tb + m
                    dve.wait_ge(square_ready, 16 * gg + (i + 1))
                    dve.scalar_tensor_tensor(out=cubic[m], in0=square[m], scalar=1.0 / GELU_A,
                                             in1=gate_bank[m], op0=ALU.add, op1=ALU.mult)\
                       .then_inc(cubic_ready, 1)
                    dve.wait_ge(tanh_ready, 16 * gg + (i + 1))
                    dve.scalar_tensor_tensor(out=cubic[m], in0=square[m], scalar=1.0,
                                             in1=gate_bank[m], op0=ALU.add, op1=ALU.mult)\
                       .then_inc(gated_ready, 1)
                    dve.wait_ge(gated_ready, 16 * gg + (i + 1))
                    if not first:
                        dve.wait_ge(inner_low_ready, 16 * gg + (i - 1))
                    dve.tensor_tensor(product[m], cubic[m], up_bank[m], ALU.mult)\
                       .then_inc(product_ready, 1)

            def add_down(gg, s, tb):
                for k in range(KT):
                    dve.wait_ge(down_ready, 32 * gg + (16 * s + 4 * tb + k + 1))
                    dve.scalar_tensor_tensor(out=x[:, k, cols(tb, TB)], in0=down_bank[k],
                                             scalar=FFN_BACK, in1=x[:, k, cols(tb, TB)],
                                             op0=ALU.mult, op1=ALU.add).then_inc(down_free, 1)

            def group(gg, s, last_group):
                for tb in range(NTB):
                    if tb < NTB - 1:
                        gelu_tiles(gg, s, tb + 1)
                    elif not last_group:
                        gelu_tiles(gg + s, 1 - s, 0)
                    if tb < NPIECE and not last_group:
                        unpack(gg + s, 1 - s, tb)
                    add_down(gg, s, tb)

            dve.memset(averager[:], 1.0 / D).then_inc(n.constants_ready, 1)
            dve.memset(eps[:], EPS).then_inc(n.constants_ready, 1)
            n.sum_pairs(dve, 0)
            unpack(0, 0, GATE, first=True)
            n.centre(dve, 0)
            unpack(0, 0, UP, first=True)
            n.sum_square_pairs(dve, 0)
            n.centre(dve, 1)
            n.scale(dve, 0)
            n.sum_square_pairs(dve, 1)
            unpack(0, 0, DOWN)
            n.scale(dve, 1)
            n.centre(dve, 2)
            n.sum_square_pairs(dve, 2)
            gelu_tiles(0, 0, 0, first=True)
            n.centre(dve, 3)
            n.scale(dve, 2)
            gelu_tiles(0, 0, 1, [0])
            n.sum_square_pairs(dve, 3)
            gelu_tiles(0, 0, 1, [1])
            dve.wait_ge(n.std_ready, NTB)
            dve.memset(signal[:], 0.0).then_inc(down_free, KT)
            n.scale(dve, 3)
            add_down(0, 0, 0)
            gelu_tiles(0, 0, 2)
            add_down(0, 0, 1)
            unpack(0, 1, GATE)
            unpack(0, 1, UP)
            gelu_tiles(0, 0, 3)
            add_down(0, 0, 2)
            unpack(0, 1, DOWN)
            gelu_tiles(0, 1, 0)
            add_down(0, 0, 3)
            group(0, 1, False)
            with dve.Fori(1, NGROUP // 2 - 1) as gg:
                group(gg, 0, False)
                group(gg, 1, False)
            group(NGROUP // 2 - 1, 0, False)
            group(NGROUP // 2 - 1, 1, True)

        @block.scalar
        def _(act):
            def weight_high(gg, s, piece):
                q = 3 * s + piece
                act.wait_ge(weight_ready, 6 * gg + (q + 1))
                act.activation(w_high[s][:, :, piece, :], weight[:, q % 2, :, :], ACT.Copy)\
                   .then_inc(w_high_ready, 1)

            def gelu_tiles(gg, s, tb, tiles=range(2), after_down=None):
                for m in tiles:
                    i = 8 * s + 2 * tb + m
                    act.wait_ge(gate_up_ready, 16 * gg + (i + 1))
                    act.activation(square[m], gate_bank[m], ACT.Square, scale=CODE).then_inc(square_ready, 1)
                    act.wait_ge(cubic_ready, 16 * gg + (i + 1))
                    act.activation(square[m], cubic[m], ACT.Tanh, scale=GELU_C * GELU_A * CODE)\
                       .then_inc(tanh_ready, 1)
                    act.wait_ge(product_ready, 16 * gg + (i + 1))
                    if after_down is not None:
                        act.wait_ge(down_ready, KT * (after_down + 1))
                    act.activation(inner[:, tb % 2, m, 0, :], product[m], ACT.Copy).then_inc(inner_high_ready, 1)

            def group(gg, s, last_group):
                for tb in range(NTB):
                    if tb < NTB - 1:
                        gelu_tiles(gg, s, tb + 1)
                    elif not last_group:
                        gelu_tiles(gg + s, 1 - s, 0)
                    if tb < NPIECE and not last_group:
                        weight_high(gg + s, 1 - s, tb)

            act.wait_ge(n.constants_ready, 2)
            weight_high(0, 0, GATE)
            n.square(act, 0)
            weight_high(0, 0, UP)
            n.standard_deviation(act, 0)
            n.square(act, 1)
            n.high(act, 0)
            n.standard_deviation(act, 1)
            weight_high(0, 0, DOWN)
            n.high(act, 1)
            n.square(act, 2)
            gelu_tiles(0, 0, 0)
            n.standard_deviation(act, 2)
            n.square(act, 3)
            n.high(act, 2)
            gelu_tiles(0, 0, 1)
            n.standard_deviation(act, 3)
            n.high(act, 3)
            gelu_tiles(0, 0, 2, after_down=0)
            act.wait_ge(n.low_ready, KT * NTB)
            weight_high(0, 1, GATE)
            weight_high(0, 1, UP)
            gelu_tiles(0, 0, 3)
            weight_high(0, 1, DOWN)
            gelu_tiles(0, 1, 0)
            group(0, 1, False)
            with act.Fori(1, NGROUP // 2 - 1) as gg:
                group(gg, 0, False)
                group(gg, 1, False)
            group(NGROUP // 2 - 1, 0, False)
            group(NGROUP // 2 - 1, 1, True)

        @block.gpsimd
        def _(pool):
            def weight_low(gg, s, piece):
                q = 3 * s + piece
                pool.wait_ge(w_high_ready, 6 * gg + (q + 1))
                pool.tensor_tensor(w_low[s][:, :, piece, :], weight[:, q % 2, :, :],
                                   f32(w_high[s][:, :, piece, :]), ALU.subtract).then_inc(w_low_ready, 1)

            def gelu_tiles(gg, s, tb):
                for m in range(2):
                    pool.wait_ge(inner_high_ready, 16 * gg + (8 * s + 2 * tb + m + 1))
                    pool.tensor_tensor(inner[:, tb % 2, m, 1, :], product[m],
                                       f32(inner[:, tb % 2, m, 0, :]), ALU.subtract)\
                        .then_inc(inner_low_ready, 1)

            def group(gg, s, last_group):
                for tb in range(NTB):
                    if tb < NTB - 1:
                        gelu_tiles(gg, s, tb + 1)
                    elif not last_group:
                        gelu_tiles(gg + s, 1 - s, 0)
                    if tb < NPIECE and not last_group:
                        weight_low(gg + s, 1 - s, tb)

            n.sum_pairs(pool, 1)
            weight_low(0, 0, GATE)
            n.sum_pairs(pool, 2)
            weight_low(0, 0, UP)
            n.low(pool, 0)
            n.sum_pairs(pool, 3)
            n.low(pool, 1)
            gelu_tiles(0, 0, 0)
            weight_low(0, 0, DOWN)
            n.low(pool, 2)
            gelu_tiles(0, 0, 1)
            n.low(pool, 3)
            gelu_tiles(0, 0, 2)
            weight_low(0, 1, GATE)
            weight_low(0, 1, UP)
            gelu_tiles(0, 0, 3)
            weight_low(0, 1, DOWN)
            gelu_tiles(0, 1, 0)
            group(0, 1, False)
            with pool.Fori(1, NGROUP // 2 - 1) as gg:
                group(gg, 0, False)
                group(gg, 1, False)
            group(NGROUP // 2 - 1, 0, False)
            group(NGROUP // 2 - 1, 1, True)


def tiles_of_block(b):
    if b == 0:
        return list(range(4))
    return [kt for j in range(4) for kt in [*range(b * j, b * j + b), 4 * b + 3 - j]]


TILES = [(b, kt) for b in range(NTB) for kt in tiles_of_block(b)]
CHUNKS = [(b, qt, c) for b in range(NTB) for qt in range(4 * b, 4 * b + 4) for c in range(b + 1)]
SLOTS = len(TILES)
FIRST_OF_BLOCK = [t for t in range(SLOTS) if t == 0 or TILES[t - 1][0] < TILES[t][0]]
LAST_OF_BLOCK = [t - 1 for t in FIRST_OF_BLOCK[1:]] + [SLOTS - 1]
SCORE_BANKS = 3
AHEAD = 4
RING = AHEAD + 1
LOW_AHEAD = 1
ROUNDED_BY_DVE = range(0, SLOTS, RING)


def chunks_of_slot(t):
    return [m for m in range(SLOTS) if m * (SLOTS - 2) // SLOTS == t]


MAXED_AT = {[t for t in range(SLOTS) if b * (b + 1) * 2 + 4 * (b + 1) - 1 in chunks_of_slot(t)][0]: b
            for b in range(NTB)}
ROWS_AT = {t + 2: b for t, b in MAXED_AT.items()}
ITEMS = [item for t in range(SLOTS)
         for item in [("chunk", m) for m in chunks_of_slot(t)] + ([("rows", ROWS_AT[t])] if t in ROWS_AT else [])]
MAX_BANKS = 3


def max_bank_of(s, item):
    return (len(ITEMS) * s + ITEMS.index(item)) % MAX_BANKS


class Heads:
    STACK = 3 * HD
    ROWS = STACK + 2
    LOAD = 7 * 16

    def __init__(self, nc, ctx, max_bank, qk_parts, v_parts):
        def sb(name, shape, dtype):
            return ctx.enter_context(nc.sbuf_tensor(name, shape, dtype))

        def sem(name):
            return ctx.enter_context(nc.semaphore(name))

        self.queries, self.keys, self.values = [], [], []
        with ExitStack() as overlaid:
            self.norm_centred = overlaid.enter_context(nc.sbuf_tensor("qkv_centred", [P, 2, KT, TB], F32))
            self.norm_pairs = overlaid.enter_context(nc.sbuf_tensor("qkv_pairs", [P, 2, TB], F32))
        self.add_slot(nc, ctx)
        self.max_bank, self.qk_parts, self.v_parts = max_bank, qk_parts, v_parts
        self.chunk_max = sb("chunk_max", [P, 2, 4, NTB], F32)
        self.minus_max = sb("minus_max", [P, 2, 4], F32)
        self.max_parts = sb("max_parts", [P, 2, 4, 2], F32R)
        self.ident = sb("ident", [P, P], F32)
        self.ident_r = sb("ident_r", [P, P], F32R)
        self.ident_b = sb("ident_b", [P, P], BF16)
        self.key_mask = sb("key_mask", [P, P], F32)
        self.query_mask = sb("query_mask", [P, P], F32)
        self.key_mask_b = sb("key_mask_b", [P, P], BF16)
        self.query_mask_b = sb("query_mask_b", [P, P], BF16)
        with ExitStack() as overlaid:
            self.wv = overlaid.enter_context(nc.sbuf_tensor("wv", [P, KT, D], F32))
            self.wv_high = overlaid.enter_context(nc.sbuf_tensor("wv_high", [P, KT, D], F32R))
            self.wv_low = overlaid.enter_context(nc.sbuf_tensor("wv_low", [P, KT, D], F32R))
        self.add_slot(nc, ctx)

        self.filled = sem("filled")
        self.constants_ready = sem("heads_constants_ready")
        self.loaded = [sem(f"head_loaded{i}") for i in range(3)]
        self.max_scores_ready = sem("max_scores_ready")
        self.max_taken = sem("max_taken")
        self.max_steps = sem("max_steps")
        self.max_parts_ready = sem("max_parts_ready")
        self.rows_in_bank = sem("rows_in_bank")
        self.rows_ready = sem("rows_ready")

    def add_slot(self, nc, ctx):
        i = len(self.queries)
        self.queries.append(ctx.enter_context(nc.sbuf_tensor(f"queries{i}", [self.ROWS, TOKENS], F32R)))
        self.keys.append(ctx.enter_context(nc.sbuf_tensor(f"keys{i}", [self.ROWS, TOKENS], F32R)))
        self.values.append(ctx.enter_context(nc.sbuf_tensor(f"values{i}", [P, TT, VCOLS], F32R)))

    def fill_ones(self, engine, i):
        engine.memset(f32(self.keys[i][self.STACK:self.ROWS, :]), 1.0).then_inc(self.constants_ready, 1)
        engine.memset(f32(self.values[i][:, :, 2 * HD:VCOLS]), 1.0).then_inc(self.constants_ready, 1)

    def load(self, sp, h, i):
        for part, row in ((0, 0), (1, HD), (0, 2 * HD)):
            sp.dma_start(f32(self.queries[i][row:row + HD, :]),
                         self.qk_parts[part, bass.ds(h * HD, HD), :]).then_inc(self.loaded[i], 16)
        for part, row in ((0, 0), (0, HD), (1, 2 * HD)):
            sp.dma_start(f32(self.keys[i][row:row + HD, :]),
                         self.qk_parts[part, bass.ds(h * HD + D, HD), :]).then_inc(self.loaded[i], 16)
        sp.dma_start(f32(self.values[i][:, :, 0:2 * HD]),
                     self.v_parts[bass.ds(h, 1)].rearrange("o p t c -> (o p) t c")).then_inc(self.loaded[i], 16)

    def wait_for_max_bank(self, pe, hp, s, item):
        before = len(ITEMS) * s + ITEMS.index(item) - MAX_BANKS
        if before < 0:
            return
        (kind, j), s = ITEMS[before % len(ITEMS)], before // len(ITEMS)
        if kind == "chunk":
            pe.wait_ge(self.max_taken, 120 * hp + (SLOTS * s + j + 1))
        else:
            pe.wait_ge(self.rows_ready, 12 * hp + (NTB * s + j + 1))

    def max_chunk(self, pe, hp, s, m):
        b, qt, c = CHUNKS[m]
        i = s % 3
        if m == 0:
            pe.wait_ge(self.loaded[i], self.LOAD * hp + self.LOAD * (s // 3 + 1))
        self.wait_for_max_bank(pe, hp, s, ("chunk", m))
        width = TB if c < b else (qt % 4 + 1) * P
        out = self.max_bank[max_bank_of(s, ("chunk", m))]
        last = pe.matmul(out[:, 0:width], self.queries[i][0:self.STACK, cols(qt, P)],
                         self.keys[i][0:self.STACK, c * TB:c * TB + width], start=True, stop=(c < b),
                         skip_group_check=True)
        if c == b:
            last = pe.matmul(out[:, width - P:width], self.ident_b[:], self.query_mask_b[:],
                             start=False, stop=True, skip_group_check=True)
        last.then_inc(self.max_scores_ready, 1)

    def rows(self, pe, hp, s, b):
        pe.wait_ge(self.max_parts_ready, 12 * hp + (4 * s + b + 1))
        self.wait_for_max_bank(pe, hp, s, ("rows", b))
        for j in range(4):
            last = pe.matmul(self.max_bank[max_bank_of(s, ("rows", b))][0:2, cols(j, P)],
                             self.max_parts[:, b % 2, j, :], self.ident_r[:],
                             start=True, stop=True, skip_group_check=True)
        last.then_inc(self.rows_in_bank, 1)

    def take_max(self, dve, hp, s, m):
        b, qt, c = CHUNKS[m]
        dve.wait_ge(self.max_scores_ready, 120 * hp + (SLOTS * s + m + 1))
        width = TB if c < b else (qt % 4 + 1) * P
        dve.tensor_reduce(self.chunk_max[:, b % 2, qt % 4, c:c + 1],
                          self.max_bank[max_bank_of(s, ("chunk", m))][:, 0:width],
                          AX.X, ALU.max).then_inc(self.max_taken, 1)

    def split_max(self, dve, hp, s, b):
        n = 4 * s + b
        m = [chunk[0] for chunk in CHUNKS].index(b) + 4 * (b + 1)
        dve.wait_ge(self.max_taken, 120 * hp + (SLOTS * s + m))
        dve.tensor_reduce(self.minus_max[:, b % 2, :], self.chunk_max[:, b % 2, :, 0:b + 1], AX.X, ALU.max,
                          negate=True).then_inc(self.max_steps, 1)
        dve.wait_ge(self.max_steps, 24 * hp + (2 * n + 1))
        if n >= 2:
            dve.wait_ge(self.rows_in_bank, 12 * hp + (n - 1))
        dve.tensor_copy(self.max_parts[:, b % 2, :, 0], self.minus_max[:, b % 2, :]).then_inc(self.max_steps, 1)
        dve.wait_ge(self.max_steps, 24 * hp + (2 * n + 2))
        dve.tensor_tensor(self.max_parts[:, b % 2, :, 1], self.minus_max[:, b % 2, :],
                          f32(self.max_parts[:, b % 2, :, 0]), ALU.subtract).then_inc(self.max_parts_ready, 1)

    def store_rows(self, act, hp, s, b):
        act.wait_ge(self.rows_in_bank, 12 * hp + (4 * s + b + 1))
        act.activation(self.queries[s % 3][self.STACK:self.ROWS, cols(b, TB)],
                       self.max_bank[max_bank_of(s, ("rows", b))][0:2, :], ACT.Copy).then_inc(self.rows_ready, 1)


FIRST_MAXIMA = 2 * NTB + 7
LEFT_TO_LAST = 3


def head_items_after(ep, s, tb):
    steps = 2 * KT * NTB - FIRST_MAXIMA
    i = 2 * NTB * ep + NTB * s + tb - FIRST_MAXIMA
    if i < 0:
        return []
    end = len(ITEMS) if i == steps - 1 else len(ITEMS) * (i + 1) // (steps + LEFT_TO_LAST)
    return ITEMS[len(ITEMS) * i // (steps + LEFT_TO_LAST):end]


def project_in(nc, x, bank, w_v, b_v, w_qk, b_qk, qk_parts, v_parts, heads):
    with ExitStack() as ctx:
        def sb(name, shape, dtype):
            return ctx.enter_context(nc.sbuf_tensor(name, shape, dtype))

        def sem(name):
            return ctx.enter_context(nc.semaphore(name))

        ITEM_BANKS = 4
        NTILES = 2 * KT
        wt_high, wt_low = [None, None], [None, None]
        for s in (1, 0):
            wt_high[s] = sb(f"wt_high{s}", [P, KT, P], F32R)
            wt_low[s] = sb(f"wt_low{s}", [P, KT, P], F32R)
        x_high = sb("qkv_x_high", [P, KT, TOKENS], F32R)
        x_low = sb("qkv_x_low", [P, KT, TOKENS], F32R)
        squares = sb("qkv_squares", [P, KT, TB], F32)
        std = sb("qkv_std", [P, TB], F32)
        averager = sb("qkv_averager", [P, P], F32)
        eps = sb("qkv_eps", [P, 1], F32)
        wv, wv_high, wv_low = heads.wv, heads.wv_high, heads.wv_low
        wt = sb("wt", [P, NTILES, KT, P], F32)
        v_bias = sb("v_bias", [P, D], F32)
        qk_bias = sb("qk_bias", [P, NTILES], F32)
        full = sb("full", [P, 2, TB], F32)
        parts = sb("parts", [P, ITEM_BANKS, 2, TB], F32R)

        n = Norm(nc, ctx, "qkv", x, x_high, x_low, [heads.norm_centred[:, tb, :, :] for tb in range(2)],
                 squares, heads.norm_pairs[:], std, averager, eps, bank[4:6], bank[6:8], None)
        wv_loaded = sem("wv_loaded")
        bias_loaded = sem("bias_loaded")
        wt_loaded = sem("wt_loaded")
        wv_high_ready = sem("wv_high_ready")
        wv_low_ready = sem("wv_low_ready")
        wt_high_ready = sem("wt_high_ready")
        wt_low_ready = sem("wt_low_ready")
        item_ready = sem("item_ready")
        full_ready = sem("full_ready")
        part_high_ready = sem("part_high_ready")
        part_low_ready = sem("part_low_ready")
        stored = [sem(f"parts_stored{s}") for s in range(ITEM_BANKS)]

        block = ctx.enter_context(nc.Block())

        @block.sync
        def _(sp):
            sp.dma_start(wv[:], w_v).then_inc(wv_loaded, 16)
            sp.dma_start(v_bias[:], b_v.partition_broadcast(P)).then_inc(bias_loaded, 16)
            sp.dma_start(qk_bias[:], b_qk).then_inc(bias_loaded, 16)
            sp.dma_start(wt[:], w_qk.rearrange("e p k o -> p e k o")).then_inc(wt_loaded, 16)
            for tt in range(TT):
                sp.wait_ge(part_low_ready, tt + 1)
                sp.dma_start(v_parts[:, :, tt, :].rearrange("h p c -> p h c"),
                             f32(parts[:, tt % ITEM_BANKS]).rearrange("p l (h c) -> p (l h) c", h=HEADS // 2))\
                  .then_inc(stored[tt % ITEM_BANKS], 16)

            def store_tile(ep, s, tb):
                sp.wait_ge(part_low_ready, 8 * ep + (TT + 4 * s + tb + 1))
                sp.dma_start(
                    qk_parts[:, bass.ds(P * ep + s * D, P), cols(tb, TB)].rearrange("l e t -> e l t"),
                    f32(parts[:, tb])).then_inc(stored[tb], 16)

            for s in range(2):
                for tb in range(NTB):
                    store_tile(0, s, tb)
            for i in range(ITEM_BANKS):
                sp.wait_ge(stored[i], 16 * (TT + 2 * NTB) // ITEM_BANKS)
            heads.load(sp, 0, 0)
            for s in range(2):
                for tb in range(NTB):
                    store_tile(1, s, tb)
            heads.load(sp, 1, 1)
            with sp.Fori(2, NTILES // 2) as ep:
                for s in range(2):
                    for tb in range(NTB):
                        store_tile(ep, s, tb)
            for s in range(ITEM_BANKS):
                sp.wait_ge(stored[s], 16 * (TT + NTILES * NTB) // ITEM_BANKS)

        @block.tensor
        def _(pe):
            def value_items(tts):
                for tt in tts:
                    tb, token_tile = divmod(tt, NTB)
                    if tt >= ITEM_BANKS:
                        pe.wait_ge(full_ready, tt - ITEM_BANKS + 1)
                    for k in range(KT):
                        if token_tile == 0:
                            pe.wait_ge(n.low_ready, KT * tb + k + 1)
                        pe.matmul(bank[tt % ITEM_BANKS], x_high[:, k, cols(tt, P)], wv_high[:, k, :],
                                  start=(k == 0), stop=False)
                        pe.matmul(bank[tt % ITEM_BANKS], x_low[:, k, cols(tt, P)], wv_high[:, k, :],
                                  start=False, stop=False)
                        last = pe.matmul(bank[tt % ITEM_BANKS], x_high[:, k, cols(tt, P)], wv_low[:, k, :],
                                         start=False, stop=(k == KT - 1))
                    last.then_inc(item_ready, 1)

            n.mean(pe, 0)
            n.mean(pe, 1)
            n.variance(pe, 0)
            n.mean(pe, 2)
            n.variance(pe, 1)
            pe.wait_ge(wv_low_ready, 1)
            value_items(range(0, 2))
            n.mean(pe, 3)
            value_items(range(2, 4))
            n.variance(pe, 2)
            value_items(range(4, 8))
            n.variance(pe, 3)
            value_items(range(8, TT))
            for ep in range(NTILES // 2):
                for s in range(2):
                    pe.wait_ge(wt_low_ready, 2 * ep + (s + 1))
                    for tb in range(NTB):
                        pe.wait_ge(full_ready, 8 * ep + (TT + 4 * s + tb - ITEM_BANKS + 1))
                        for k in range(KT):
                            last = split_products(pe, bank[tb], wt_high[s][:, k, :], wt_low[s][:, k, :],
                                                  x_high[:, k, cols(tb, TB)], x_low[:, k, cols(tb, TB)],
                                                  k == 0, k == KT - 1)
                        last.then_inc(item_ready, 1)
                        for kind, j in head_items_after(ep, s, tb):
                            if kind == "chunk":
                                if j == 0:
                                    pe.wait_ge(heads.constants_ready, 8)
                                heads.max_chunk(pe, 0, 0, j)
                            else:
                                heads.rows(pe, 0, 0, j)

        @block.vector
        def _(dve):
            dve.memset(averager[:], 1.0 / D).then_inc(n.constants_ready, 1)
            dve.memset(eps[:], EPS).then_inc(n.constants_ready, 1)
            def value_items(tts):
                for tt in tts:
                    dve.wait_ge(item_ready, tt + 1)
                    if tt >= 2:
                        dve.wait_ge(part_low_ready, tt - 1)
                    dve.tensor_tensor(full[:, tt % 2, :], bank[tt % ITEM_BANKS], v_bias[:], ALU.add)\
                       .then_inc(full_ready, 1)

            n.sum_pairs(dve, 0)
            n.centre(dve, 0)
            n.sum_square_pairs(dve, 0)
            n.centre(dve, 1)
            n.scale(dve, 0)
            n.sum_square_pairs(dve, 1)
            n.scale(dve, 1)
            n.centre(dve, 2)
            dve.wait_ge(bias_loaded, 32)
            value_items(range(0, 3))
            n.sum_square_pairs(dve, 2)
            value_items(range(3, 4))
            n.centre(dve, 3)
            n.scale(dve, 2)
            n.sum_square_pairs(dve, 3)
            value_items(range(4, 8))
            n.scale(dve, 3)
            value_items(range(8, TT))
            heads.fill_ones(dve, 0)
            heads.fill_ones(dve, 1)
            dve.wait_ge(heads.filled, 6)
            dve.tensor_copy(heads.ident_r[:], heads.ident[:]).then_inc(heads.constants_ready, 1)
            dve.tensor_copy(heads.ident_b[:], heads.ident[:]).then_inc(heads.constants_ready, 1)
            dve.tensor_copy(heads.key_mask_b[:], heads.key_mask[:]).then_inc(heads.constants_ready, 1)
            dve.tensor_copy(heads.query_mask_b[:], heads.query_mask[:]).then_inc(heads.constants_ready, 1)
            for ep in range(NTILES // 2):
                for s in range(2):
                    for tb in range(NTB):
                        i = TT + 4 * s + tb
                        dve.wait_ge(item_ready, 8 * ep + (i + 1))
                        dve.wait_ge(part_low_ready, 8 * ep + (i - 1))
                        dve.tensor_scalar(full[:, tb % 2, :], bank[tb],
                                          qk_bias[:, 2 * ep + s:2 * ep + s + 1], None, ALU.add)\
                           .then_inc(full_ready, 1)
                        for kind, j in head_items_after(ep, s, tb):
                            if kind == "chunk":
                                heads.take_max(dve, 0, 0, j)
                                if j + 1 == SLOTS or CHUNKS[j + 1][0] > CHUNKS[j][0]:
                                    heads.split_max(dve, 0, 0, CHUNKS[j][0])

        @block.scalar
        def _(act):
            def tile_high(ep, s):
                act.wait_ge(item_ready, 8 * ep + (TT + 4 * (s - 1)))
                act.activation(wt_high[s][:], wt[:, bass.ds(2 * ep + s, 1), :, :].rearrange("p o k c -> p (o k) c"),
                               ACT.Copy).then_inc(wt_high_ready, 1)

            def pair(ep, last_pair):
                for s in range(2):
                    if not (last_pair and s == 1):
                        tile_high(ep + s, 1 - s)
                    for tb in range(NTB):
                        i = TT + 4 * s + tb
                        act.wait_ge(full_ready, 8 * ep + (i + 1))
                        act.wait_ge(stored[tb], 32 * ep + 16 * (i // ITEM_BANKS))
                        act.activation(parts[:, tb, 0, :], full[:, tb % 2, :], ACT.Copy)\
                           .then_inc(part_high_ready, 1)
                        for kind, j in head_items_after(ep, s, tb):
                            if kind == "rows":
                                heads.store_rows(act, 0, 0, j)

            def value_items(tts):
                for tt in tts:
                    act.wait_ge(full_ready, tt + 1)
                    if tt >= ITEM_BANKS:
                        act.wait_ge(stored[tt % ITEM_BANKS], 16 * (tt // ITEM_BANKS))
                    act.activation(parts[:, tt % ITEM_BANKS].rearrange("p a (h l d) -> p (a h) l d", l=2, d=HD)[:, :, 0, :],
                                   full[:, tt % 2, :].rearrange("p (h d) -> p h d", d=HD), ACT.Copy)\
                       .then_inc(part_high_ready, 1)

            act.wait_ge(n.constants_ready, 2)
            n.square(act, 0)
            act.wait_ge(wv_loaded, 16)
            act.activation(wv_high[:], wv[:], ACT.Copy).then_inc(wv_high_ready, 1)
            n.standard_deviation(act, 0)
            n.square(act, 1)
            n.high(act, 0)
            n.standard_deviation(act, 1)
            n.high(act, 1)
            n.square(act, 2)
            value_items(range(0, 4))
            n.standard_deviation(act, 2)
            n.square(act, 3)
            n.high(act, 2)
            act.wait_ge(wt_loaded, 16)
            act.activation(wt_high[0][:], wt[:, 0, :, :], ACT.Copy).then_inc(wt_high_ready, 1)
            value_items(range(4, 8))
            n.standard_deviation(act, 3)
            n.high(act, 3)
            value_items(range(8, TT))
            for ep in range(NTILES // 2):
                pair(ep, ep == NTILES // 2 - 1)

        @block.gpsimd
        def _(pool):
            def tile_low(ep, s):
                pool.wait_ge(wt_high_ready, 2 * ep + (s + 1))
                pool.tensor_tensor(wt_low[s][:],
                                   wt[:, bass.ds(2 * ep + s, 1), :, :].rearrange("p o k c -> p (o k) c"),
                                   f32(wt_high[s][:]), ALU.subtract)\
                    .then_inc(wt_low_ready, 1)

            def pair(ep, last_pair):
                for s in range(2):
                    if not (last_pair and s == 1):
                        tile_low(ep + s, 1 - s)
                    for tb in range(NTB):
                        pool.wait_ge(part_high_ready, 8 * ep + (TT + 4 * s + tb + 1))
                        pool.tensor_tensor(parts[:, tb, 1, :], full[:, tb % 2, :],
                                           f32(parts[:, tb, 0, :]), ALU.subtract).then_inc(part_low_ready, 1)

            def value_items(tts):
                for tt in tts:
                    by_head = parts[:, tt % ITEM_BANKS].rearrange("p a (h l d) -> p (a h) l d", l=2, d=HD)
                    pool.wait_ge(part_high_ready, tt + 1)
                    pool.tensor_tensor(by_head[:, :, 1, :], full[:, tt % 2, :].rearrange("p (h d) -> p h d", d=HD),
                                       f32(by_head[:, :, 0, :]), ALU.subtract).then_inc(part_low_ready, 1)

            n.sum_pairs(pool, 1)
            n.sum_pairs(pool, 2)
            pool.wait_ge(wv_high_ready, 1)
            pool.tensor_tensor(wv_low[:], wv[:], f32(wv_high[:]), ALU.subtract).then_inc(wv_low_ready, 1)
            n.low(pool, 0)
            n.sum_pairs(pool, 3)
            n.low(pool, 1)
            value_items(range(0, 4))
            n.low(pool, 2)
            value_items(range(4, 8))
            n.low(pool, 3)
            tile_low(0, 0)
            pool.memset(heads.ident[:], 0.0).then_inc(heads.filled, 1)
            pool.memset(heads.key_mask[:], 0.0).then_inc(heads.filled, 1)
            pool.memset(heads.query_mask[:], 0.0).then_inc(heads.filled, 1)
            pool.wait_ge(heads.filled, 3)
            pool.affine_select(out=heads.ident[:], in_=heads.ident[:], compare_op=ALU.not_equal, fill=1.0, base=0,
                               pattern=[[-1, P]], channel_multiplier=1).then_inc(heads.filled, 1)
            pool.affine_select(out=heads.key_mask[:], in_=heads.key_mask[:], compare_op=ALU.is_ge, fill=MASKED, base=0,
                               pattern=[[1, P]], channel_multiplier=-1).then_inc(heads.filled, 1)
            pool.affine_select(out=heads.query_mask[:], in_=heads.query_mask[:], compare_op=ALU.is_ge, fill=MASKED,
                               base=0, pattern=[[-1, P]], channel_multiplier=1).then_inc(heads.filled, 1)
            value_items(range(8, TT))
            with pool.Fori(0, NTILES // 2 - 1) as ep:
                pair(ep, False)
            pair(NTILES // 2 - 1, True)


def high_by_dve(t):
    return t in ROUNDED_BY_DVE


def low_by_gpsimd(t):
    return not high_by_dve(t)


def low_rank(t):
    mine = [u for u in range(SLOTS) if low_by_gpsimd(u) == low_by_gpsimd(t)]
    return mine.index(t) + 1, len(mine)


class OutProjection:

    def __init__(self, nc, ctx):
        def sb(name, shape, dtype):
            return ctx.enter_context(nc.sbuf_tensor(name, shape, dtype))

        def sem(name):
            return ctx.enter_context(nc.semaphore(name))

        self.wo = sb("wo", [P, KT, D], F32)
        self.wo_high = sb("wo_high", [P, KT, D], F32R)
        self.wo_low = sb("wo_low", [P, KT, D], F32R)
        self.out_bias = sb("out_bias", [P, KT], F32)
        self.inverse_all = sb("inverse_all", [P, HEADS * TOKENS // P], F32)
        self.from_high = sb("from_high", [P, 2, KT, TB], F32)
        self.from_low = sb("from_low", [P, 2, KT, TB], F32)
        self.inverse = sb("inverse", [P, 2, KT, TB], F32)
        self.wo_loaded = sem("wo_loaded")
        self.bias_loaded = sem("out_bias_loaded")
        self.wo_high_ready = sem("wo_high_ready")
        self.wo_low_ready = sem("wo_low_ready")
        self.sums_loaded = sem("sums_loaded")
        self.inverse_ready = sem("inverse_ready")
        self.inverse_stored = sem("inverse_stored")
        self.early_loaded = [sem(f"early_loaded{i}") for i in range(2)]

    def inverse_tile(self, heads):
        per_row = len(heads) * TOKENS // P
        first = heads[0] * TOKENS // P
        return self.inverse_all[:, first:first + per_row], per_row


HPT = P // HD
EARLY_HEADS = range(0, HEADS - HPT)
LAST_HEADS = range(HEADS - HPT, HEADS)
EARLY = KT - 1


def load_from_heads(queue, o, o_parts, tb, tiles, loaded):
    for part, dst in ((0, o.from_high), (1, o.from_low)):
        queue.dma_start(dst[:, tb % 2, tiles, :],
                        o_parts[part].rearrange("(k p) t -> p k t", p=P)[:, tiles, cols(tb, TB)])\
             .then_inc(loaded, 16)


def load_inverse(queue, o, inverses, tb, k, loaded):
    queue.dma_start(o.inverse[:, tb % 2, k, :],
                    inverses[cols(k, HPT), cols(tb, TB)].unsqueeze(1).broadcast_to([HPT, HD, TB]))\
         .then_inc(loaded, 16)


def move_sums(queue, o, dram, heads, to_chip, moved):
    tile, per_row = o.inverse_tile(heads)
    rows = dram[heads[0]:heads[-1] + 1].rearrange("h t -> (h t)").rearrange("(a t) -> a t", t=per_row)
    queue.dma_start(tile if to_chip else rows, rows if to_chip else tile).then_inc(moved, 16)


def attention(nc, bank, o_parts, sums, inverses, w_out, b_out, heads, o):
    with ExitStack() as ctx:
        def sb(name, shape, dtype):
            return ctx.enter_context(nc.sbuf_tensor(name, shape, dtype))

        def sem(name):
            return ctx.enter_context(nc.semaphore(name))

        heads.add_slot(nc, ctx)
        ROWS, queries, keys, values = heads.ROWS, heads.queries, heads.keys, heads.values
        probs = sb("probs", [P, RING, TB], F32)
        probs_high = sb("probs_high", [P, RING, TB], F32R)
        probs_low = sb("probs_low", [P, RING, TB], F32R)
        heads_out = sb("heads_out", [VCOLS, 2, TB], F32)

        start = sb("start", [P, 3], F32)

        score_bank, out_bank = bank[0:SCORE_BANKS], [bank[3], bank[7]]

        scores_ready = sem("scores_ready")
        probs_ready = sem("probs_ready")
        high_ready = sem("high_ready")
        low_by_dve = sem("low_by_dve")
        low_by_pool = sem("low_by_pool")
        out_ready = sem("out_ready")
        out_free = sem("out_free")
        out_stored = [sem(f"out_stored{i}") for i in range(2)]

        block = ctx.enter_context(nc.Block())

        @block.sync
        def _(sp):
            def store(h0, s, blocks=range(NTB)):
                for b in blocks:
                    sp.wait_ge(out_free, 4 * h0 + (4 * s + b + 1 + 2))
                    sp.dma_start(o_parts[:, bass.ds(h0 * HD + s * HD, HD), cols(b, TB)],
                                 heads_out[0:2 * HD, b % 2, :]).then_inc(out_stored[b % 2], 16)
                    sp.dma_start(sums[bass.ds(h0 + s, 1), cols(b, TB)],
                                 heads_out[2 * HD:VCOLS, b % 2, :]).then_inc(out_stored[b % 2], 16)

            heads.load(sp, 2, 2)
            sp.dma_start(o.wo[:], w_out).then_inc(o.wo_loaded, 16)
            sp.dma_start(o.out_bias[:], b_out).then_inc(o.bias_loaded, 16)
            with sp.Fori(0, HEADS // 3 - 1) as hp:
                for s in range(3):
                    store(3 * hp, s)
                    heads.load(sp, 3 * hp + (s + 3), s)
            store(HEADS - 4, 0)
            heads.load(sp, HEADS - 1, 0)
            for i in range(2):
                sp.wait_ge(out_stored[i], 32 * (len(EARLY_HEADS) * NTB // 2 + 1))
            move_sums(sp, o, sums, EARLY_HEADS, True, o.sums_loaded)
            for tb in range(2):
                load_from_heads(sp, o, o_parts, tb, slice(0, EARLY), o.early_loaded[tb])
            store(HEADS - 4, 1)
            store(HEADS - 4, 2)
            sp.wait_ge(o.inverse_ready, 1)
            move_sums(sp, o, inverses, EARLY_HEADS, False, o.inverse_stored)
            store(HEADS - 4, 3, [0, 1])
            sp.wait_ge(o.inverse_stored, 16)
            for tb in range(2):
                for k in range(EARLY):
                    load_inverse(sp, o, inverses, tb, k, o.early_loaded[tb])
            store(HEADS - 4, 3, [2, 3])
            for i in range(2):
                sp.wait_ge(out_stored[i], 32 * (HEADS * NTB // 2 + 1))

        @block.tensor
        def _(pe):
            def scores(hp, s, t, first=False):
                b, kt = TILES[t]
                i = s % 3
                if t in FIRST_OF_BLOCK:
                    pe.wait_ge(heads.rows_ready, 12 * hp + (4 * s + b + 1))
                    if s == 2 and b == 0:
                        pe.wait_ge(heads.constants_ready, 10)
                if not (first and t < SCORE_BANKS):
                    pe.wait_ge(probs_ready, 120 * hp + (SLOTS * s + t - SCORE_BANKS + 1))
                q0 = max(b * TB, kt * P)
                width = (b + 1) * TB - q0
                out = score_bank[(SLOTS * s + t) % SCORE_BANKS]
                last = pe.matmul(out[:, 0:width], keys[i][0:ROWS, cols(kt, P)],
                                 queries[i][0:ROWS, q0:q0 + width], start=True, stop=(kt < 4 * b),
                                 skip_group_check=True)
                if kt >= 4 * b:
                    last = pe.matmul(out[:, 0:P], heads.ident_b[:], heads.key_mask_b[:],
                                     start=False, stop=True, skip_group_check=True)
                last.then_inc(scores_ready, 1)

            def with_values(hp, s, t):
                b, kt = TILES[t]
                i = s % 3
                if t in FIRST_OF_BLOCK:
                    pe.wait_ge(out_free, 12 * hp + (4 * s + b + 1))
                if high_by_dve(t):
                    per_head = len(ROUNDED_BY_DVE)
                    pe.wait_ge(high_ready, 3 * per_head * hp + (per_head * s + ROUNDED_BY_DVE.index(t) + 1))
                else:
                    pe.wait_ge(probs_ready, 120 * hp + (SLOTS * s + t + 1))
                off = max(0, kt * P - b * TB)
                out = out_bank[b % 2][0:VCOLS, off:TB]
                pe.matmul(out, values[i][:, kt, :], probs_high[:, t % RING, 0:TB - off],
                          start=(t in FIRST_OF_BLOCK), stop=False, skip_group_check=True)
                rank, per_head = low_rank(t)
                pe.wait_ge(low_by_pool if low_by_gpsimd(t) else low_by_dve,
                           3 * per_head * hp + (per_head * s + rank))
                last = pe.matmul(out, values[i][:, kt, :], probs_low[:, t % RING, 0:TB - off],
                                 start=False, stop=(t in LAST_OF_BLOCK), skip_group_check=True)
                if t in LAST_OF_BLOCK:
                    last.then_inc(out_ready, 1)

            def head(hp, s, has_next):
                for t in range(SLOTS):
                    if t + AHEAD < SLOTS:
                        scores(hp, s, t + AHEAD)
                    elif has_next:
                        scores(hp, s + 1, t + AHEAD - SLOTS)
                    if has_next:
                        for m in chunks_of_slot(t):
                            heads.max_chunk(pe, hp, s + 1, m)
                        if t in ROWS_AT:
                            heads.rows(pe, hp, s + 1, ROWS_AT[t])
                    with_values(hp, s, t)

            for t in range(AHEAD):
                scores(0, 0, t, first=True)
            with pe.Fori(0, HEADS // 3) as hp:
                for s in range(3):
                    head(hp, s, True)
            head(HEADS // 3, 0, False)

        @block.vector
        def _(dve):
            def low(hp, s, t):
                if low_by_gpsimd(t):
                    return
                b, kt = TILES[t]
                width = TB - max(0, kt * P - b * TB)
                dve.wait_ge(probs_ready, 120 * hp + (SLOTS * s + t + 1))
                if high_by_dve(t):
                    per_head = len(ROUNDED_BY_DVE)
                    dve.tensor_copy(probs_high[:, t % RING, 0:width], probs[:, t % RING, 0:width])\
                       .then_inc(high_ready, 1)
                    dve.wait_ge(high_ready, 3 * per_head * hp + (per_head * s + ROUNDED_BY_DVE.index(t) + 1))
                dve.tensor_tensor(probs_low[:, t % RING, 0:width], probs[:, t % RING, 0:width],
                                  f32(probs_high[:, t % RING, 0:width]), ALU.subtract).then_inc(low_by_dve, 1)

            def head(hp, s, has_next):
                for t in range(SLOTS):
                    if t + LOW_AHEAD < SLOTS:
                        low(hp, s, t + LOW_AHEAD)
                    elif has_next:
                        low(hp, s + 1, t + LOW_AHEAD - SLOTS)
                    if has_next:
                        for m in chunks_of_slot(t):
                            heads.take_max(dve, hp, s + 1, m)
                        if t in MAXED_AT:
                            heads.split_max(dve, hp, s + 1, MAXED_AT[t])

            heads.fill_ones(dve, 2)
            for t in range(LOW_AHEAD):
                low(0, 0, t)
            with dve.Fori(0, HEADS // 3) as hp:
                for s in range(3):
                    head(hp, s, True)
            dve.wait_ge(o.sums_loaded, 16)
            early, _ = o.inverse_tile(EARLY_HEADS)
            dve.reciprocal(early, early).then_inc(o.inverse_ready, 1)
            head(HEADS // 3, 0, False)

        @block.scalar
        def _(act):
            def exps(hp, s, t):
                b, kt = TILES[t]
                width = TB - max(0, kt * P - b * TB)
                act.wait_ge(scores_ready, 120 * hp + (SLOTS * s + t + 1))
                source = score_bank[(SLOTS * s + t) % SCORE_BANKS][:, 0:width]
                last = act.activation(probs[:, t % RING, 0:width], source, ACT.Exp, scale=SM_SCALE)
                if not high_by_dve(t):
                    last = act.activation(probs_high[:, t % RING, 0:width], source, ACT.Exp, scale=SM_SCALE)
                last.then_inc(probs_ready, 1)

            def take_out(hp, s, b):
                act.wait_ge(out_ready, 12 * hp + (4 * s + b + 1))
                act.wait_ge(out_stored[b % 2], 192 * hp + 32 * ((4 * s + b) // 2 + 1))
                act.activation(heads_out[:, b % 2, :], out_bank[b % 2][0:VCOLS, :], ACT.Copy)\
                   .then_inc(out_free, 1)

            def head(hp, s, has_next):
                for t in range(SLOTS):
                    if t + AHEAD < SLOTS:
                        exps(hp, s, t + AHEAD)
                    elif has_next:
                        exps(hp, s + 1, t + AHEAD - SLOTS)
                    if has_next and t in ROWS_AT:
                        heads.store_rows(act, hp, s + 1, ROWS_AT[t])
                    if t - 1 in LAST_OF_BLOCK:
                        take_out(hp, s, TILES[t - 1][0])
                take_out(hp, s, NTB - 1)

            for t in range(AHEAD):
                exps(0, 0, t)
            with act.Fori(0, HEADS // 3) as hp:
                for s in range(3):
                    head(hp, s, True)
            act.wait_ge(o.wo_loaded, 16)
            act.activation(o.wo_high[:], o.wo[:], ACT.Copy).then_inc(o.wo_high_ready, 1)
            head(HEADS // 3, 0, False)

        @block.gpsimd
        def _(pool):
            def low(hp, s, t):
                if not low_by_gpsimd(t):
                    return
                b, kt = TILES[t]
                width = TB - max(0, kt * P - b * TB)
                pool.wait_ge(probs_ready, 120 * hp + (SLOTS * s + t + 1))
                pool.tensor_tensor(probs_low[:, t % RING, 0:width], probs[:, t % RING, 0:width],
                                   f32(probs_high[:, t % RING, 0:width]), ALU.subtract).then_inc(low_by_pool, 1)

            def head(hp, s):
                for t in range(SLOTS):
                    low(hp, s, t)

            pool.memset(start[:, 0:1], 0.0).then_inc(out_free, 2)
            pool.memset(start[:, 1:2], 0.0).then_inc(out_stored[0], 32)
            pool.memset(start[:, 2:3], 0.0).then_inc(out_stored[1], 32)
            with pool.Fori(0, HEADS // 3) as hp:
                for s in range(3):
                    head(hp, s)
            head(HEADS // 3, 0)
            pool.wait_ge(o.wo_high_ready, 1)
            pool.tensor_tensor(o.wo_low[:], o.wo[:], f32(o.wo_high[:]), ALU.subtract).then_inc(o.wo_low_ready, 1)


STEPS = [(tb, k) for tb in range(2) for k in range(EARLY)] + [(tb, k) for tb in range(2) for k in range(EARLY, KT)]
STEPS += [(tb, k) for tb in range(2, NTB) for k in range(KT)]


def steps_to(tb, k):
    return STEPS.index((tb, k)) + 1


def project_out(nc, x, bank, o_parts, sums, inverses, o):
    with ExitStack() as ctx:
        def sb(name, shape, dtype):
            return ctx.enter_context(nc.sbuf_tensor(name, shape, dtype))

        def sem(name):
            return ctx.enter_context(nc.semaphore(name))

        from_high, from_low, inverse = o.from_high, o.from_low, o.inverse
        normed_high = sb("normed_high", [P, 2, KT, TB], F32R)
        normed_low = sb("normed_low", [P, 2, KT, TB], F32R)

        block_loaded = [sem(f"block_loaded{i}") for i in range(2)]
        inverse_loaded = [sem(f"inverse_loaded{i}") for i in range(2)]
        added = sem("added")
        scaled = sem("scaled")
        scaled_high = sem("scaled_high")
        scaled_low = sem("scaled_low")
        out_tile_ready = sem("out_tile_ready")
        x_updated = sem("x_updated")

        block = ctx.enter_context(nc.Block())

        @block.sync
        def _(sp):
            for tb in range(2):
                load_from_heads(sp, o, o_parts, tb, slice(EARLY, KT), block_loaded[tb])
            for tb in range(2, NTB):
                sp.wait_ge(scaled_low, steps_to(tb - 2, EARLY - 1))
                load_from_heads(sp, o, o_parts, tb, slice(0, EARLY), o.early_loaded[tb % 2])
                for k in range(EARLY):
                    load_inverse(sp, o, inverses, tb, k, o.early_loaded[tb % 2])
            sp.wait_ge(o.inverse_stored, 32)
            for tb in range(2, NTB):
                sp.wait_ge(scaled_low, steps_to(tb - 2, KT - 1))
                load_from_heads(sp, o, o_parts, tb, slice(EARLY, KT), block_loaded[tb % 2])
                load_inverse(sp, o, inverses, tb, EARLY, inverse_loaded[tb % 2])

        @block.tensor
        def _(pe):
            def step(tb, k, f, last_of_tile):
                last = split_products(pe, bank[(KT * tb + f) % 8], o.wo_high[:, k, cols(f, P)],
                                      o.wo_low[:, k, cols(f, P)], normed_high[:, tb % 2, k, :],
                                      normed_low[:, tb % 2, k, :], k == 0, k == KT - 1)
                if last_of_tile:
                    last.then_inc(out_tile_ready, 1)

            pe.wait_ge(o.wo_low_ready, 1)
            for tb, k in STEPS[:2 * KT]:
                pe.wait_ge(scaled_low, steps_to(tb, k))
                for f in range(KT):
                    step(tb, k, f, k == KT - 1)
            for tb in range(2, NTB):
                for f in range(KT):
                    pe.wait_ge(x_updated, KT * tb + f - 7)
                    for k in range(KT):
                        if f == 0:
                            pe.wait_ge(scaled_low, steps_to(tb, k))
                        step(tb, k, f, k == KT - 1)

        @block.vector
        def _(dve):
            def scale(tb, k):
                i = tb % 2
                if k < EARLY:
                    dve.wait_ge(o.early_loaded[i], (32 + 16 * EARLY) * (tb // 2 + 1))
                else:
                    dve.wait_ge(block_loaded[i], 32 * (tb // 2 + 1))
                dve.tensor_tensor(from_high[:, i, k], from_high[:, i, k], from_low[:, i, k], ALU.add)\
                   .then_inc(added, 1)
                dve.wait_ge(added, steps_to(tb, k))
                if k == EARLY:
                    dve.wait_ge(inverse_loaded[i], 16 * (tb // 2 + 1))
                dve.tensor_tensor(from_high[:, i, k], from_high[:, i, k], inverse[:, i, k], ALU.mult)\
                   .then_inc(scaled, 1)

            def update(tb):
                for f in range(KT):
                    t = KT * tb + f
                    dve.wait_ge(out_tile_ready, t + 1)
                    dve.scalar_tensor_tensor(out=x[:, f, cols(tb, TB)], in0=bank[t % 8],
                                             scalar=o.out_bias[:, f:f + 1], in1=x[:, f, cols(tb, TB)],
                                             op0=ALU.add, op1=ALU.add).then_inc(x_updated, 1)

            for tb, k in STEPS[:EARLY]:
                scale(tb, k)
            dve.wait_ge(o.sums_loaded, 32)
            last_heads, _ = o.inverse_tile(LAST_HEADS)
            dve.reciprocal(last_heads, last_heads).then_inc(o.inverse_ready, 1)
            for tb, k in STEPS[EARLY:2 * KT]:
                scale(tb, k)
            dve.wait_ge(o.bias_loaded, 16)
            for tb in range(NTB):
                if tb + 2 < NTB:
                    for k in range(KT):
                        scale(tb + 2, k)
                update(tb)

        @block.scalar
        def _(act):
            move_sums(act, o, sums, LAST_HEADS, True, o.sums_loaded)
            for n, (tb, k) in enumerate(STEPS):
                if n == EARLY:
                    act.wait_ge(o.inverse_ready, 2)
                    move_sums(act, o, inverses, LAST_HEADS, False, o.inverse_stored)
                    act.wait_ge(o.inverse_stored, 32)
                    load_inverse(act, o, inverses, 0, EARLY, inverse_loaded[0])
                    load_inverse(act, o, inverses, 1, EARLY, inverse_loaded[1])
                act.wait_ge(scaled, n + 1)
                if tb >= 2 and k == 0:
                    act.wait_ge(out_tile_ready, KT * (tb - 1))
                act.activation(normed_high[:, tb % 2, k], from_high[:, tb % 2, k], ACT.Copy)\
                   .then_inc(scaled_high, 1)

        @block.gpsimd
        def _(pool):
            for n, (tb, k) in enumerate(STEPS):
                pool.wait_ge(scaled_high, n + 1)
                pool.tensor_tensor(normed_low[:, tb % 2, k], from_high[:, tb % 2, k],
                                   f32(normed_high[:, tb % 2, k]), ALU.subtract).then_inc(scaled_low, 1)


def attend(nc, x, bank, w_v, b_v, w_qk, b_qk, w_out, b_out, qk_parts, v_parts, o_parts, sums, inverses):
    with ExitStack() as ctx:
        heads = Heads(nc, ctx, bank[4:7], qk_parts, v_parts)
        project_in(nc, x, bank, w_v, b_v, w_qk, b_qk, qk_parts, v_parts, heads)
        o = OutProjection(nc, ctx)
        attention(nc, bank, o_parts, sums, inverses, w_out, b_out, heads, o)
        project_out(nc, x, bank, o_parts, sums, inverses, o)


def build(nc, x_in, packed, scales, w_v, b_v, w_qk, b_qk, w_out, b_out, out):
    def scratch(name, shape):
        return nc.dram_tensor(name, shape, F32, kind="Internal").ap()

    qk_parts = scratch("qk_parts", (2, 2 * D, TOKENS))
    v_parts = scratch("v_parts", (HEADS, P, TT, 2 * HD))
    o_parts = scratch("o_parts", (2, D, TOKENS))
    sums = scratch("sums", (HEADS, TOKENS))
    inverses = scratch("inverses", (HEADS, TOKENS))
    with ExitStack() as ctx:
        x = ctx.enter_context(nc.sbuf_tensor("x", [P, KT, TOKENS], F32))
        psum = ctx.enter_context(nc.psum_tensor("psum", [P, 8, TB], F32))
        bank = [psum[:, i, :] for i in range(8)]
        ffn(nc, "ffn1", x, bank, packed, scales, x_in, None)
        attend(nc, x, bank, w_v, b_v, w_qk, b_qk, w_out, b_out, qk_parts, v_parts, o_parts, sums, inverses)
        ffn(nc, "ffn2", x, bank, packed, scales, None, out)
def laid_out(L0_attn_x, L0_attn_w_qkv, L0_attn_b_qkv, L0_attn_w_out, L0_attn_b_out,
             L0_ffn_gate_W_packed, L0_ffn_gate_scales, L0_ffn_up_W_packed, L0_ffn_up_scales,
             L0_ffn_down_W_packed, L0_ffn_down_scales):
    import numpy as np

    def features(a):
        return a.reshape(2, P, 2, -1).transpose(1, 0, 2, 3).reshape(P, KT, -1)

    def gate_words(w):
        w = w.reshape(NGROUP, P, 2, 2, P)
        return w.transpose(0, 4, 3, 2, 1).reshape(NGROUP, P, PIECE)

    def gate_scales(s):
        s = s.reshape(NGROUP, P, 2, 2, SCALE_ROWS)
        return s.transpose(0, 4, 3, 2, 1).reshape(NGROUP, SCALE_ROWS, PIECE)

    def out_features(w):
        return w.reshape(w.shape[0], 2, P, 2).transpose(0, 1, 3, 2).reshape(w.shape[0], D)

    x = np.asarray(L0_attn_x)[0]
    down = out_features(np.asarray(L0_ffn_down_W_packed).T).reshape(NGROUP, P, PIECE)
    down_s = out_features(np.asarray(L0_ffn_down_scales).T).reshape(NGROUP, SCALE_ROWS, PIECE)
    packed = np.stack([gate_words(np.asarray(L0_ffn_gate_W_packed)),
                       gate_words(np.asarray(L0_ffn_up_W_packed)), down], axis=1)
    scales = np.stack([gate_scales(np.asarray(L0_ffn_gate_scales)),
                       gate_scales(np.asarray(L0_ffn_up_scales)), down_s], axis=1)
    w_qkv = features(np.asarray(L0_attn_w_qkv).T)
    b_qkv = np.asarray(L0_attn_b_qkv)
    arrays = {
        "x_in": features(x.T),
        "packed": packed,
        "scales": scales,
        "w_v": w_qkv[:, :, 2 * D:],
        "b_v": b_qkv[2 * D:].reshape(1, D),
        "w_qk": w_qkv[:, :, :2 * D].reshape(P, KT, 2, KT, P).transpose(3, 2, 0, 1, 4).reshape(2 * KT, P, KT, P),
        "b_qk": b_qkv[:2 * D].reshape(2, KT, P).transpose(2, 1, 0).reshape(P, 2 * KT),
        "w_out": out_features(np.asarray(L0_attn_w_out).T).reshape(KT, P, D).transpose(1, 0, 2),
        "b_out": out_features(np.asarray(L0_attn_b_out).reshape(1, D)).reshape(KT, P).T,
    }
    return {name: np.ascontiguousarray(a) for name, a in arrays.items()}


def kernel(**inputs):
    import numpy as np
    import concourse.bacc as bacc
    from concourse.bass_utils import run_bass_kernel_spmd

    arrays = laid_out(**inputs)
    nc = bacc.Bacc("TRN2", target_bir_lowering=False, num_devices=1)
    args = [nc.dram_tensor(name, a.shape, mybir.dt.from_np(a.dtype), kind="ExternalInput").ap()
            for name, a in arrays.items()]
    out = nc.dram_tensor("out", (P, KT, TOKENS), F32, kind="ExternalOutput").ap()
    build(nc, *args, out)
    result = run_bass_kernel_spmd(nc, [arrays], core_ids=[0]).results[0]["out"]
    y = np.asarray(result).reshape(P, 2, 2, TOKENS).transpose(3, 1, 0, 2)
    return np.ascontiguousarray(y.reshape(1, TOKENS, D))
```
